# Optimizing a Trainium2 kernel written in Bass

```python
import numpy as np
import jax
import jax.numpy as jnp

def _softmax(x, axis=-1):
    return jax.nn.softmax(x, axis=axis)

def _gelu(x):
    return jax.nn.gelu(x, approximate=True)

def _silu(x):
    return jax.nn.silu(x)

def _sigmoid(x):
    return jax.nn.sigmoid(x)

def _layernorm(x, axis=-1, eps=1e-05):
    m = jnp.mean(x, axis=axis, keepdims=True)
    v = jnp.var(x, axis=axis, keepdims=True)
    return (x - m) / jnp.sqrt(v + eps)

def _scatter_add(tgt, idx, src, axis=0):
    return tgt.at[idx].add(src)

def _segment_sum(src, seg, n):
    return jax.ops.segment_sum(src, seg, n)
kernel_name = 'mk_adaln_d2_jaxref_r8_aeb957'

def setup_inputs(seed: int=0):
    np.random.seed(seed)
    _w = jnp.asarray

    def _L0_attn_setup():
        import jax, jax.numpy as jnp
        import numpy as np
        EPS = 1e-06

        def _rmsnorm(x, w):
            x32 = x.astype(jnp.float32)
            n = x32 * jax.lax.rsqrt(jnp.mean(x32 * x32, axis=-1, keepdims=True) + EPS)
            return n.astype(x.dtype) * w

        def _reference_tuple_inner(u, dt, A, Bmat, C, D, norm_w):
            u = _rmsnorm(u, norm_w)
            Bsz, T, _ = u.shape
            dts = jax.nn.sigmoid(dt)
            a = jnp.exp(-dts * jnp.abs(A))
            t = jnp.arange(T, dtype=jnp.float32)
            h = dts[:, None] * a[:, None] ** t[None, :]
            u_proj = jnp.einsum('bti,is->bst', u, Bmat)
            k = jnp.flip(h, axis=1)[:, None, :]
            x = jax.lax.conv_general_dilated(u_proj, k, window_strides=(1,), padding=[(T - 1, T - 1)], dimension_numbers=('NCW', 'OIW', 'NCW'), feature_group_count=u_proj.shape[1])[:, :, :T]
            x = jnp.transpose(x, (0, 2, 1))
            y = jnp.einsum('bts,so->bto', x, C) + D
            return (y, x[:, -1])
        key = jax.random.key(seed)
        ks = jax.random.split(key, 8)
        I, S, O = (128, 64, 128)
        Bsz, T = (4, 256)
        return {'u': jax.random.normal(ks[0], (Bsz, T, I), dtype=jnp.float32), 'dt': jax.random.normal(ks[1], (S,), dtype=jnp.float32), 'A': jax.random.normal(ks[2], (S,), dtype=jnp.float32), 'Bmat': jax.random.normal(ks[3], (I, S), dtype=jnp.float32) / np.sqrt(S), 'C': jax.random.normal(ks[4], (S, O), dtype=jnp.float32) / np.sqrt(S), 'D': jax.random.normal(ks[5], (O,), dtype=jnp.float32), 'norm_w': jnp.ones((I,), dtype=jnp.float32)}
    _L0_attn_in = _L0_attn_setup()

    def _L0_ffn_setup():
        import jax, jax.numpy as jnp
        import numpy as np
        B, T, E, C, H, G = (2, 256, 8, 128, 256, 16)
        key = jax.random.key(seed)
        ks = jax.random.split(key, 7)
        return {'hidden_states': jax.random.normal(ks[0], (B, T, C), jnp.float32), 'w_red': jax.random.normal(ks[1], (C, G), jnp.float32) * 0.02, 'wg': jax.random.normal(ks[2], (E, G), jnp.float32), 'W1': jax.random.normal(ks[3], (E, C, H), jnp.float32) * 0.02, 'b1': jax.random.normal(ks[4], (E, H), jnp.float32) * 0.02, 'W2': jax.random.normal(ks[5], (E, H, C), jnp.float32) * 0.02, 'b2': jax.random.normal(ks[6], (E, C), jnp.float32) * 0.02}
    _L0_ffn_in = _L0_ffn_setup()
    _L0_c = _w((lambda *s: np.random.randn(*s).astype(np.float32) * 0.05)(8, 128))
    _L0_wmod = _w((lambda *s: np.random.randn(*s).astype(np.float32) * 0.05)(128, 6 * 128) * 128 ** (-0.5))

    def _L1_attn_setup():
        import jax, jax.numpy as jnp
        import numpy as np
        B, L, DIM = (4, 512, 128)
        H, DQK, DV, DINNER, CHUNK = (16, 64, 64, 64, 64)
        BASE_LR, BASE_WD = (0.001, 0.9)
        key = jax.random.key(seed)
        ks = jax.random.split(key, 9)

        def s(k, shape, scale):
            return jax.random.normal(k, shape, jnp.float32) * scale
        return {'x': jax.random.normal(ks[0], (B, L, DIM), jnp.float32), 'Wq': s(ks[1], (H * DQK, DIM), DIM ** (-0.5)), 'Wk': s(ks[2], (H * DQK, DIM), DIM ** (-0.5)), 'Wv': s(ks[3], (H * DV, DIM), DIM ** (-0.5)), 'Wlr': s(ks[4], (2 * H, DIM), DIM ** (-0.5)), 'Wbeta': s(ks[5], (2 * H, DIM), DIM ** (-0.5)), 'Wo': s(ks[6], (DIM, H * DV), (H * DV) ** (-0.5)), 'W_in_init': s(ks[7], (1, DINNER, H, DQK), DQK ** (-0.5)), 'W_out_init': s(ks[8], (1, DINNER, H, DV), DINNER ** (-0.5))}
    _L1_attn_in = _L1_attn_setup()

    def _L1_ffn_setup():
        import jax, jax.numpy as jnp
        import numpy as np
        E = 8
        TOP_K = 2
        B, S, D = (2, 512, 128)
        H = 512
        CAPACITY = 256

        def _moe(x, Wg, W1, b1, W2, b2):
            b, s, d = x.shape
            xf = x.reshape(b * s, d)
            logits = xf.astype(jnp.float32) @ Wg.astype(jnp.float32)
            probs = jax.nn.softmax(logits, axis=-1)
            vals, idx = jax.lax.top_k(probs, TOP_K)
            w = vals / (jnp.sum(vals, axis=-1, keepdims=True) + 1e-09)
            counts = jnp.zeros((E,), dtype=jnp.int32)
            combine = jnp.zeros((b * s, E), dtype=jnp.float32)
            for k in range(TOP_K):
                oh = jax.nn.one_hot(idx[:, k], E, dtype=jnp.int32)
                pos = jnp.cumsum(oh, axis=0) - 1 + counts[None, :]
                keep = (oh == 1) & (pos < CAPACITY)
                counts = counts + jnp.sum(keep.astype(jnp.int32), axis=0)
                combine = combine + w[:, k][:, None] * keep.astype(jnp.float32)
            out = jnp.zeros_like(xf)
            for e in range(E):
                h = jax.nn.gelu(xf @ W1[e] + b1[e])
                ye = h @ W2[e] + b2[e]
                out = out + combine[:, e][:, None].astype(xf.dtype) * ye
            return out.reshape(b, s, d)
        key = jax.random.key(seed)
        k0, k1, k2, k3 = jax.random.split(key, 4)
        return {'x': jax.random.normal(k0, (B, S, D), dtype=jnp.float32), 'Wg': jax.random.normal(k1, (D, E), dtype=jnp.float32) * 0.02, 'W1': jax.random.normal(k2, (E, D, H), dtype=jnp.float32) * 0.02, 'b1': jnp.zeros((E, H), dtype=jnp.float32), 'W2': jax.random.normal(k3, (E, H, D), dtype=jnp.float32) * 0.02, 'b2': jnp.zeros((E, D), dtype=jnp.float32)}
    _L1_ffn_in = _L1_ffn_setup()
    _L1_c = _w((lambda *s: np.random.randn(*s).astype(np.float32) * 0.05)(8, 128))
    _L1_wmod = _w((lambda *s: np.random.randn(*s).astype(np.float32) * 0.05)(128, 6 * 128) * 128 ** (-0.5))
    _d = {'L0_attn_u': _L0_attn_in['u'], 'L0_attn_dt': _L0_attn_in['dt'], 'L0_attn_A': _L0_attn_in['A'], 'L0_attn_Bmat': _L0_attn_in['Bmat'], 'L0_attn_C': _L0_attn_in['C'], 'L0_attn_D': _L0_attn_in['D'], 'L0_attn_norm_w': _L0_attn_in['norm_w'], 'L0_ffn_w_red': _L0_ffn_in['w_red'], 'L0_ffn_wg': _L0_ffn_in['wg'], 'L0_ffn_W1': _L0_ffn_in['W1'], 'L0_ffn_b1': _L0_ffn_in['b1'], 'L0_ffn_W2': _L0_ffn_in['W2'], 'L0_ffn_b2': _L0_ffn_in['b2'], 'L0_c': _L0_c, 'L0_wmod': _L0_wmod, 'L1_attn_Wq': _L1_attn_in['Wq'], 'L1_attn_Wk': _L1_attn_in['Wk'], 'L1_attn_Wv': _L1_attn_in['Wv'], 'L1_attn_Wlr': _L1_attn_in['Wlr'], 'L1_attn_Wbeta': _L1_attn_in['Wbeta'], 'L1_attn_Wo': _L1_attn_in['Wo'], 'L1_attn_W_in_init': _L1_attn_in['W_in_init'], 'L1_attn_W_out_init': _L1_attn_in['W_out_init'], 'L1_ffn_Wg': _L1_ffn_in['Wg'], 'L1_ffn_W1': _L1_ffn_in['W1'], 'L1_ffn_b1': _L1_ffn_in['b1'], 'L1_ffn_W2': _L1_ffn_in['W2'], 'L1_ffn_b2': _L1_ffn_in['b2'], 'L1_c': _L1_c, 'L1_wmod': _L1_wmod}
    _x0 = _d['L0_attn_u']
    _d['L0_attn_u'] = jax.random.normal(jax.random.fold_in(jax.random.key(seed), 1), (8, 512, 128), dtype=_x0.dtype)
    del _x0
    return _d

def reference(L0_attn_u, L0_attn_dt, L0_attn_A, L0_attn_Bmat, L0_attn_C, L0_attn_D, L0_attn_norm_w, L0_ffn_w_red, L0_ffn_wg, L0_ffn_W1, L0_ffn_b1, L0_ffn_W2, L0_ffn_b2, L0_c, L0_wmod, L1_attn_Wq, L1_attn_Wk, L1_attn_Wv, L1_attn_Wlr, L1_attn_Wbeta, L1_attn_Wo, L1_attn_W_in_init, L1_attn_W_out_init, L1_ffn_Wg, L1_ffn_W1, L1_ffn_b1, L1_ffn_W2, L1_ffn_b2, L1_c, L1_wmod):

    def _L0_attn_ref(u, dt, A, Bmat, C, D, norm_w):
        import jax, jax.numpy as jnp
        import numpy as np
        EPS = 1e-06

        def _rmsnorm(x, w):
            x32 = x.astype(jnp.float32)
            n = x32 * jax.lax.rsqrt(jnp.mean(x32 * x32, axis=-1, keepdims=True) + EPS)
            return n.astype(x.dtype) * w

        def _reference_tuple_inner(u, dt, A, Bmat, C, D, norm_w):
            u = _rmsnorm(u, norm_w)
            Bsz, T, _ = u.shape
            dts = jax.nn.sigmoid(dt)
            a = jnp.exp(-dts * jnp.abs(A))
            t = jnp.arange(T, dtype=jnp.float32)
            h = dts[:, None] * a[:, None] ** t[None, :]
            u_proj = jnp.einsum('bti,is->bst', u, Bmat)
            k = jnp.flip(h, axis=1)[:, None, :]
            x = jax.lax.conv_general_dilated(u_proj, k, window_strides=(1,), padding=[(T - 1, T - 1)], dimension_numbers=('NCW', 'OIW', 'NCW'), feature_group_count=u_proj.shape[1])[:, :, :T]
            x = jnp.transpose(x, (0, 2, 1))
            y = jnp.einsum('bts,so->bto', x, C) + D
            return (y, x[:, -1])
        return _reference_tuple_inner(u, dt, A, Bmat, C, D, norm_w)[0]

    def _L0_ffn_ref(hidden_states, w_red, wg, W1, b1, W2, b2):
        import jax, jax.numpy as jnp
        import numpy as np
        B, T, E, C, H, G = (2, 256, 8, 128, 256, 16)
        b, t, c = hidden_states.shape
        x = hidden_states.reshape(-1, c)
        x_red = x @ w_red
        wg_n = wg / jnp.maximum(jnp.linalg.norm(wg, axis=1, keepdims=True), 0.0001)
        logits = x_red @ wg_n.T
        gates = jax.nn.softmax(logits, axis=1)
        scores = jnp.max(gates, axis=1)
        idx = jnp.argmax(gates, axis=1)
        h = jnp.einsum('nc,ech->neh', x, W1) + b1[None]
        h = jnp.take_along_axis(h, idx[:, None, None], axis=1)[:, 0, :]
        h = jax.nn.gelu(h, approximate=False)
        o = jnp.einsum('nh,ehc->nec', h, W2) + b2[None]
        o = jnp.take_along_axis(o, idx[:, None, None], axis=1)[:, 0, :]
        o = o * scores[:, None]
        return o.reshape(b, t, c)

    def _L1_attn_ref(x, Wq, Wk, Wv, Wlr, Wbeta, Wo, W_in_init, W_out_init):
        import jax, jax.numpy as jnp
        import numpy as np
        B, L, DIM = (4, 512, 128)
        H, DQK, DV, DINNER, CHUNK = (16, 64, 64, 64, 64)
        BASE_LR, BASE_WD = (0.001, 0.9)
        b, l, _ = x.shape
        nc = l // CHUNK
        q = jax.nn.silu(x @ Wq.T).reshape(b, l, H, DQK)
        k = jax.nn.silu(x @ Wk.T).reshape(b, l, H, DQK)
        v = (x @ Wv.T).reshape(b, l, H, DV)
        lr = jax.nn.sigmoid(x @ Wlr.T) * BASE_LR
        wd = jax.nn.sigmoid(x @ Wbeta.T) * BASE_WD

        def chunked(t):
            return jnp.moveaxis(t.reshape(b, nc, CHUNK, *t.shape[2:]), 1, 0)
        qc, kc, vc = (chunked(q), chunked(k), chunked(v))
        lr_c = chunked(lr).mean(axis=2)
        wd_c = chunked(wd).mean(axis=2)
        lr_in, lr_out = (lr_c[..., :H], lr_c[..., H:])
        wd_in, wd_out = (wd_c[..., :H], wd_c[..., H:])
        W_in0 = jnp.broadcast_to(W_in_init, (b, DINNER, H, DQK))
        W_out0 = jnp.broadcast_to(W_out_init, (b, DINNER, H, DV))

        def step(carry, xs):
            W_in, W_out = carry
            qi, ki, vi, li, lo, wi, wo = xs
            p_q = jax.nn.softmax(jnp.einsum('bnhd,bDhd->bnhD', qi, W_in), axis=1)
            o = jnp.einsum('bnhD,bDhd->bnhd', p_q, W_out)
            p = jax.nn.softmax(jnp.einsum('bnhd,bDhd->bnhD', ki, W_in), axis=1)
            grad_out = jnp.einsum('bnhD,bnhd->bDhd', -p, vi)
            a = jnp.einsum('bDhd,bnhd->bnhD', W_out, vi)
            s = jnp.sum(p * a, axis=-1, keepdims=True)
            g_z = -(p * a - p * s)
            grad_in = jnp.einsum('bnhd,bnhD->bDhd', ki, g_z)
            W_in = wi[:, None, :, None] * W_in - li[:, None, :, None] * grad_in
            W_out = wo[:, None, :, None] * W_out - lo[:, None, :, None] * grad_out
            return ((W_in, W_out), o)
        _, outs = jax.lax.scan(step, (W_in0, W_out0), (qc, kc, vc, lr_in, lr_out, wd_in, wd_out))
        o = jnp.moveaxis(outs, 0, 1).reshape(b, l, H * DV)
        return o @ Wo.T

    def _L1_ffn_ref(x, Wg, W1, b1, W2, b2):
        import jax, jax.numpy as jnp
        import numpy as np
        E = 8
        TOP_K = 2
        B, S, D = (2, 512, 128)
        H = 512
        CAPACITY = 256

        def _moe(x, Wg, W1, b1, W2, b2):
            b, s, d = x.shape
            xf = x.reshape(b * s, d)
            logits = xf.astype(jnp.float32) @ Wg.astype(jnp.float32)
            probs = jax.nn.softmax(logits, axis=-1)
            vals, idx = jax.lax.top_k(probs, TOP_K)
            w = vals / (jnp.sum(vals, axis=-1, keepdims=True) + 1e-09)
            counts = jnp.zeros((E,), dtype=jnp.int32)
            combine = jnp.zeros((b * s, E), dtype=jnp.float32)
            for k in range(TOP_K):
                oh = jax.nn.one_hot(idx[:, k], E, dtype=jnp.int32)
                pos = jnp.cumsum(oh, axis=0) - 1 + counts[None, :]
                keep = (oh == 1) & (pos < CAPACITY)
                counts = counts + jnp.sum(keep.astype(jnp.int32), axis=0)
                combine = combine + w[:, k][:, None] * keep.astype(jnp.float32)
            out = jnp.zeros_like(xf)
            for e in range(E):
                h = jax.nn.gelu(xf @ W1[e] + b1[e])
                ye = h @ W2[e] + b2[e]
                out = out + combine[:, e][:, None].astype(xf.dtype) * ye
            return out.reshape(b, s, d)
        return _moe(x, Wg, W1, b1, W2, b2)
    x = L0_attn_u
    mod = (_silu(L0_c) @ L0_wmod).reshape(L0_c.shape[0], 6, 1, -1)
    sa, ca, ga, sb, cb, gb = (mod[:, 0], mod[:, 1], mod[:, 2], mod[:, 3], mod[:, 4], mod[:, 5])
    ga = (2 * (ga >= 0) - 1) * jnp.maximum(jnp.abs(ga), 0.25)
    gb = (2 * (gb >= 0) - 1) * jnp.maximum(jnp.abs(gb), 0.25)
    h = _layernorm(x, axis=-1) * (1 + ca) + sa
    x = x + ga * _L0_attn_ref(h, L0_attn_dt, L0_attn_A, L0_attn_Bmat, L0_attn_C, L0_attn_D, L0_attn_norm_w)
    h = _layernorm(x, axis=-1) * (1 + cb) + sb
    x = x + gb * _L0_ffn_ref(h, L0_ffn_w_red, L0_ffn_wg, L0_ffn_W1, L0_ffn_b1, L0_ffn_W2, L0_ffn_b2)
    mod = (_silu(L1_c) @ L1_wmod).reshape(L1_c.shape[0], 6, 1, -1)
    sa, ca, ga, sb, cb, gb = (mod[:, 0], mod[:, 1], mod[:, 2], mod[:, 3], mod[:, 4], mod[:, 5])
    ga = (2 * (ga >= 0) - 1) * jnp.maximum(jnp.abs(ga), 0.25)
    gb = (2 * (gb >= 0) - 1) * jnp.maximum(jnp.abs(gb), 0.25)
    h = _layernorm(x, axis=-1) * (1 + ca) + sa
    x = x + ga * _L1_attn_ref(h, L1_attn_Wq, L1_attn_Wk, L1_attn_Wv, L1_attn_Wlr, L1_attn_Wbeta, L1_attn_Wo, L1_attn_W_in_init, L1_attn_W_out_init)
    h = _layernorm(x, axis=-1) * (1 + cb) + sb
    x = x + gb * _L1_ffn_ref(h, L1_ffn_Wg, L1_ffn_W1, L1_ffn_b1, L1_ffn_W2, L1_ffn_b2)
    return x

_drawn_inputs = setup_inputs


def setup_inputs(seed=0):
    import zlib

    import numpy as np

    out = dict(_drawn_inputs(seed))
    spreads = {'L0_attn_norm_w': (1.0, 0.2), 'L1_ffn_b1': (0.0, 0.8), 'L1_ffn_b2': (0.0, 0.8)}
    factors = {'L0_ffn_w_red': 8.0,
     'L0_ffn_wg': 8.0,
     'L0_ffn_W1': 8.0,
     'L0_ffn_b1': 8.0,
     'L0_ffn_W2': 8.0,
     'L0_ffn_b2': 8.0,
     'L1_attn_Wq': 8.0,
     'L1_attn_Wk': 8.0,
     'L1_attn_Wv': 8.0,
     'L1_attn_Wlr': 8.0,
     'L1_attn_Wbeta': 8.0,
     'L1_attn_Wo': 8.0,
     'L1_attn_W_in_init': 8.0,
     'L1_attn_W_out_init': 8.0,
     'L1_ffn_Wg': 5.862,
     'L1_ffn_W1': 8.0,
     'L1_ffn_W2': 8.0,
     'L1_c': 5.423,
     'L1_wmod': 5.495}
    for name, (base, spread) in spreads.items():
        noise = np.random.default_rng([zlib.crc32(name.encode()), seed]).standard_normal(out[name].shape)
        drawn = base * np.exp(spread * noise) if base else spread * noise
        out[name] = jnp.asarray(drawn.astype(out[name].dtype))
    for name, factor in factors.items():
        out[name] = (out[name] * factor).astype(out[name].dtype)
    return out
```

```python
from contextlib import ExitStack

import concourse.bass as bass
from concourse import mybir

ALU = mybir.AluOpType
ACT = mybir.ActivationFunctionType
AX_X = mybir.AxisListType.X
F32 = mybir.dt.float32
BF16 = mybir.dt.bfloat16
I32 = mybir.dt.int32
ds = bass.ds

P = 128
B, L, C = 8, 512, 128
BP = B // 2
CH = 64
NC = L // CH
T = BP * NC
W8 = NC * C
S = 64
G = 16
E = 8
F0 = 256
F1 = 512
CAP = 256
H, D = 16, 64
HP = H // 2
HD = H * D
TILES0 = T + E
GRP = 4
SLOTS1 = E * CAP
LN_EPS, RMS_EPS = 1e-5, 1e-6
BASE_LR, BASE_WD = 0.001, 0.9
SA, CA, GA, SB, CB, GB = range(6)


class Chain:

    def __init__(self, eng, sem):
        self.eng, self.sem, self.base, self.k = eng, sem, 0, 0

    def link(self, ins):
        ins.then_inc(self.sem, 1)
        self.k += 1
        self.eng.wait_ge(self.sem, self.base + self.k)

    def enter(self, i, per):
        self.outer, self.per = self.base + self.k, per
        self.base, self.k = self.outer + i * per, 0

    def leave(self, n):
        assert self.k == self.per, (self.k, self.per)
        self.base, self.k = self.outer + n * self.per, 0


def program(nc, A):
    ctx = ExitStack()
    with ctx:
        def sb(name, shape, dt=F32):
            return ctx.enter_context(nc.sbuf_tensor(name, shape, dt))

        def sem(name):
            return ctx.enter_context(nc.semaphore(name))

        x_sb = sb("x_sb", [P, T * C])
        mod = [sb(f"mod{l}", [P, BP * 6 * C]) for l in range(2)]
        ga_d = sb("ga_d", [P, BP * C])
        ident = sb("ident", [P, P])
        ones_f = sb("ones_f", [P, P])
        hT = sb("hT", [P, (T + 1) * P])
        w_qkv = sb("w_qkv", [P, 3 * HD])
        w_o = sb("w_o", [P, HP * C])
        w_init = sb("w_init", [P, 3 * HP * P])
        small = sb("small", [P, 512])
        masks = sb("masks", [P, 4 * P], BF16)
        before, before_own, all_ones, own_ones = (masks[:, n * P:(n + 1) * P] for n in range(4))
        iota_b = sb("iota_b", [P, CAP], BF16)
        consts = sb("consts", [P, 128])
        iota_t, first_w, iota_e, edges, tile_no = (consts[:, a:b] for a, b in ((0, 40), (40, 48), (48, 56), (56, 88), (88, 120)))
        part_no, batch_bit = consts[:, 120:121], consts[:, 121:122]
        arena = sb("arena", [P, 27648])

        def view(at, n, dt=F32):
            v = arena[:, at:at + n]
            return v if dt is F32 else v.bitcast(dt)

        sums, var, rstd = small[:, 0:T], small[:, 32:32 + T], small[:, 64:64 + T]
        ln_eps, rms_eps = small[:, 96:97], small[:, 97:98]
        dt2, a2, dts, decay = (small[:, 98 + n:99 + n] for n in range(4))
        tmp1 = small[:, 102:106]

        ps = [ctx.enter_context(nc.psum_tensor(f"ps{i}", [P, 1024], F32)) for i in range(4)]

        xc = view(0, T * C)
        sq = view(4096, T * C)
        h_st = [view(8192 + 1024 * u, W8) for u in range(2)]
        hT_st = [view(10240 + 1024 * u, W8) for u in range(2)]
        hsq = view(12288, W8)
        rms = view(13312, L)
        us = view(13824, L)
        xs = view(14336, L)
        yg = view(14848, W8)
        a_bc = view(15872, L)
        nb = view(16384, S)
        bmat = view(16448, S)
        normw = view(16512, 1)
        cmat = view(16576, C)
        d_bc = view(16704, C)
        ct = view(17000, 16)
        cth = view(17016, 16)
        st = [view(17100 + 512 * l, 512) for l in range(2)]
        wm = [view(18200 + 768 * l, 768) for l in range(2)]

        w1a, w2a, b1a, b2a = view(12288, E * F0), view(14336, E * F0), view(16384, E * F0), view(18432, E * C)
        logits, shifted, e_exp, pick, onehot, cum, rank, scr = (view(19456 + 256 * n, T * E) for n in range(8))
        onehot_b = view(21504, T * E // 2, BF16)
        n_cmp = view(21632, 320)
        tile_hot = view(21952, T * 40)
        w_gate, wg_n, wg_s, wg_t, wred_t = view(23232, E), view(23240, 16), view(23256, 16), view(23272, E), view(23280, C)
        r_hot = view(0, T * P // 2, BF16)
        t_rhs = view(2048, T * 80 // 2, BF16)
        gx = [view(4096 + 512 * u, GRP * C) for u in range(2)]
        xg = view(5120, GRP * C)
        hb = view(5632, GRP * F0)
        hgT = view(6656, GRP * F0)
        o_st = [view(7680 + 512 * u, GRP * C) for u in range(2)]
        back = [view(8704 + 1024 * u, W8) for u in range(4)]
        route = sb("route", [P, 1024])
        mx, m2, slot_f, tile_f, row_f, score, e_sum, n_tiles, t_end, t_start = (route[:, 32 * n:32 * n + 32] for n in range(10))
        wk, pos, e_of, keep = (route[:, 320 + 64 * n:384 + 64 * n] for n in range(4))
        id_f = route[:, 576:656]
        ids_i = route[:, 656:696].bitcast(I32)
        t_exp_i = route[:, 696:736].bitcast(I32)
        slot_i = route[:, 736:800].bitcast(I32)
        tile_i = route[:, 800:832].bitcast(I32)
        idx_st = [route[:, 832 + n:833 + n].bitcast(I32) for n in range(32)]
        t_exp_f = route[:, 864:904]
        w1s = [view(12288 + 512 * u, F1) for u in range(2)]
        w2s = [view(13312 + 512 * u, F1) for u in range(2)]
        b1t, b2b = view(14336, E * 4), view(14400, E * C)
        wg1 = view(15424, E)
        lg1, sh1, pr1 = view(15488, 256), view(15744, 256), view(16000, 256)
        oh1 = view(16256, 512)
        ohb1 = view(16768, 256, BF16)
        run1 = view(17024, 512)
        rk1, scr1 = view(17536, 512), view(18048, 512)
        own_t, both_t, off1 = view(18560, 64), view(18624, 64), view(18688, 64)
        rhs1 = view(18752, 512, BF16)
        cnt1 = view(19264, 16)
        pos_hot = [view(19328 + 256 * u, 256, BF16) for u in range(2)]
        gx1 = [view(4096 + 256 * u, 2 * C) for u in range(2)]
        xg1 = view(5120, 2 * C)
        hg1 = view(5632, 4 * 2 * C)
        o1_st = [view(7680 + 256 * u, 2 * C) for u in range(2)]

        h_dram = [nc.dram_tensor(f"h_rows{f}", (B * L, C), F32, kind="Internal").ap() for f in range(2)]
        o_dram = [nc.dram_tensor(f"o_rows{f}", (n, C), F32, kind="Internal").ap() for f, n in enumerate((TILES0 * P, SLOTS1))]

        sel = view(12288, 2048)
        w_lb = view(14336, S)
        tg = [view(512 * u, 512) for u in range(2)]
        rate_sums = view(1024, 64)
        rate_spread = view(1536, 64 * CH)
        qk = view(0, 2048)
        vT = view(2048, 1024)
        k_tok, v_tok = view(3072, 1024), view(4096, 1024)
        zs = view(5120, 2048)
        prob = view(7168, 2048)
        p_tok, pa, g_tok = view(9216, 1024), view(10240, 1024), view(11264, 1024)
        oT = view(12288, 1024)
        th = [view(13312 + 1024 * u, 1024) for u in range(2)]
        w_dec = view(15360, 4096)
        w_in, w_out, w_outT = view(19456, 2048), view(21504, 2048), view(23552, 2048)
        wd = view(25600, 1024)
        lr = view(26624, 1024)
        y_gated = small[:, 128:256]
        z_max, z_sum, z_rec = small[:, 256:288], small[:, 288:320], small[:, 320:352]
        s_sum = small[:, 352:368]

        phase_end, passed = sem("phase_end"), sem("passed")
        x_in, c_in, wm_in, a0_in = sem("x_in"), sem("c_in"), sem("wm_in"), sem("a0_in")
        dve_step2 = sem("dve_step2")
        consts_made, dve_step, act_step, pool_step = sem("consts_made"), sem("dve_step"), sem("act_step"), sem("pool_step")
        cond_tanh, cond_spread = sem("cond_tanh"), sem("cond_spread")
        mod_mm, mod_out = sem("mod_mm"), sem("mod_out")
        ln_centered, ln_squared, ln_var, ln_std, ln_scaled = (sem("ln_" + n) for n in ("centered", "squared", "var", "std", "scaled"))
        h_ready, h_turned, hT_ready, hT_used = (sem(n) for n in ("h_ready", "h_turned", "hT_ready", "hT_used"))
        a0_exp, a0_par, a0_sq, a0_up, a0_rms, a0_scan, a0_y, a0_gated, a0_yg_used = (
            sem("a0_" + n) for n in ("exp", "par", "sq", "up", "rms", "scan", "y", "gated", "yg_used"))
        a1_w, sel_made, wlb_in = sem("a1_w"), sem("sel_made"), sem("wlb_in")
        rt_mm, rt_tanh, rt_sum, rt_spread, rt_wd, rt_lr, rt_cred = (sem("rt_" + n) for n in ("mm", "tanh", "sum", "spread", "wd", "lr", "cred"))
        pe_z, pe_a, pe_vt, pe_kt, pe_pv, pe_pq, pe_pk, pe_pt, pe_o, pe_gout, pe_y, pe_gin, pe_wt = (
            sem("pe_" + n) for n in ("z", "a", "vt", "kt", "pv", "pq", "pk", "pt", "o", "gout", "y", "gin", "wt"))
        win_set, wout_set = sem("win_set"), sem("wout_set")
        z_centered, z_summed, pk_norm, silu_done, g_done, wout_new, y_scaled, win_new = (
            sem(n) for n in ("z_centered", "z_summed", "pk_norm", "silu_done", "g_done", "wout_new", "y_scaled", "win_new"))
        z_exp, vT_out, tanh_out, vtok_out, ktok_out, ptok_out, oT_out, woutT_out = (
            sem(n) for n in ("z_exp", "vT_out", "tanh_out", "vtok_out", "ktok_out", "ptok_out", "oT_out", "woutT_out"))
        pq_norm, v_scaled, k_scaled, dec_done, x_added = (sem(n) for n in ("pq_norm", "v_scaled", "k_scaled", "dec_done", "x_added"))
        h_stored = [sem(f"h_stored{u}") for u in range(2)]
        lg_mm, lg_out, ex_done, oh_done, cnt_done, rhs_ready, ids_mm, ids_ready, gw = (
            sem(n) for n in ("lg_mm", "lg_out", "ex_done", "oh_done", "cnt_done", "rhs_ready", "ids_mm", "ids_ready", "gw"))
        f0_w, f1_w, f1_b, pool_step2 = sem("f0_w"), sem("f1_w"), sem("f1_b"), sem("pool_step2")
        gathered = [sem(f"gathered{u}") for u in range(2)]
        x_turned, xg_ready, h_mm, hb_ready, hg_ready, hg_turned, hgT_ready, o_mm, o_ready = (
            sem("ex_" + n) for n in ("x_turned", "xg_ready", "h_mm", "hb_ready", "hg_ready", "hg_turned", "hgT_ready", "o_mm", "o_ready"))
        o_stored = [sem(f"o_stored{u}") for u in range(2)]
        back_in = [sem(f"back_in{u}") for u in range(2)]
        back_used, hot_made, hot_used = sem("back_used"), sem("hot_made"), sem("hot_used")
        out_sem = sem("out_sem")

        block = ctx.enter_context(nc.Block())

        def tiles(ap, i, n=NC):
            return ap[:, ds(i * (n * C), n * C)].rearrange("p (t c) -> p t c", c=C)

        def mod_of(l, bp, j):
            return mod[l][:, ds(bp * (6 * C) + j * C, C)]

        def over_tiles(ap, n=NC):
            return ap.unsqueeze(1).to_broadcast([P, n, C])

        def finish(eng, n):
            eng.drain().then_inc(phase_end, 1)
            eng.wait_ge(phase_end, 5 * n)

        def apart(eng):
            eng.sem_inc(passed, 1)

        @block.sync
        def _(sp):
            for b in range(B):
                bp, be = divmod(b, 2)
                sp.dma_start(x_sb[be * CH:(be + 1) * CH, bp * W8:(bp + 1) * W8].rearrange("p (t c) -> p t c", c=C),
                             A["L0_attn_u"][b].rearrange("(t p) c -> p t c", p=CH)).then_inc(x_in, 16)
            for l in range(2):
                sp.dma_start(ct[:, 8 * l:8 * l + 8], A[f"L{l}_cT"]).then_inc(c_in, 16)
                sp.dma_start(wm[l], A[f"L{l}_wmod"]).then_inc(wm_in, 16)
            col = lambda v: v.rearrange("(a b) -> a b", b=1)
            row = lambda v: v.rearrange("(a b) -> a b", a=1)
            for be in range(2):
                half = slice(be * S, be * S + S)
                sp.dma_start(dt2[half], col(A["L0_attn_dt"])).then_inc(a0_in, 16)
                sp.dma_start(a2[half], col(A["L0_attn_A"])).then_inc(a0_in, 16)
                sp.dma_start(cmat[half], A["L0_attn_C"]).then_inc(a0_in, 16)
            sp.dma_start(bmat, A["L0_attn_Bmat"]).then_inc(a0_in, 16)
            sp.dma_start(normw, col(A["L0_attn_norm_w"])).then_inc(a0_in, 16)
            sp.dma_start(d_bc, row(A["L0_attn_D"]).to_broadcast([P, C])).then_inc(a0_in, 16)
            for n, w in enumerate(("Wq", "Wk", "Wv")):
                sp.dma_start(w_qkv[:, n * HD:(n + 1) * HD], A[f"L1_attn_{w}T"]).then_inc(a1_w, 16)
            sp.dma_start(w_o[:, :].rearrange("r (p c) -> r p c", c=C),
                         A["L1_attn_WoT"].rearrange("(p r) c -> r p c", r=P)).then_inc(a1_w, 16)
            sp.wait_ge(consts_made, 1)
            w3 = w_init[:, :].rearrange("r (k p c) -> r k p c", k=3, c=P)
            for k, n in enumerate(("W_inT", "W_out", "W_outT")):
                for h in range(2):
                    half = slice(h * D, h * D + D)
                    sp.dma_start(w3[half, k, :, half], A[n].rearrange("(p h) r c -> h r p c", h=2)[h]).then_inc(a1_w, 16)
            finish(sp, 1)
            finish(sp, 2)

            def store_h(f, k):
                with sp.Fori(0, 2) as i:
                    for u in range(2):
                        bp = i * 2 + u
                        sp.wait_ge(h_ready, bp + (4 * k + 1))
                        sp.dma_start(h_dram[f][ds(bp * (NC * P), NC * P), :].rearrange("(t p) c -> p t c", p=P),
                                     h_st[u].rearrange("p (t c) -> p t c", c=C)).then_inc(h_stored[u], 16)

            sp.dma_start(w1a.rearrange("c (e f) -> c e f", e=E), A["L0_ffn_W1"].rearrange("e c f -> c e f")).then_inc(f0_w, 16)
            sp.dma_start(w2a.rearrange("r (e j c) -> r e j c", e=E, j=2),
                         A["L0_ffn_W2"].rearrange("e (j r) c -> r e j c", r=P)).then_inc(f0_w, 16)
            sp.dma_start(b1a, A["L0_ffn_b1"].rearrange("(a e) f -> a (e f)", a=1).to_broadcast([P, E * F0])).then_inc(f0_w, 16)
            sp.dma_start(b2a, A["L0_ffn_b2"].rearrange("(a e) f -> a (e f)", a=1).to_broadcast([P, E * C])).then_inc(f0_w, 16)
            sp.dma_start(wg_s[0:E, :], A["L0_ffn_wg"]).then_inc(gw, 16)
            sp.dma_start(wred_t[0:16, :], A["L0_ffn_w_redT"]).then_inc(gw, 16)
            store_h(0, 1)
            finish(sp, 3)
            finish(sp, 4)
            with sp.Fori(0, TILES0 // GRP // 2) as i:
                for u in range(2):
                    g = i * 2 + u
                    sp.wait_ge(o_ready, g * GRP + GRP)
                    sp.dma_start(o_dram[0][ds(g * (GRP * P), GRP * P), :].rearrange("(t p) c -> p t c", p=P),
                                 o_st[u].rearrange("p (t c) -> p t c", c=C)).then_inc(o_stored[u], 16)
            for u in range(2):
                sp.wait_ge(o_stored[u], 16 * (TILES0 // GRP // 2) + 16)
            finish(sp, 5)
            finish(sp, 6)
            sp.dma_start(w_lb[:, 0:32], A["L1_attn_WlrT"]).then_inc(wlb_in, 16)
            sp.dma_start(w_lb[:, 32:64], A["L1_attn_WbetaT"]).then_inc(wlb_in, 16)
            finish(sp, 7)
            finish(sp, 8)
            finish(sp, 9)

            sp.dma_start(wg1, A["L1_ffn_Wg"]).then_inc(gw, 16)
            sp.dma_start(b1t, A["L1_b1_cols"]).then_inc(f1_b, 16)
            sp.dma_start(b2b, A["L1_ffn_b2"].rearrange("(a e) f -> a (e f)", a=1).to_broadcast([P, E * C])).then_inc(f1_b, 16)
            store_h(1, 3)
            finish(sp, 10)
            with sp.Fori(0, E // 2) as i:
                for u in range(2):
                    e = i * 2 + u
                    sp.wait_ge(o_mm, e + (TILES0 - 1))
                    sp.dma_start(w1s[u], A["L1_ffn_W1"].rearrange("e c f -> (e c) f")[ds(e * C, C), :]).then_inc(f1_w, 16)
                    sp.dma_start(w2s[u].rearrange("r (j c) -> r j c", j=4),
                                 A["L1_ffn_W2"].rearrange("e f c -> (e f) c")[ds(e * F1, F1), :].rearrange("(j r) c -> r j c", r=P)
                                 ).then_inc(f1_w, 16)
                    sp.wait_ge(o_ready, e + (TILES0 + 1))
                    sp.dma_start(o_dram[1][ds(e * CAP, CAP), :].rearrange("(t p) c -> p t c", p=P),
                                 o1_st[u].rearrange("p (t c) -> p t c", c=C)).then_inc(o_stored[u], 16)
            for u in range(2):
                sp.wait_ge(o_stored[u], 16 * (TILES0 // GRP // 2 + E // 2) + 16)
            finish(sp, 11)
            finish(sp, 12)

            for b in range(B):
                bp, be = divmod(b, 2)
                sp.dma_start(A["out"][b].rearrange("(t p) c -> p t c", p=CH),
                             x_sb[be * CH:(be + 1) * CH, bp * W8:(bp + 1) * W8].rearrange("p (t c) -> p t c", c=C)
                             ).then_inc(out_sem, 16)
            sp.wait_ge(out_sem, 16 * B)

        @block.gpsimd
        def _(pool):
            chain = Chain(pool, pool_step)
            chain.link(pool.memset(ident[:, :], 0.0))
            chain.link(pool.memset(ones_f[:, :], 1.0))
            chain.link(pool.memset(ln_eps, LN_EPS))
            chain.link(pool.memset(rms_eps, RMS_EPS))
            chain.link(pool.memset(w_init[:, :], 0.0))
            chain.link(pool.memset(hT[:, T * P:(T + 1) * P], 0.0))
            chain.link(pool.affine_select(out=ident[:, :], in_=ident[:, :], compare_op=ALU.not_equal, fill=1.0, base=0,
                               pattern=[[-1, P]], channel_multiplier=1))
            chain.link(pool.memset(masks[:, :], 1.0))
            chain.link(pool.memset(part_no, 0.0))
            chain.link(pool.affine_select(out=masks[:, 0:2 * P].rearrange("q (k p) -> q k p", k=2), in_=masks[:, 0:2 * P].rearrange("q (k p) -> q k p", k=2),
                               compare_op=ALU.is_gt, fill=0.0, base=0, pattern=[[0, 2], [1, P]], channel_multiplier=-1))
            chain.link(pool.memset(before_own[0:CH, CH:P], 0.0))
            chain.link(pool.memset(own_ones[0:CH, CH:P], 0.0))
            chain.link(pool.memset(own_ones[CH:P, 0:CH], 0.0))
            imprecise = dict(allow_small_or_imprecise_dtypes=True)
            chain.link(pool.iota(iota_b[:, :], pattern=[[1, CAP]], base=0, channel_multiplier=0, **imprecise))
            chain.link(pool.iota(iota_t, pattern=[[1, 40]], base=0, channel_multiplier=0, **imprecise))
            chain.link(pool.iota(first_w, pattern=[[-1, E]], base=E, channel_multiplier=0, **imprecise))
            chain.link(pool.iota(iota_e, pattern=[[1, E]], base=0, channel_multiplier=0, **imprecise))
            chain.link(pool.iota(edges, pattern=[[P, T]], base=0, channel_multiplier=0, **imprecise))
            chain.link(pool.iota(tile_no, pattern=[[1, T]], base=0, channel_multiplier=0, **imprecise))
            chain.link(pool.iota(part_no, pattern=[[0, 1]], base=0, channel_multiplier=1, **imprecise))
            chain.link(pool.memset(batch_bit[0:CH], 0.0))
            chain.link(pool.memset(batch_bit[CH:P], 1.0))
            pool.sem_inc(consts_made, 1)
            for u in range(2):
                pool.sem_inc(h_stored[u], 16)
                pool.sem_inc(o_stored[u], 16)
            pool.sem_inc(h_turned, 2)
            finish(pool, 1)

            def add_shift(l, k, j, f=None):
                with pool.Fori(0, 2) as i:
                    for u in range(2):
                        bp = i * 2 + u
                        pool.wait_ge(ln_scaled, bp + (4 * k + 1))
                        pool.wait_ge(h_turned, bp + (4 * k + 1))
                        if f is not None:
                            pool.wait_ge(h_stored[u], i * 16 + (32 * f + 16))
                        pool.tensor_tensor(h_st[u].rearrange("p (t c) -> p t c", c=C), tiles(xc, bp),
                                           over_tiles(mod_of(l, bp, j)), ALU.add).then_inc(h_ready, 1)
                        yield bp

            for bp in add_shift(0, 0, SA):
                pass
            with pool.Fori(0, BP) as bp:
                pool.wait_ge(a0_gated, bp + 1)
                y3 = yg.rearrange("p (t c) -> p t c", c=C)
                chain.enter(bp, 1)
                chain.link(pool.tensor_tensor(y3, y3, over_tiles(ga_d[:, ds(bp * C, C)]), ALU.add))
                pool.tensor_tensor(tiles(x_sb, bp), tiles(x_sb, bp), y3, ALU.add).then_inc(a0_yg_used, 1)
            chain.leave(BP)
            finish(pool, 2)

            def gather_back(f, base):
                with pool.Fori(0, 2) as i:
                    for u in range(2):
                        bp = i * 2 + u
                        pool.wait_ge(back_used, bp + (4 * f + 1))
                        for k in range(f + 1):
                            for t in range(NC):
                                pool.tensor_copy(idx_st[8 * (2 * u + k) + t], slot_i[:, ds(bp * NC + (k * T + t), 1)]
                                                 ).then_inc(pool_step2, 1)
                        pool.wait_ge(pool_step2, bp * (NC * (f + 1)) + (base + NC * (f + 1)))
                        apart(pool)
                        for k in range(f + 1):
                            for t in range(NC):
                                pool.indirect_dma_start(
                                    back[2 * u + k][:, t * C:(t + 1) * C], None, o_dram[f][:, :],
                                    bass.IndirectOffsetOnAxis(ap=idx_st[8 * (2 * u + k) + t], axis=0),
                                    bounds_check=o_dram[f].shape[0] - 1, oob_is_err=False).then_inc(back_in[u], 16)

            for bp in add_shift(0, 1, SB, f=0):
                pass
            finish(pool, 3)
            finish(pool, 4)
            for u in range(2):
                pool.wait_ge(h_stored[u], 48)
            n0 = 0
            with pool.Fori(0, TILES0 // GRP // 2) as i:
                for u in range(2):
                    g = i * 2 + u
                    pool.wait_ge(x_turned, g + 1)
                    for t in range(GRP):
                        pool.tensor_copy(idx_st[GRP * u + t], ids_i[:, ds(g * GRP + t, 1)]).then_inc(pool_step2, 1)
                    pool.wait_ge(pool_step2, g * GRP + (n0 + GRP))
                    apart(pool)
                    for t in range(GRP):
                        pool.indirect_dma_start(gx[u][:, t * C:(t + 1) * C], None, h_dram[0][:, :],
                                                bass.IndirectOffsetOnAxis(ap=idx_st[GRP * u + t], axis=0),
                                                bounds_check=B * L - 1, oob_is_err=False).then_inc(gathered[u], 16)
            n0 += TILES0
            finish(pool, 5)
            gather_back(0, n0)
            n0 += T
            finish(pool, 6)

            chain.link(pool.memset(sel[0:64, :], 0.0))
            pool.affine_select(out=sel[0:64, :].rearrange("k (i p h m) -> k i p h m", i=2, p=HP, h=2),
                               in_=sel[0:64, :].rearrange("k (i p h m) -> k i p h m", i=2, p=HP, h=2),
                               compare_op=ALU.not_equal, fill=1.0, base=-2 * H,
                               pattern=[[-H, 2], [-2, HP], [-1, 2], [0, D]], channel_multiplier=1).then_inc(sel_made, 1)
            for bp in add_shift(1, 2, SA):
                pass
            finish(pool, 7)
            finish(pool, 8)

            pool.sem_inc(x_added, 1)
            with pool.Fori(0, BP) as bp:
                with pool.Fori(0, NC) as c:
                    t = bp * NC + c
                    pool.wait_ge(win_set, bp * 2 + 2)
                    pool.wait_ge(wout_set, bp * 4 + 4)
                    for be in range(2):
                        pool.wait_ge(win_new, t * 2 + (be + 1))
                        pool.wait_ge(wout_new, t * 2 + (be + 1))
                        for k, w in enumerate((w_in, w_out)):
                            last = pool.tensor_tensor(
                                w_dec[:, (2 * k + be) * 1024:(2 * k + be + 1) * 1024].rearrange("r (p c) -> r p c", c=P),
                                w[:, be * 1024:(be + 1) * 1024].rearrange("r (p c) -> r p c", c=P),
                                wd[:, ds(t * 32 + (16 * be + 8 * k), HP)].unsqueeze(2).to_broadcast([P, HP, P]), ALU.mult)
                        last.then_inc(dec_done, 1)
                    pool.wait_ge(z_summed, t * 2 + 2)
                    z4 = zs.rearrange("r (e p k n) -> r e p k n", e=2, p=HP, k=2)
                    r4 = z_rec.rearrange("r (e p k) -> r e p k", e=2, p=HP)
                    pool.tensor_tensor(prob[:, 0:1024].rearrange("r (p e n) -> r e p n", e=2, n=CH), z4[:, :, :, 0, :],
                                       r4[:, :, :, 0].unsqueeze(3).to_broadcast([P, 2, HP, CH]), ALU.mult).then_inc(pq_norm, 1)
                    for buf, at, ready, done in ((v_tok, H, vtok_out, v_scaled), (k_tok, 0, ktok_out, k_scaled)):
                        pool.wait_ge(ready, t + 1)
                        b3 = buf.rearrange("r (h d) -> r h d", d=D)
                        pool.tensor_tensor(b3, b3, lr[:, ds(t * 32 + at, H)].unsqueeze(2).to_broadcast([P, H, D]),
                                           ALU.mult).then_inc(done, 1)
                    pool.wait_ge(y_scaled, t + 1)
                    pool.tensor_tensor(x_sb[:, ds(t * C, C)], x_sb[:, ds(t * C, C)], y_gated, ALU.add).then_inc(x_added, 1)
            finish(pool, 9)

            for bp in add_shift(1, 3, SB, f=1):
                pass
            finish(pool, 10)
            for u in range(2):
                pool.wait_ge(h_stored[u], 80)
            pool.wait_ge(ids_ready, 2)
            with pool.Fori(0, E // 2) as i:
                for u in range(2):
                    e = i * 2 + u
                    pool.wait_ge(x_turned, e + (TILES0 // GRP + 1))
                    for t in range(2):
                        pool.tensor_copy(idx_st[2 * u + t], ids_i[:, ds(e + E * t, 1)]).then_inc(pool_step2, 1)
                    pool.wait_ge(pool_step2, e * 2 + (n0 + 2))
                    apart(pool)
                    for t in range(2):
                        pool.indirect_dma_start(gx1[u][:, t * C:(t + 1) * C], None, h_dram[1][:, :],
                                                bass.IndirectOffsetOnAxis(ap=idx_st[2 * u + t], axis=0),
                                                bounds_check=B * L - 1, oob_is_err=False).then_inc(gathered[u], 16)
            n0 += 2 * E
            finish(pool, 11)
            gather_back(1, n0)
            finish(pool, 12)

        @block.scalar
        def _(act):
            act.wait_ge(c_in, 32)
            act.activation(cth, ct, ACT.Tanh, scale=0.5).then_inc(cond_tanh, 1)
            for l in range(2):
                for bp in range(BP):
                    n = BP * l + bp
                    act.wait_ge(mod_mm, n + 1)
                    act.activation(mod[l][:, bp * 6 * C:(bp + 1) * 6 * C], ps[n % 4][:, 0:6 * C],
                                   ACT.Copy).then_inc(mod_out, 1)
            act.wait_ge(a0_in, 16 * 9)
            act.activation(tmp1[:, 0:1], dt2, ACT.Exp, scale=-1.0).then_inc(a0_exp, 1)
            act.wait_ge(a0_par, 1)
            act.activation(decay, tmp1[:, 3:4], ACT.Exp, scale=-1.0).then_inc(a0_exp, 1)
            finish(act, 1)

            def squares_and_std(k):
                with act.Fori(0, BP) as i:
                    act.wait_ge(ln_centered, i + (4 * k + 1))
                    act.activation(tiles(sq, i), tiles(xc, i), ACT.Square).then_inc(ln_squared, 1)
                act.wait_ge(ln_var, 4 * (k + 1))
                act.activation(rstd, var, ACT.Sqrt, bias=ln_eps, scale=1.0 / C).then_inc(ln_std, 1)

            squares_and_std(0)
            with act.Fori(0, 2) as i:
                for u in range(2):
                    bp = i * 2 + u
                    act.wait_ge(h_turned, bp + 3)
                    act.activation(hT_st[u].rearrange("c (e t n) -> c t e n", e=2, n=CH),
                                   ps[u][:, :].rearrange("c (t e n) -> c t e n", e=2, n=CH), ACT.Copy
                                   ).then_inc(hT_ready, 1)
                    act.wait_ge(hT_ready, bp + 1)
                    if u == 0:
                        pass
                    act.activation(hsq, hT_st[u], ACT.Square).then_inc(a0_sq, 1)
                    act.wait_ge(a0_up, bp + 1)
                    act.activation(rms, ps[2][:, 0:L], ACT.Sqrt, bias=rms_eps, scale=1.0 / C).then_inc(a0_rms, 1)
            finish(act, 2)

            def out_of_turn(k):
                with act.Fori(0, 2) as i:
                    for u in range(2):
                        bp = i * 2 + u
                        act.wait_ge(h_turned, bp + (4 * k + 3))
                        act.activation(hT_st[u], ps[u][:, :], ACT.Copy).then_inc(hT_ready, 1)

            act.wait_ge(gw, 33)
            act.activation(wg_n[0:E, 0:1], wg_t[0:E, 0:1], ACT.Sqrt).then_inc(gw, 1)
            squares_and_std(1)
            out_of_turn(1)
            finish(act, 3)
            act.wait_ge(oh_done, 1)
            act.activation(e_exp, shifted, ACT.Exp).then_inc(ex_done, 1)
            finish(act, 4)
            with act.Fori(0, TILES0 // GRP) as g:
                act.wait_ge(x_turned, g + 3)
                act.activation(xg, ps[0][:, 0:GRP * C], ACT.Copy).then_inc(xg_ready, 1)
                act.wait_ge(hb_ready, g * GRP + GRP)
                act.activation(hb, hb, ACT.Gelu).then_inc(hg_ready, 1)
            finish(act, 5)
            finish(act, 6)

            squares_and_std(2)
            with act.Fori(0, 2) as i:
                for u in range(2):
                    bp = i * 2 + u
                    act.wait_ge(h_turned, bp + (2 * BP + 3))
                    act.activation(hT[:, ds(bp * W8, W8)], ps[u][:, :], ACT.Copy).then_inc(hT_ready, 1)
            finish(act, 7)
            with act.Fori(0, 4) as i:
                for u in range(2):
                    n = i * 2 + u
                    act.wait_ge(rt_mm, n + 1)
                    act.wait_ge(rt_sum, n + 1)
                    act.activation(tg[u][0:64, :], ps[u][0:64, 0:512], ACT.Tanh, scale=0.5).then_inc(rt_tanh, 1)
            finish(act, 8)

            act.wait_ge(pe_pv, 1)
            act.activation(vT, ps[0][:, :], ACT.Copy).then_inc(vT_out, 1)
            act.wait_ge(pe_pq, 1)
            act.activation(th[0], ps[1][:, :], ACT.Tanh, scale=0.5).then_inc(tanh_out, 1)
            act.wait_ge(pe_pk, 1)
            act.activation(th[1], ps[2][:, :], ACT.Tanh, scale=0.5).then_inc(tanh_out, 1)
            with act.Fori(0, BP) as bp:
                act.wait_ge(woutT_out, bp * (2 * NC) + 2)
                for be in range(2):
                    for k, w in ((1, w_out), (2, w_outT)):
                        act.activation(w[:, be * 1024:(be + 1) * 1024], w_init[:, k * 1024:(k + 1) * 1024],
                                       ACT.Copy).then_inc(wout_set, 1)
                with act.Fori(0, NC) as c:
                    t = bp * NC + c
                    for be in range(2):
                        z = zs[:, be * 1024:(be + 1) * 1024]
                        act.wait_ge(z_centered, t * 2 + (be + 1))
                        act.activation(z, z, ACT.Exp, scale=0.5).then_inc(z_exp, 1)
                    act.wait_ge(pe_vt, t + 1)
                    act.activation(v_tok, ps[3][:, :], ACT.Copy).then_inc(vtok_out, 1)
                    act.wait_ge(pe_pv, t + 2)
                    act.activation(vT, ps[0][:, :], ACT.Copy).then_inc(vT_out, 1)
                    act.wait_ge(pe_kt, t + 1)
                    act.activation(k_tok, ps[3][:, :], ACT.Copy).then_inc(ktok_out, 1)
                    act.wait_ge(pe_pq, t + 2)
                    act.activation(th[0], ps[1][:, :], ACT.Tanh, scale=0.5).then_inc(tanh_out, 1)
                    act.wait_ge(pe_pk, t + 2)
                    act.activation(th[1], ps[0][:, :], ACT.Tanh, scale=0.5).then_inc(tanh_out, 1)
                    act.wait_ge(pe_pt, t + 1)
                    act.activation(p_tok, ps[3][:, :], ACT.Copy).then_inc(ptok_out, 1)
                    act.wait_ge(pe_o, t + 1)
                    act.activation(oT, ps[1][:, :], ACT.Copy).then_inc(oT_out, 1)
                    for be, bank in ((0, 0), (1, 3)):
                        act.wait_ge(pe_wt, t * 2 + (be + 1))
                        act.activation(w_outT[:, be * 1024:(be + 1) * 1024], ps[bank][:, :], ACT.Copy).then_inc(woutT_out, 1)
            finish(act, 9)

            squares_and_std(3)
            out_of_turn(3)
            act.wait_ge(oh_done, 2)
            act.activation(pr1, sh1, ACT.Exp).then_inc(ex_done, 1)
            finish(act, 10)
            g0 = TILES0 // GRP
            act.wait_ge(f1_b, 32)
            with act.Fori(0, E) as e:
                act.wait_ge(x_turned, e + (g0 + 3))
                act.activation(xg1, ps[0][:, 0:2 * C], ACT.Copy).then_inc(xg_ready, 1)
                act.wait_ge(h_mm, e + (TILES0 + 1))
                for j in range(4):
                    last = act.activation(hg1[:, j * 256:(j + 1) * 256], ps[1][:, j * 256:(j + 1) * 256],
                                          ACT.Gelu_apprx_tanh, bias=b1t[:, ds(e * 4 + j, 1)])
                last.then_inc(hg_ready, 1)
            finish(act, 11)
            finish(act, 12)

        @block.vector
        def _(dve):
            chain = Chain(dve, dve_step)
            dve.wait_ge(cond_tanh, 1)
            chain.link(dve.scalar_tensor_tensor(cth, cth, 1.0, ct, ALU.add, ALU.mult))
            for l in range(2):
                dve.tensor_scalar(st[l].rearrange("k (b n) -> k b n", n=CH),
                                  cth[:, 8 * l:8 * l + 8].unsqueeze(2).to_broadcast([P, B, CH]), 0.5, None, ALU.mult
                                  ).then_inc(cond_spread, 1)
            dve.wait_ge(a0_exp, 1)
            chain.link(dve.tensor_scalar(tmp1[:, 1:2], tmp1[:, 0:1], 1.0, None, ALU.add))
            chain.link(dve.reciprocal(dts, tmp1[:, 1:2]))
            chain.link(dve.scalar_tensor_tensor(tmp1[:, 2:3], a2, -1.0, a2, ALU.mult, ALU.max))
            dve.tensor_tensor(tmp1[:, 3:4], tmp1[:, 2:3], dts, ALU.mult).then_inc(a0_par, 1)
            chain.link(dve.tensor_scalar(nb, bmat, normw, None, ALU.mult))
            dve.wait_ge(a0_exp, 2)
            chain.link(dve.tensor_copy(a_bc, decay.to_broadcast([P, L])))
            for l in range(2):
                dve.wait_ge(mod_out, BP * (l + 1))
                m = mod[l][:, :].rearrange("p (b j c) -> p b j c", j=6, c=C)
                t3 = xc[:, 0:BP * C].rearrange("p (b c) -> p b c", c=C)
                t4 = xc[:, BP * C:2 * BP * C].rearrange("p (b c) -> p b c", c=C)
                for j in (CA, CB):
                    chain.link(dve.tensor_scalar(m[:, :, j, :], m[:, :, j, :], 1.0, None, ALU.add))
                for j in (GA, GB):
                    g = m[:, :, j, :]
                    chain.link(dve.tensor_scalar(t3, g, 0.0, 2.0, ALU.is_ge, ALU.mult))
                    chain.link(dve.scalar_tensor_tensor(t4, g, -1.0, g, ALU.mult, ALU.max))
                    chain.link(dve.tensor_scalar(t4, t4, 0.25, None, ALU.max))
                    chain.link(dve.scalar_tensor_tensor(g, t3, -1.0, t4, ALU.add, ALU.mult))
            m = mod[0][:, :].rearrange("p (b j c) -> p b j c", j=6, c=C)
            chain.link(dve.tensor_tensor(ga_d[:, :].rearrange("p (b c) -> p b c", c=C), m[:, :, GA, :],
                                         d_bc.unsqueeze(1).to_broadcast([P, BP, C]), ALU.mult))
            dve.wait_ge(x_in, 16 * B)
            finish(dve, 1)

            def layer_norm(l, k, j):
                with dve.Fori(0, BP) as i:
                    chain.enter(i, 1)
                    chain.link(dve.tensor_reduce(sums[:, ds(i * NC, NC)], tiles(x_sb, i), AX_X, ALU.add))
                    dve.scalar_tensor_tensor(tiles(xc, i), sums[:, ds(i * NC, NC)].unsqueeze(2).to_broadcast([P, NC, C]),
                                             -1.0 / C, tiles(x_sb, i), ALU.mult, ALU.add).then_inc(ln_centered, 1)
                chain.leave(BP)
                with dve.Fori(0, BP) as i:
                    dve.wait_ge(ln_squared, i + (4 * k + 1))
                    dve.tensor_reduce(var[:, ds(i * NC, NC)], tiles(sq, i), AX_X, ALU.add).then_inc(ln_var, 1)
                dve.wait_ge(ln_std, k + 1)
                chain.link(dve.reciprocal(rstd, rstd))
                with dve.Fori(0, BP) as i:
                    chain.enter(i, 1)
                    chain.link(dve.tensor_tensor(tiles(xc, i), tiles(xc, i),
                                                 rstd[:, ds(i * NC, NC)].unsqueeze(2).to_broadcast([P, NC, C]), ALU.mult))
                    dve.tensor_tensor(tiles(xc, i), tiles(xc, i), over_tiles(mod_of(l, i, j)), ALU.mult
                                      ).then_inc(ln_scaled, 1)
                chain.leave(BP)

            layer_norm(0, 0, CA)
            with dve.Fori(0, BP) as bp:
                chain.enter(bp, 2)
                dve.wait_ge(a0_rms, bp + 1)
                chain.link(dve.reciprocal(us, rms))
                chain.link(dve.scalar_tensor_tensor(us, ps[2][:, L:2 * L], dts, us, ALU.mult, ALU.mult))
                dve.tensor_tensor_scan(xs, a_bc, us, 0.0, ALU.mult, ALU.add).then_inc(a0_scan, 1)
                dve.wait_ge(a0_y, bp + 1)
                dve.wait_ge(a0_yg_used, bp + 1)
                dve.tensor_tensor(yg.rearrange("p (t c) -> p t c", c=C), ps[3][:, :].rearrange("p (t c) -> p t c", c=C),
                                  over_tiles(mod_of(0, bp, GA)), ALU.mult).then_inc(a0_gated, 1)
            chain.leave(BP)
            finish(dve, 2)

            def logits_out(k, dst):
                with dve.Fori(0, 2) as i:
                    for u in range(2):
                        bp = i * 2 + u
                        dve.wait_ge(lg_mm, bp + (4 * k + 1))
                        dve.tensor_copy(dst[:, ds(bp * (NC * E), NC * E)], ps[2][:, u * 512:u * 512 + NC * E]).then_inc(lg_out, 1)

            te = lambda ap: ap.rearrange("p (t e) -> p t e", e=E)
            over_e = lambda ap: ap.unsqueeze(2).to_broadcast([P, ap.shape[1], E])
            over_t = lambda ap, n=T: ap.unsqueeze(1).to_broadcast([P, n, ap.shape[1]])

            dve.wait_ge(gw, 32)
            chain.link(dve.tensor_tensor(wg_n[0:E, :], wg_s[0:E, :], wg_s[0:E, :], ALU.mult))
            dve.tensor_reduce(wg_t[0:E, 0:1], wg_n[0:E, :], AX_X, ALU.add).then_inc(gw, 1)
            dve.wait_ge(gw, 34)
            chain.link(dve.tensor_scalar(wg_t[0:E, 1:2], wg_n[0:E, 0:1], 1e-4, None, ALU.max))
            chain.link(dve.reciprocal(wg_t[0:E, 2:3], wg_t[0:E, 1:2]))
            dve.tensor_scalar(wg_n[0:E, :], wg_s[0:E, :], wg_t[0:E, 2:3], None, ALU.mult).then_inc(gw, 1)
            dve.wait_ge(gw, 36)
            dve.tensor_copy(wg_t[0:16, :], ps[3][0:16, 0:E]).then_inc(gw, 1)
            dve.wait_ge(gw, 38)
            dve.tensor_copy(w_gate, ps[3][:, 512:512 + E]).then_inc(gw, 1)
            layer_norm(0, 1, CB)
            logits_out(0, logits)
            finish(dve, 3)
            chain.link(dve.tensor_reduce(mx, te(logits), AX_X, ALU.max))
            chain.link(dve.tensor_tensor(te(shifted), te(logits), over_e(mx), ALU.subtract))
            chain.link(dve.scalar_tensor_tensor(te(pick), te(shifted), 0.0, over_t(first_w), ALU.is_equal, ALU.mult))
            dve.tensor_reduce(m2, te(pick), AX_X, ALU.max).then_inc(oh_done, 1)
            dve.wait_ge(oh_done, 1)
            chain.link(dve.tensor_tensor(te(onehot), te(pick), over_e(m2), ALU.is_equal))
            dve.tensor_copy(onehot_b, onehot).then_inc(rhs_ready, 1)
            dve.wait_ge(ex_done, 1)
            chain.link(dve.tensor_reduce(e_sum, te(e_exp), AX_X, ALU.add))
            chain.link(dve.reciprocal(score, e_sum))
            dve.wait_ge(cnt_done, 1)
            before_p, totals = ps[3][:, 0:256], ps[3][:, 512:768]
            for e in range(E):
                last = dve.tensor_tensor_scan(te(cum)[:, :, e], ones_f[:, 0:T], te(totals)[:, :, e], 0.0, ALU.mult, ALU.add)
            chain.link(last)
            chain.link(dve.tensor_tensor(rank, cum, totals, ALU.subtract))
            chain.link(dve.tensor_tensor(rank, rank, before_p, ALU.add))
            cnt = te(cum)[:, T - 1, :]
            c3 = n_cmp[:, 0:E * T].rearrange("p (e t) -> p e t", t=T)
            chain.link(dve.tensor_tensor(c3, cnt.unsqueeze(2).to_broadcast([P, E, T]), over_t(edges, E), ALU.is_gt))
            chain.link(dve.tensor_reduce(n_tiles[:, 0:E], c3, AX_X, ALU.add))
            chain.link(dve.tensor_tensor_scan(t_end[:, 0:E], ones_f[:, 0:E], n_tiles[:, 0:E], 0.0, ALU.mult, ALU.add))
            chain.link(dve.tensor_tensor(t_start[:, 0:E], t_end[:, 0:E], n_tiles[:, 0:E], ALU.subtract))
            chain.link(dve.tensor_scalar(t_start[:, 0:E], t_start[:, 0:E], float(P), None, ALU.mult))
            chain.link(dve.tensor_tensor(te(rank), te(rank), over_t(t_start[:, 0:E]), ALU.add))
            chain.link(dve.tensor_tensor(rank, rank, onehot, ALU.mult))
            chain.link(dve.tensor_reduce(slot_f, te(rank), AX_X, ALU.add))
            chain.link(dve.tensor_copy(slot_i[:, 0:T], slot_f))
            chain.link(dve.tensor_scalar(tile_i, slot_i[:, 0:T], 7, None, ALU.arith_shift_right))
            chain.link(dve.tensor_copy(tile_f, tile_i))
            chain.link(dve.scalar_tensor_tensor(row_f, tile_f, -float(P), slot_f, ALU.mult, ALU.add))
            c3 = n_cmp.rearrange("p (t e) -> p t e", e=E)
            chain.link(dve.tensor_tensor(c3, iota_t.unsqueeze(2).to_broadcast([P, 40, E]), over_t(t_end[:, 0:E], 40), ALU.is_ge))
            chain.link(dve.tensor_reduce(t_exp_f, c3, AX_X, ALU.add))
            chain.link(dve.tensor_scalar(t_exp_f, t_exp_f, float(E - 1), None, ALU.min))
            chain.link(dve.tensor_copy(t_exp_i, t_exp_f))
            t3 = tile_hot.rearrange("p (t s) -> p t s", s=40)
            r3 = t_rhs.rearrange("p (t k s) -> p t k s", k=2, s=40)
            chain.link(dve.tensor_tensor(t3, over_t(iota_t), tile_f.unsqueeze(2).to_broadcast([P, T, 40]), ALU.is_equal))
            dve.tensor_tensor(r3[:, :, 0, :], t3, tile_no.unsqueeze(2).to_broadcast([P, T, 40]), ALU.mult)
            dve.tensor_scalar(r3[:, :, 1, :], t3, part_no, None, ALU.mult).then_inc(rhs_ready, 1)
            with dve.Fori(0, T // 8) as i:
                dve.tensor_tensor(r_hot[:, ds(i * (8 * P), 8 * P)].rearrange("p (t s) -> p t s", s=P), over_t(iota_b[:, 0:P], 8),
                                  row_f[:, ds(i * 8, 8)].unsqueeze(2).to_broadcast([P, 8, P]), ALU.is_equal).then_inc(hot_made, 1)
            dve.wait_ge(ids_mm, 1)
            chain.link(dve.tensor_copy(id_f, ps[2][:, 0:80]))
            chain.link(dve.scalar_tensor_tensor(id_f[:, 0:40], id_f[:, 0:40], float(P), id_f[:, 40:80], ALU.mult, ALU.add))
            chain.link(dve.tensor_copy(ids_i, id_f[:, 0:40]))
            finish(dve, 4)
            dve.wait_ge(f0_w, 64)

            def add_bias1(g):
                for t in range(GRP):
                    e = dve.value_load(t_exp_i[0:1, ds(g * GRP + t, 1)], min_val=0, max_val=E - 1)
                    dve.wait_ge(h_mm, g * GRP + (t // 2 * 2 + 2))
                    dve.tensor_tensor(hb[:, t * F0:(t + 1) * F0], ps[1][:, t * F0:(t + 1) * F0], b1a[:, ds(e * F0, F0)],
                                      ALU.add).then_inc(hb_ready, 1)

            def turned_out(g):
                dve.wait_ge(hg_turned, g + 1)
                dve.tensor_copy(hgT, ps[2][:, :]).then_inc(hgT_ready, 1)

            def add_bias2(g, u, i):
                dve.wait_ge(o_stored[u], i * 16 + 16)
                apart(dve)
                for t in range(GRP):
                    e = dve.value_load(t_exp_i[0:1, ds(g * GRP + t, 1)], min_val=0, max_val=E - 1)
                    dve.wait_ge(o_mm, g * GRP + GRP)
                    dve.tensor_tensor(o_st[u][:, t * C:(t + 1) * C], ps[3][:, t * C:(t + 1) * C], b2a[:, ds(e * C, C)],
                                      ALU.add).then_inc(o_ready, 1)

            with dve.Fori(0, TILES0 // GRP // 2) as i:
                for u in range(2):
                    g = i * 2 + u
                    add_bias1(g)
                    turned_out(g)
                    add_bias2(g, u, i)
            finish(dve, 5)

            def combine(l, f, n_back):
                with dve.Fori(0, 2) as i:
                    for u in range(2):
                        bp = i * 2 + u
                        b3 = [back[2 * u + k].rearrange("p (t c) -> p t c", c=C) for k in range(f + 1)]
                        chain.enter(i * 2 + u, 0)
                        dve.wait_ge(back_in[u], i * (128 * (f + 1)) + (256 * f + 128 * (f + 1)))
                        per = 3 * f + 2
                        for k in range(f + 1):
                            w = (score if f == 0 else wk[:, k * T:(k + 1) * T])[:, ds(bp * NC, NC)]
                            dve.tensor_tensor(b3[k], b3[k], w.unsqueeze(2).to_broadcast([P, NC, C]), ALU.mult).then_inc(dve_step2, 1)
                        n = n_back + f + 1
                        dve.wait_ge(dve_step2, bp * per + n)
                        if f:
                            dve.tensor_tensor(b3[0], b3[0], b3[1], ALU.add).then_inc(dve_step2, 1)
                            n += 1
                            dve.wait_ge(dve_step2, bp * per + n)
                        dve.tensor_tensor(b3[0], b3[0], over_tiles(mod_of(l, bp, GB)), ALU.mult).then_inc(dve_step2, 1)
                        n += 1
                        dve.wait_ge(dve_step2, bp * per + n)
                        if f:
                            dve.tensor_tensor(tiles(x_sb, bp), tiles(x_sb, bp), b3[0], ALU.add).then_inc(dve_step2, 1)
                            n += 1
                            dve.wait_ge(dve_step2, bp * per + n)
                            dve.sem_inc(back_used, 1)
                        else:
                            dve.tensor_tensor(tiles(x_sb, bp), tiles(x_sb, bp), b3[0], ALU.add).then_inc(back_used, 1)
                        chain.base, chain.k = chain.outer, 0
                return n_back + 4 * (3 * f + 2)

            n_back = combine(0, 0, 0)
            finish(dve, 6)

            layer_norm(1, 2, CA)
            finish(dve, 7)
            with dve.Fori(0, 4) as i:
                for u in range(2):
                    n = i * 2 + u
                    dve.wait_ge(rt_tanh, n + 1)
                    dve.tensor_reduce(rate_sums[0:64, ds(n * 8, 8)], tg[u][0:64, :].rearrange("r (g n) -> r g n", n=CH),
                                      AX_X, ALU.add).then_inc(rt_sum, 1)
            dve.wait_ge(rt_sum, 10)
            dve.tensor_copy(rate_spread[0:32, :].rearrange("r (g n) -> r g n", n=CH),
                            rate_sums[0:32, :].unsqueeze(2).to_broadcast([32, 64, CH])).then_inc(rt_spread, 1)
            dve.wait_ge(rt_wd, 1)
            for k in range(2):
                dve.tensor_scalar(wd.rearrange("r (g k p) -> r k p g", k=2, p=HP)[:, k],
                                  ps[2][:, k * 512:(k + 1) * 512].rearrange("r (p g) -> r p g", p=HP),
                                  BASE_WD * 0.5 / CH, BASE_WD * 0.5, ALU.mult, ALU.add)
            dve.wait_ge(rt_lr, 1)
            for k in range(2):
                f = BASE_LR * (0.25, 0.5)[k]
                dve.tensor_scalar(lr.rearrange("r (t k h) -> r k t h", k=2, h=H)[:, k],
                                  ps[3][:, :].rearrange("r (t k h) -> r k t h", k=2, h=H)[:, k],
                                  f / CH, f, ALU.mult, ALU.add)
            finish(dve, 8)

            for j, bank in ((0, 1), (1, 2)):
                dve.wait_ge(tanh_out, j + 1)
                dve.scalar_tensor_tensor(qk[:, j * 1024:(j + 1) * 1024], th[j], 1.0, ps[bank][:, :],
                                         ALU.add, ALU.mult).then_inc(silu_done, 1)
            with dve.Fori(0, BP) as bp:
                dve.wait_ge(win_new, bp * (2 * NC) + 2)
                for be in range(2):
                    dve.tensor_copy(w_in[:, be * 1024:(be + 1) * 1024], w_init[:, 0:1024]).then_inc(win_set, 1)
                with dve.Fori(0, NC) as c:
                    t = bp * NC + c
                    chain.enter(t, 6)
                    for be in range(2):
                        g = slice(16 * be, 16 * be + 16)
                        z3 = zs[:, be * 1024:(be + 1) * 1024].rearrange("r (g n) -> r g n", n=CH)
                        p3 = ps[be][:, :].rearrange("r (g n) -> r g n", n=CH)
                        dve.wait_ge(pe_z, t * 2 + (be + 1))
                        chain.link(dve.tensor_reduce(z_max[:, g], p3, AX_X, ALU.max))
                        dve.tensor_tensor(z3, p3, z_max[:, g].unsqueeze(2).to_broadcast([P, 16, CH]), ALU.subtract
                                          ).then_inc(z_centered, 1)
                    for be in range(2):
                        g = slice(16 * be, 16 * be + 16)
                        dve.wait_ge(z_exp, t * 2 + (be + 1))
                        chain.link(dve.tensor_reduce(z_sum[:, g], zs[:, be * 1024:(be + 1) * 1024].rearrange(
                            "r (g n) -> r g n", n=CH), AX_X, ALU.add))
                        dve.reciprocal(z_rec[:, g], z_sum[:, g]).then_inc(z_summed, 1)
                    dve.wait_ge(z_summed, t * 2 + 2)
                    z4 = zs.rearrange("r (e p k n) -> r e p k n", e=2, p=HP, k=2)
                    r4 = z_rec.rearrange("r (e p k) -> r e p k", e=2, p=HP)
                    dve.tensor_tensor(prob[:, 1024:2048].rearrange("r (p e n) -> r e p n", e=2, n=CH), z4[:, :, :, 1, :],
                                      r4[:, :, :, 1].unsqueeze(3).to_broadcast([P, 2, HP, CH]), ALU.mult).then_inc(pk_norm, 1)
                    for j, bank in ((0, 1), (1, 0)):
                        dve.wait_ge(tanh_out, t * 2 + (j + 3))
                        dve.scalar_tensor_tensor(qk[:, j * 1024:(j + 1) * 1024], th[j], 1.0, ps[bank][:, :],
                                                 ALU.add, ALU.mult).then_inc(silu_done, 1)
                    h3 = lambda ap: ap.rearrange("r (h d) -> r h d", d=D)
                    dve.wait_ge(pe_a, t + 1)
                    dve.wait_ge(ptok_out, t + 1)
                    chain.link(dve.tensor_tensor(pa, p_tok, ps[2][:, :], ALU.mult))
                    chain.link(dve.tensor_reduce(s_sum, h3(pa), AX_X, ALU.add))
                    dve.tensor_tensor(h3(pa), h3(ps[2][:, :]), s_sum.unsqueeze(2).to_broadcast([P, H, D]), ALU.subtract
                                      ).then_inc(dve_step2, 1)
                    dve.wait_ge(dve_step2, t + (n_back + 1))
                    dve.tensor_tensor(g_tok, pa, p_tok, ALU.mult).then_inc(g_done, 1)

                    def update(w, k, be, bank, done):
                        for h in range(2):
                            half = slice(h * D, h * D + D)
                            last = dve.tensor_tensor(
                                w[half, be * 1024:(be + 1) * 1024].rearrange("r (p c) -> r p c", c=P)[:, :, half],
                                w_dec[half, (2 * k + be) * 1024:(2 * k + be + 1) * 1024].rearrange("r (p c) -> r p c", c=P)[:, :, half],
                                ps[bank][half, :].rearrange("r (p c) -> r p c", c=P)[:, :, half], ALU.add)
                        last.then_inc(done, 1)

                    for be, bank in ((0, 0), (1, 3)):
                        dve.wait_ge(dec_done, t * 2 + (be + 1))
                        dve.wait_ge(pe_gout, t * 2 + (be + 1))
                        update(w_out, 1, be, bank, wout_new)
                    dve.wait_ge(pe_y, t + 1)
                    dve.wait_ge(x_added, t + 1)
                    dve.tensor_tensor(y_gated, ps[1][:, 0:C], mod_of(1, bp, GA), ALU.mult).then_inc(y_scaled, 1)
                    for be, bank in ((0, 2), (1, 1)):
                        dve.wait_ge(pe_gin, t * 2 + (be + 1))
                        update(w_in, 0, be, bank, win_new)
            chain.base = chain.outer + T * chain.per
            chain.k = 0
            finish(dve, 9)

            layer_norm(1, 3, CB)
            logits_out(1, lg1)
            dve.wait_ge(lg_out, 10)
            chain.link(dve.tensor_reduce(mx, te(lg1), AX_X, ALU.max))
            dve.tensor_tensor(te(sh1), te(lg1), over_e(mx), ALU.subtract).then_inc(oh_done, 1)
            dve.wait_ge(ex_done, 2)
            chain.link(dve.tensor_reduce(e_sum, te(pr1), AX_X, ALU.add))
            chain.link(dve.reciprocal(e_sum, e_sum))
            chain.link(dve.tensor_tensor(te(pr1), te(pr1), over_e(e_sum), ALU.mult))
            top = [slot_f, tile_f]
            for k in range(2):
                hot = oh1[:, k * 256:(k + 1) * 256]
                chain.link(dve.tensor_reduce(top[k], te(pr1), AX_X, ALU.max))
                chain.link(dve.tensor_tensor(te(sh1), te(pr1), over_e(top[k]), ALU.is_equal))
                chain.link(dve.tensor_tensor(te(sh1), te(sh1), over_t(first_w), ALU.mult))
                chain.link(dve.tensor_reduce(m2, te(sh1), AX_X, ALU.max))
                chain.link(dve.tensor_tensor(te(hot), te(sh1), over_e(m2), ALU.is_equal))
                if k == 0:
                    chain.link(dve.scalar_tensor_tensor(pr1, hot, -2.0, pr1, ALU.mult, ALU.add))
            dve.tensor_copy(ohb1, oh1).then_inc(rhs_ready, 1)
            chain.link(dve.tensor_tensor(row_f, top[0], top[1], ALU.add))
            chain.link(dve.tensor_scalar(row_f, row_f, 1e-9, None, ALU.add))
            chain.link(dve.reciprocal(row_f, row_f))
            for k in range(2):
                chain.link(dve.tensor_tensor(wk[:, k * T:(k + 1) * T], top[k], row_f, ALU.mult))
            dve.wait_ge(cnt_done, 2)
            own, both, pref = ps[3][:, 512:1024], ps[2][:, 0:512], ps[3][:, 0:512]
            sums_over_c = lambda ap: ap.rearrange("p (k c e) -> p k e c", c=NC, e=E)
            k3 = lambda ap: ap.rearrange("p (k e) -> p k e", e=E)
            chain.link(dve.tensor_reduce(k3(own_t), sums_over_c(own), AX_X, ALU.add))
            chain.link(dve.tensor_reduce(k3(both_t), sums_over_c(both), AX_X, ALU.add))
            chain.link(dve.tensor_tensor(off1, both_t, own_t, ALU.subtract))
            chain.link(dve.tensor_scalar(off1, off1, batch_bit, None, ALU.mult))
            b4, o4 = (ap.rearrange("p (k b e) -> p k b e", k=2, b=BP) for ap in (both_t, off1))
            c2 = k3(cnt1)
            chain.link(dve.memset(cnt1, 0.0))
            for b in range(BP):
                chain.link(dve.tensor_tensor(o4[:, :, b, :], o4[:, :, b, :], c2, ALU.add))
                chain.link(dve.tensor_tensor(c2, c2, b4[:, :, b, :], ALU.add))
            chain.link(dve.tensor_scalar(cnt1[:, 0:E], cnt1[:, 0:E], float(CAP), None, ALU.min))
            chain.link(dve.tensor_tensor(o4[:, 1, :, :], o4[:, 1, :, :], cnt1[:, 0:E].unsqueeze(1).to_broadcast([P, BP, E]), ALU.add))
            r4, w4 = (ap.rearrange("p (k c e) -> p k c e", c=NC, e=E) for ap in (run1, own))
            chain.link(dve.tensor_copy(r4[:, :, 0, :], k3(off1)))
            for c in range(1, NC):
                chain.link(dve.tensor_tensor(r4[:, :, c, :], r4[:, :, c - 1, :], w4[:, :, c - 1, :], ALU.add))
            chain.link(dve.tensor_tensor(rk1, run1, pref, ALU.add))
            chain.link(dve.tensor_tensor(scr1, rk1, oh1, ALU.mult))
            chain.link(dve.tensor_reduce(pos, te(scr1), AX_X, ALU.add))
            chain.link(dve.tensor_tensor(te(scr1), te(oh1), over_t(iota_e, 2 * T), ALU.mult))
            chain.link(dve.tensor_reduce(e_of, te(scr1), AX_X, ALU.add))
            chain.link(dve.tensor_scalar(keep, pos, float(CAP), None, ALU.is_lt))
            chain.link(dve.tensor_tensor(wk, wk, keep, ALU.mult))
            chain.link(dve.scalar_tensor_tensor(e_of, e_of, float(CAP), pos, ALU.mult, ALU.add))
            chain.link(dve.tensor_tensor(e_of, e_of, keep, ALU.mult))
            chain.link(dve.tensor_copy(slot_i, e_of))
            r5 = rhs1.rearrange("p (t m e) -> p t m e", m=2, e=E)
            for k in range(2):
                dve.tensor_tensor(r5[:, k * T:(k + 1) * T, 0, :], te(oh1[:, k * 256:(k + 1) * 256]), over_e(tile_no), ALU.mult)
            dve.tensor_scalar(r5[:, :, 1, :], te(oh1), part_no, None, ALU.mult).then_inc(rhs_ready, 1)
            with dve.Fori(0, T // 2) as i:
                for u in range(2):
                    t = i * 2 + u
                    dve.wait_ge(hot_used, t + 1)
                    for k in range(2):
                        last = dve.tensor_scalar(pos_hot[u][:, k * CAP:(k + 1) * CAP], iota_b[:, :], pos[:, ds(t + k * T, 1)],
                                                 None, ALU.is_equal)
                    last.then_inc(hot_made, 1)
            dve.wait_ge(ids_mm, 2)
            id3 = id_f[:, 0:32].rearrange("p (j m) -> p j m", j=2)
            chain.link(dve.tensor_copy(id3, ps[0][:, :].rearrange("p (j m) -> p j m", j=2)[:, :, 0:16]))
            chain.link(dve.scalar_tensor_tensor(id3[:, :, 0:E], id3[:, :, 0:E], float(P), id3[:, :, E:2 * E], ALU.mult, ALU.add))
            chain.link(dve.tensor_copy(ids_i[:, 0:2 * E].rearrange("p (j e) -> p j e", j=2), id3[:, :, 0:E]))
            dve.sem_inc(ids_ready, 2)
            finish(dve, 10)
            with dve.Fori(0, E // 2) as i:
                for u in range(2):
                    e = i * 2 + u
                    dve.wait_ge(o_stored[u], i * 16 + (16 * (TILES0 // GRP // 2) + 16))
                    dve.wait_ge(o_mm, e + (TILES0 + 1))
                    dve.tensor_tensor(o1_st[u].rearrange("p (t c) -> p t c", c=C), ps[3][:, 0:2 * C].rearrange("p (t c) -> p t c", c=C),
                                      over_tiles(b2b[:, ds(e * C, C)], 2), ALU.add).then_inc(o_ready, 1)
            finish(dve, 11)
            n_back = combine(1, 1, n_back + T)
            finish(dve, 12)

        @block.tensor
        def _(pe):
            pe.wait_ge(wm_in, 32)
            for l in range(2):
                pe.wait_ge(cond_spread, l + 1)
                for bp in range(BP):
                    n = BP * l + bp
                    if n >= 4:
                        pe.wait_ge(mod_out, n - 3)
                    for a, b in ((0, 512), (512, 768)):
                        mm = pe.matmul(ps[n % 4][:, a:b], st[l][:, bp * P:(bp + 1) * P], wm[l][:, a:b],
                                       start=True, stop=True)
                    mm.then_inc(mod_mm, 1)
            pe.wait_ge(consts_made, 1)
            pe.sem_inc(a0_yg_used, 1)
            finish(pe, 1)

            def turn(u, bp, k, last_use):
                pe.wait_ge(h_ready, bp + (4 * k + 1))
                for t in range(NC):
                    mm = pe.transpose(ps[u][:, t * P:(t + 1) * P], h_st[u][:, t * C:(t + 1) * C], ident[:, :])
                mm.then_inc(h_turned, 1)

            with pe.Fori(0, 2) as i:
                for u in range(2):
                    bp = i * 2 + u
                    turn(u, bp, 0, None)
                    pe.wait_ge(a0_sq, bp + 1)
                    for be in range(2):
                        pe.matmul(ps[2][be * S:(be + 1) * S, 0:L], ones_f[:, 0:S], hsq[:, be * L:(be + 1) * L],
                                  start=True, stop=True)
                    for be in range(2):
                        mm = pe.matmul(ps[2][be * S:(be + 1) * S, L:2 * L], nb, hT_st[u][:, be * L:(be + 1) * L],
                                       start=True, stop=True)
                    mm.then_inc(a0_up, 1)
                    pe.wait_ge(a0_scan, bp + 1)
                    apart(pe)
                    for t in range(NC):
                        for be in range(2):
                            half = slice(be * S, be * S + S)
                            mm = pe.matmul(ps[3][be * CH:(be + 1) * CH, t * C:(t + 1) * C],
                                           xs[half, t * CH:(t + 1) * CH], cmat[half, :], start=True, stop=True)
                    mm.then_inc(a0_y, 1)
            finish(pe, 2)

            def turn_and_gate(k, f, w):
                with pe.Fori(0, 2) as i:
                    for u in range(2):
                        bp = i * 2 + u
                        turn(u, bp, k, None)
                        pe.wait_ge(hT_ready, bp + (4 * k + 1))
                        pe.wait_ge(lg_out, bp + (4 * f + 1))
                        for t in range(NC):
                            mm = pe.matmul(ps[2][:, u * 512 + t * E:u * 512 + (t + 1) * E], hT_st[u][:, t * P:(t + 1) * P], w,
                                           start=True, stop=True)
                        mm.then_inc(lg_mm, 1)

            pe.wait_ge(gw, 35)
            pe.transpose(ps[3][0:16, 0:E], wg_n[0:E, :], ident[0:E, 0:E]).then_inc(gw, 1)
            pe.wait_ge(gw, 37)
            pe.matmul(ps[3][:, 512:512 + E], wred_t[0:16, :], wg_t[0:16, :], start=True, stop=True).then_inc(gw, 1)
            pe.wait_ge(gw, 39)
            pe.sem_inc(lg_out, 2)
            turn_and_gate(1, 0, w_gate)
            pe.sem_inc(x_turned, 2)
            pe.sem_inc(back_used, 2)
            finish(pe, 3)
            pe.wait_ge(rhs_ready, 1)
            pe.matmul(ps[3][:, 0:T * E], before, onehot_b, start=True, stop=True)
            pe.matmul(ps[3][:, 512:512 + T * E], all_ones, onehot_b, start=True, stop=True).then_inc(cnt_done, 1)
            pe.wait_ge(rhs_ready, 2)
            for t in range(T):
                if t % 8 == 0:
                    pe.wait_ge(hot_made, t // 8 + 1)
                mm = pe.matmul(ps[2][:, 0:80], r_hot[:, t * P:(t + 1) * P], t_rhs[:, t * 80:(t + 1) * 80],
                               start=(t == 0), stop=(t == T - 1))
            mm.then_inc(ids_mm, 1)
            finish(pe, 4)

            pe.wait_ge(f0_w, 64)

            def turn_x(g, u, i):
                pe.wait_ge(gathered[u], i * (16 * GRP) + 16 * GRP)
                for t in range(GRP):
                    mm = pe.transpose(ps[0][:, t * P:(t + 1) * P], gx[u][:, t * C:(t + 1) * C], ident[:, :])
                mm.then_inc(x_turned, 1)

            def first_product(g):
                pe.wait_ge(xg_ready, g + 1)
                for t in range(GRP):
                    e = pe.value_load(t_exp_i[0:1, ds(g * GRP + t, 1)], min_val=0, max_val=E - 1)
                    pe.matmul(ps[1][:, t * F0:(t + 1) * F0], xg[:, t * P:(t + 1) * P], w1a[:, ds(e * F0, F0)],
                              start=True, stop=True).then_inc(h_mm, 1)

            def turn_hidden(g):
                pe.wait_ge(hg_ready, g + 1)
                for t in range(2 * GRP):
                    mm = pe.transpose(ps[2][:, t * P:(t + 1) * P], hb[:, t * P:(t + 1) * P], ident[:, :])
                mm.then_inc(hg_turned, 1)

            def second_product(g):
                pe.wait_ge(hgT_ready, g + 1)
                apart(pe)
                for t in range(GRP):
                    e = pe.value_load(t_exp_i[0:1, ds(g * GRP + t, 1)], min_val=0, max_val=E - 1)
                    for j in range(2):
                        mm = pe.matmul(ps[3][:, t * C:(t + 1) * C], hgT[:, (2 * t + j) * P:(2 * t + j + 1) * P],
                                       w2a[:, ds(e * F0 + j * C, C)], start=(j == 0), stop=(j == 1))
                    mm.then_inc(o_mm, 1)

            with pe.Fori(0, TILES0 // GRP // 2) as i:
                for u in range(2):
                    g = i * 2 + u
                    turn_x(g, u, i)
                    first_product(g)
                    turn_hidden(g)
                    second_product(g)
            finish(pe, 5)
            finish(pe, 6)

            with pe.Fori(0, 2) as i:
                for u in range(2):
                    bp = i * 2 + u
                    pe.wait_ge(hT_ready, bp + (2 * BP - 1))
                    turn(u, bp, 2, None)
            pe.sem_inc(rt_sum, 2)
            finish(pe, 7)
            pe.wait_ge(wlb_in, 32)
            with pe.Fori(0, 4) as i:
                for u in range(2):
                    n = i * 2 + u
                    pe.wait_ge(rt_sum, n + 1)
                    pe.matmul(ps[u][0:64, 0:512], w_lb, hT[:, ds(n * 512, 512)], start=True, stop=True).then_inc(rt_mm, 1)
            pe.wait_ge(rt_sum, 10)
            for n in range(2 * HP):
                mm = pe.matmul(ps[2][:, n * 64:(n + 1) * 64], sel[0:64, n * P:(n + 1) * P], rate_sums[0:64, :],
                               start=True, stop=True)
            mm.then_inc(rt_wd, 1)
            pe.wait_ge(rt_spread, 1)
            for t in range(T):
                mm = pe.matmul(ps[3][:, t * 32:(t + 1) * 32], rate_spread[0:32, t * P:(t + 1) * P], ident[0:32, 0:32],
                               start=True, stop=True)
            mm.then_inc(rt_lr, 1)
            pe.sem_inc(win_new, 2)
            pe.sem_inc(wout_new, 2)
            pe.sem_inc(woutT_out, 2)
            finish(pe, 8)

            def project(j, bank, at, done):
                for p in range(HP):
                    mm = pe.matmul(ps[bank][:, p * P:(p + 1) * P], w_qkv[:, j * HD + p * P:j * HD + (p + 1) * P],
                                   hT[:, ds(at, P)], start=True, stop=True)
                mm.then_inc(done, 1)

            def turn_pairs(src, bank, done):
                for p in range(HP):
                    mm = pe.transpose(ps[bank][:, p * P:(p + 1) * P], src(p), ident[:, :])
                mm.then_inc(done, 1)

            def gradient(left, right, be, bank, done):
                half = slice(be * CH, be * CH + CH)
                for p in range(HP):
                    c = slice(p * P, (p + 1) * P)
                    mm = pe.matmul(ps[bank][:, c], left[half, c], right[half, c], start=True, stop=True)
                mm.then_inc(done, 1)

            pe.wait_ge(a1_w, 16 * 10)
            project(2, 0, 0, pe_pv)
            project(0, 1, 0, pe_pq)
            project(1, 2, 0, pe_pk)
            pe.wait_ge(vT_out, 1)
            with pe.Fori(0, BP) as bp:
                with pe.Fori(0, NC) as c:
                    t = bp * NC + c
                    pe.wait_ge(win_set, bp * 2 + 2)
                    pe.wait_ge(wout_set, bp * 4 + 4)
                    w4 = lambda w, be, p: w[:, be * 1024 + p * P:be * 1024 + (p + 1) * P]
                    pe.wait_ge(silu_done, t * 2 + 2)
                    for be in range(2):
                        pe.wait_ge(win_new, t * 2 + (be + 1))
                        pe.wait_ge(woutT_out, t * 2 + 1)
                        for p in range(HP):
                            mm = pe.matmul(ps[be][:, p * P:(p + 1) * P].rearrange("r (k n) -> r k n", k=2), w4(w_in, be, p),
                                           qk.rearrange("r (k p e n) -> r k p e n", k=2, p=HP, e=2)[:, :, p, be, :],
                                           start=True, stop=True)
                        mm.then_inc(pe_z, 1)
                    pe.wait_ge(woutT_out, t * 2 + 2)
                    pe.wait_ge(vT_out, t + 1)
                    for p in range(HP):
                        for be in range(2):
                            mm = pe.matmul(ps[2][be * CH:(be + 1) * CH, p * P:(p + 1) * P],
                                           vT[:, p * P + be * CH:p * P + (be + 1) * CH], w4(w_outT, be, p),
                                           start=True, stop=True)
                    mm.then_inc(pe_a, 1)
                    turn_pairs(lambda p: vT[:, p * P:(p + 1) * P], 3, pe_vt)
                    pe.wait_ge(z_centered, t * 2 + 1)
                    project(2, 0, t * P + P, pe_pv)
                    pe.wait_ge(vtok_out, t + 1)
                    turn_pairs(lambda p: qk[:, 1024 + p * P:1024 + (p + 1) * P], 3, pe_kt)
                    pe.wait_ge(z_centered, t * 2 + 2)
                    project(0, 1, t * P + P, pe_pq)
                    pe.wait_ge(vT_out, t + 2)
                    project(1, 0, t * P + P, pe_pk)
                    pe.wait_ge(ktok_out, t + 1)
                    pe.wait_ge(pk_norm, t + 1)
                    turn_pairs(lambda p: prob[:, 1024 + p * P:1024 + (p + 1) * P], 3, pe_pt)
                    pe.wait_ge(silu_done, t * 2 + 3)
                    pe.wait_ge(pq_norm, t + 1)
                    for p in range(HP):
                        for be in range(2):
                            mm = pe.matmul(ps[1][:, p * P + be * CH:p * P + (be + 1) * CH], w4(w_out, be, p),
                                           prob[:, p * P + be * CH:p * P + (be + 1) * CH], start=True, stop=True)
                    mm.then_inc(pe_o, 1)
                    pe.wait_ge(silu_done, t * 2 + 4)
                    pe.wait_ge(ptok_out, t + 1)
                    pe.wait_ge(v_scaled, t + 1)
                    for be, bank in ((0, 0), (1, 3)):
                        gradient(p_tok, v_tok, be, bank, pe_gout)
                    pe.wait_ge(oT_out, t + 1)
                    for p in range(HP):
                        mm = pe.matmul(ps[1][:, 0:C], oT[:, p * P:(p + 1) * P], w_o[:, p * C:(p + 1) * C],
                                       start=(p == 0), stop=(p == HP - 1))
                    mm.then_inc(pe_y, 1)
                    pe.wait_ge(g_done, t + 1)
                    pe.wait_ge(k_scaled, t + 1)
                    gradient(k_tok, g_tok, 0, 2, pe_gin)
                    pe.wait_ge(y_scaled, t + 1)
                    gradient(k_tok, g_tok, 1, 1, pe_gin)
                    for be, bank in ((0, 0), (1, 3)):
                        pe.wait_ge(wout_new, t * 2 + (be + 3))
                        turn_pairs(lambda p: w4(w_out, be, p), bank, pe_wt)
            finish(pe, 9)

            pe.wait_ge(gw, 55)
            turn_and_gate(3, 1, wg1)
            pe.sem_inc(hot_used, 2)
            pe.wait_ge(rhs_ready, 3)
            pe.matmul(ps[3][:, 0:512], before_own, ohb1, start=True, stop=True)
            pe.matmul(ps[3][:, 512:1024], own_ones, ohb1, start=True, stop=True)
            pe.wait_ge(lg_out, 10)
            pe.matmul(ps[2][:, 0:512], all_ones, ohb1, start=True, stop=True).then_inc(cnt_done, 1)
            pe.wait_ge(rhs_ready, 4)

            def slot_numbers(t, u, first, last):
                pe.wait_ge(hot_made, t + (T // 8 + 1))
                for k in range(2):
                    for j in range(2):
                        mm = pe.matmul(ps[0][:, j * 512:j * 512 + 16], pos_hot[u][:, k * CAP + j * P:k * CAP + (j + 1) * P],
                                       rhs1[:, ds((t + k * T) * 16, 16)], start=first and k == 0, stop=last and k == 1)
                mm.then_inc(hot_used, 1)
                return mm

            for u in range(2):
                slot_numbers(u, u, u == 0, False)
            with pe.Fori(1, T // 2 - 1) as i:
                for u in range(2):
                    slot_numbers(i * 2 + u, u, False, False)
            for u in range(2):
                slot_numbers(T - 2 + u, u, False, u == 1)
            pe.wait_ge(hot_used, T + 2)
            pe.sem_inc(ids_mm, 1)
            finish(pe, 10)
            g0 = TILES0 // GRP
            with pe.Fori(0, E // 2) as i:
                for u in range(2):
                    e = i * 2 + u
                    pe.wait_ge(gathered[u], i * 32 + (16 * TILES0 // 2 + 32))
                    for t in range(2):
                        mm = pe.transpose(ps[0][:, t * P:(t + 1) * P], gx1[u][:, t * C:(t + 1) * C], ident[:, :])
                    mm.then_inc(x_turned, 1)
                    pe.wait_ge(f1_w, e * 32 + 32)
                    pe.wait_ge(xg_ready, e + (g0 + 1))
                    for j in range(4):
                        mm = pe.matmul(ps[1][:, j * 256:(j + 1) * 256], w1s[u][:, j * P:(j + 1) * P], xg1, start=True, stop=True)
                    mm.then_inc(h_mm, 1)
                    pe.wait_ge(hg_ready, e + (g0 + 1))
                    for t in range(2):
                        for j in range(4):
                            mm = pe.matmul(ps[3][:, t * C:(t + 1) * C], hg1[:, j * 256 + t * P:j * 256 + (t + 1) * P],
                                           w2s[u][:, j * C:(j + 1) * C], start=(j == 0), stop=(j == 3))
                    mm.then_inc(o_mm, 1)
            finish(pe, 11)
            finish(pe, 12)


INS = ["L0_attn_u", "L0_attn_dt", "L0_attn_A", "L0_attn_Bmat", "L0_attn_C", "L0_attn_D", "L0_attn_norm_w",
       "L0_ffn_wg", "L0_ffn_W1", "L0_ffn_b1", "L0_ffn_W2", "L0_ffn_b2", "L0_wmod",
       "L1_ffn_Wg", "L1_ffn_W1", "L1_ffn_b1", "L1_ffn_W2", "L1_ffn_b2", "L1_wmod"]


def layouts(inputs):
    import numpy as np

    a = {n: np.ascontiguousarray(inputs[n]) for n in INS}
    t = lambda x, *axes: np.ascontiguousarray(np.transpose(np.asarray(x), axes))
    a["L0_cT"], a["L1_cT"] = t(inputs["L0_c"], 1, 0), t(inputs["L1_c"], 1, 0)
    for n in ("Wq", "Wk", "Wv", "Wlr", "Wbeta", "Wo"):
        a[f"L1_attn_{n}T"] = t(inputs[f"L1_attn_{n}"], 1, 0)
    w_in, w_out = np.asarray(inputs["L1_attn_W_in_init"])[0], np.asarray(inputs["L1_attn_W_out_init"])[0]
    a["L0_ffn_w_redT"] = t(inputs["L0_ffn_w_red"], 1, 0)
    a["L1_b1_cols"] = t(np.asarray(inputs["L1_ffn_b1"]).reshape(E, F1 // P, P), 2, 0, 1).reshape(P, -1)
    a["W_inT"] = t(w_in, 1, 2, 0)
    a["W_out"] = t(w_out, 1, 0, 2)
    a["W_outT"] = t(w_out, 1, 2, 0)
    return a


def kernel(**inputs):
    import numpy as np
    import concourse.bacc as bacc
    from concourse.bass_utils import run_bass_kernel_spmd

    nc = bacc.Bacc("TRN2", target_bir_lowering=False, num_devices=1)
    arrays = layouts(inputs)
    A = {n: nc.dram_tensor(f"in_{n}", a.shape, mybir.dt.from_np(a.dtype), kind="ExternalInput").ap()
         for n, a in arrays.items()}
    A["out"] = nc.dram_tensor("out_x", (B, L, C), F32, kind="ExternalOutput").ap()
    program(nc, A)
    r = run_bass_kernel_spmd(nc, [{f"in_{n}": a for n, a in arrays.items()}], core_ids=[0])
    return r.results[0]["out_x"]
```

```python
from contextlib import ExitStack

import concourse.bass as bass
from concourse import mybir

ALU = mybir.AluOpType
ACT = mybir.ActivationFunctionType
AX_X = mybir.AxisListType.X
F32 = mybir.dt.float32
BF16 = mybir.dt.bfloat16
I32 = mybir.dt.int32
ds = bass.ds

P = 128
B, L, C = 8, 512, 128
BP = B // 2
CH = 64
NC = L // CH
T = BP * NC
W8 = NC * C
S = 64
G = 16
E = 8
F0 = 256
F1 = 512
CAP = 256
H, D = 16, 64
HP = H // 2
HD = H * D
TILES0 = T + E
GRP = 4
SLOTS1 = E * CAP
LN_EPS, RMS_EPS = 1e-5, 1e-6
BASE_LR, BASE_WD = 0.001, 0.9
SA, CA, GA, SB, CB, GB = range(6)


class Chain:

    def __init__(self, eng, sem):
        self.eng, self.sem, self.base, self.k = eng, sem, 0, 0

    def link(self, ins):
        ins.then_inc(self.sem, 1)
        self.k += 1
        self.eng.wait_ge(self.sem, self.base + self.k)

    def enter(self, i, per):
        self.outer, self.per = self.base + self.k, per
        self.base, self.k = self.outer + i * per, 0

    def leave(self, n):
        assert self.k == self.per, (self.k, self.per)
        self.base, self.k = self.outer + n * self.per, 0


def program(nc, A):
    ctx = ExitStack()
    with ctx:
        def sb(name, shape, dt=F32):
            return ctx.enter_context(nc.sbuf_tensor(name, shape, dt))

        def sem(name):
            return ctx.enter_context(nc.semaphore(name))

        x_sb = sb("x_sb", [P, T * C])
        mod = [sb(f"mod{l}", [P, BP * 6 * C]) for l in range(2)]
        ga_d = sb("ga_d", [P, BP * C])
        ident = sb("ident", [P, P])
        ones_f = sb("ones_f", [P, P])
        hT = sb("hT", [P, (T + 1) * P])
        w_qkv = sb("w_qkv", [P, 3 * HD])
        w_o = sb("w_o", [P, HP * C])
        w_init = sb("w_init", [P, 2 * HP * P])
        small = sb("small", [P, 512])
        masks = sb("masks", [P, 4 * P], BF16)
        before, before_own, all_ones, own_ones = (masks[:, n * P:(n + 1) * P] for n in range(4))
        iota_b = sb("iota_b", [P, CAP], BF16)
        consts = sb("consts", [P, 128])
        iota_t, first_w, iota_e, edges, tile_no = (consts[:, a:b] for a, b in ((0, 40), (40, 48), (48, 56), (56, 88), (88, 120)))
        part_no, batch_bit = consts[:, 120:121], consts[:, 121:122]
        arena = sb("arena", [P, 27648])

        def view(at, n, dt=F32):
            v = arena[:, at:at + n]
            return v if dt is F32 else v.bitcast(dt)

        sums, var, rstd = small[:, 0:T], small[:, 32:32 + T], small[:, 64:64 + T]
        ln_eps, rms_eps = small[:, 96:97], small[:, 97:98]
        dt2, a2, dts, decay = (small[:, 98 + n:99 + n] for n in range(4))
        tmp1 = small[:, 102:106]

        ps = [ctx.enter_context(nc.psum_tensor(f"ps{i}", [P, 1024], F32)) for i in range(4)]

        xc = view(0, T * C)
        sq = view(4096, T * C)
        h_st = [view(8192 + 1024 * u, W8) for u in range(2)]
        hT_st = [view(10240 + 1024 * u, W8) for u in range(2)]
        hsq = view(12288, W8)
        rms = view(13312, L)
        us = view(13824, L)
        xs = view(14336, L)
        yg = view(14848, W8)
        a_bc = view(15872, L)
        nb = view(16384, S)
        bmat = view(16448, S)
        normw = view(16512, 1)
        cmat = view(16576, C)
        d_bc = view(16704, C)
        ct = view(17000, 16)
        cth = view(17016, 16)
        st = [view(17100 + 512 * l, 512) for l in range(2)]
        wm = [view(18200 + 768 * l, 768) for l in range(2)]

        w1a, w2a, b1a, b2a = view(12288, E * F0), view(14336, E * F0), view(16384, E * F0), view(18432, E * C)
        logits, shifted, e_exp, pick, onehot, cum, rank, scr = (view(19456 + 256 * n, T * E) for n in range(8))
        onehot_b = view(21504, T * E // 2, BF16)
        n_cmp = view(21632, 320)
        tile_hot = view(21952, T * 40)
        w_gate, wg_n, wg_s, wg_t, wred_t = view(23232, E), view(23240, 16), view(23256, 16), view(23272, E), view(23280, C)
        r_hot = view(0, T * P // 2, BF16)
        t_rhs = view(2048, T * 80 // 2, BF16)
        gx = [view(4096 + 512 * u, GRP * C) for u in range(2)]
        xg = view(5120, GRP * C)
        hb = view(5632, GRP * F0)
        hgT = view(6656, GRP * F0)
        o_st = [view(7680 + 512 * u, GRP * C) for u in range(2)]
        back = [view(8704 + 1024 * u, W8) for u in range(4)]
        route = sb("route", [P, 1024])
        mx, m2, slot_f, tile_f, row_f, score, e_sum, n_tiles, t_end, t_start = (route[:, 32 * n:32 * n + 32] for n in range(10))
        wk, pos, e_of, keep = (route[:, 320 + 64 * n:384 + 64 * n] for n in range(4))
        id_f = route[:, 576:656]
        ids_i = route[:, 656:696].bitcast(I32)
        t_exp_i = route[:, 696:736].bitcast(I32)
        slot_i = route[:, 736:800].bitcast(I32)
        tile_i = route[:, 800:832].bitcast(I32)
        idx_st = [route[:, 832 + n:833 + n].bitcast(I32) for n in range(32)]
        t_exp_f = route[:, 864:904]
        w1s = [view(12288 + 512 * u, F1) for u in range(2)]
        w2s = [view(13312 + 512 * u, F1) for u in range(2)]
        b1t, b2b = view(14336, E * 4), view(14400, E * C)
        wg1 = view(15424, E)
        lg1, sh1, pr1 = view(15488, 256), view(15744, 256), view(16000, 256)
        oh1 = view(16256, 512)
        ohb1 = view(16768, 256, BF16)
        run1 = view(17024, 512)
        rk1, scr1 = view(17536, 512), view(18048, 512)
        own_t, both_t, off1 = view(18560, 64), view(18624, 64), view(18688, 64)
        rhs1 = view(18752, 512, BF16)
        cnt1 = view(19264, 16)
        pos_hot = [view(19328 + 256 * u, 256, BF16) for u in range(2)]
        gx1 = [view(4096 + 256 * u, 2 * C) for u in range(2)]
        xg1 = view(5120, 2 * C)
        hg1 = [view(5632 + 1024 * u, 4 * 2 * C) for u in range(2)]
        back1 = view(0, 2 * BP * W8)
        o1_st = [view(7680 + 256 * u, 2 * C) for u in range(2)]

        h_dram = [nc.dram_tensor(f"h_rows{f}", (B * L, C), F32, kind="Internal").ap() for f in range(2)]
        o_dram = nc.dram_tensor("o_rows", (TILES0 * P, C), F32, kind="Internal").ap()
        y_dram = nc.dram_tensor("y_rows", (P + 2 * B * L, C), F32, kind="Internal").ap()

        sel = view(12288, 2048)
        w_lb = view(14336, S)
        tg = [view(512 * u, 512) for u in range(2)]
        rate_sums = view(1024, 64)
        rate_spread = view(1536, 64 * CH)
        qk = view(0, 2048)
        vT = view(2048, 1024)
        k_tok, v_tok = view(3072, 1024), view(4096, 1024)
        zs = view(5120, 2048)
        prob = view(7168, 2048)
        p_tok, pa = view(9216, 1024), v_tok
        g_pad, v_pad = view(10240, 2048), sb("v_pad", [P, 2048])[:, :]
        oT = view(12288, 1024)
        th = [view(13312 + 1024 * u, 1024) for u in range(2)]
        w_dec = view(15360, 4096)
        w_in, w_out, w_outT = view(19456, 2048), view(21504, 2048), view(23552, 2048)
        wd = view(25600, 1024)
        lr = view(26624, 1024)
        y_gated = small[:, 128:256]
        z_max, z_sum, z_rec = small[:, 256:288], small[:, 288:320], small[:, 320:352]
        s_sum = small[:, 352:368]

        phase_end, passed = sem("phase_end"), sem("passed")
        x_in, c_in, wm_in, a0_in = sem("x_in"), sem("c_in"), sem("wm_in"), sem("a0_in")
        dve_step2 = sem("dve_step2")
        consts_made, dve_step, act_step, pool_step = sem("consts_made"), sem("dve_step"), sem("act_step"), sem("pool_step")
        cond_tanh, cond_spread = sem("cond_tanh"), sem("cond_spread")
        mod_mm, mod_out = sem("mod_mm"), sem("mod_out")
        ln_centered, ln_squared, ln_var, ln_std, ln_scaled = (sem("ln_" + n) for n in ("centered", "squared", "var", "std", "scaled"))
        h_ready, h_turned, hT_ready, hT_used = (sem(n) for n in ("h_ready", "h_turned", "hT_ready", "hT_used"))
        a0_exp, a0_par, a0_sq, a0_up, a0_rms, a0_scan, a0_y, a0_gated, a0_yg_used = (
            sem("a0_" + n) for n in ("exp", "par", "sq", "up", "rms", "scan", "y", "gated", "yg_used"))
        a1_w, sel_made, wlb_in = sem("a1_w"), sem("sel_made"), sem("wlb_in")
        rt_mm, rt_tanh, rt_sum, rt_spread, rt_wd, rt_lr, rt_cred = (sem("rt_" + n) for n in ("mm", "tanh", "sum", "spread", "wd", "lr", "cred"))
        pe_z, pe_a, pe_vt, pe_kt, pe_pv, pe_pq, pe_pk, pe_pt, pe_o, pe_gout, pe_y, pe_gin, pe_wt = (
            sem("pe_" + n) for n in ("z", "a", "vt", "kt", "pv", "pq", "pk", "pt", "o", "gout", "y", "gin", "wt"))
        win_set, wout_set = sem("win_set"), sem("wout_set")
        z_centered, z_summed, pk_norm, silu_done, g_done, wout_new, y_scaled, win_new = (
            sem(n) for n in ("z_centered", "z_summed", "pk_norm", "silu_done", "g_done", "wout_new", "y_scaled", "win_new"))
        z_exp, vT_out, tanh_out, vtok_out, ktok_out, ptok_out, oT_out, woutT_out = (
            sem(n) for n in ("z_exp", "vT_out", "tanh_out", "vtok_out", "ktok_out", "ptok_out", "oT_out", "woutT_out"))
        pq_norm, v_scaled, k_scaled, dec_done, x_added = (sem(n) for n in ("pq_norm", "v_scaled", "k_scaled", "dec_done", "x_added"))
        h_stored = [sem(f"h_stored{u}") for u in range(2)]
        lg_mm, lg_out, ex_done, oh_done, cnt_done, rhs_ready, ids_mm, ids_ready, gw = (
            sem(n) for n in ("lg_mm", "lg_out", "ex_done", "oh_done", "cnt_done", "rhs_ready", "ids_mm", "ids_ready", "gw"))
        f0_w, f1_b, pool_step2 = sem("f0_w"), sem("f1_b"), sem("pool_step2")
        f1_w = [sem(f"f1_w{u}") for u in range(2)]
        y_zeroed, y_idx, y_scattered, o1_free, y_sum, x_final = (
            sem(n) for n in ("y_zeroed", "y_idx", "y_scattered", "o1_free", "y_sum", "x_final"))
        y_in = [sem(f"y_in{bp}") for bp in range(BP)]
        gathered = [sem(f"gathered{u}") for u in range(2)]
        x_turned, xg_ready, h_mm, hb_ready, hg_ready, hg_turned, hgT_ready, o_mm, o_ready = (
            sem("ex_" + n) for n in ("x_turned", "xg_ready", "h_mm", "hb_ready", "hg_ready", "hg_turned", "hgT_ready", "o_mm", "o_ready"))
        o_stored = [sem(f"o_stored{u}") for u in range(2)]
        back_in = [sem(f"back_in{u}") for u in range(2)]
        back_used, hot_made, hot_used = sem("back_used"), sem("hot_made"), sem("hot_used")
        out_sem = sem("out_sem")

        block = ctx.enter_context(nc.Block())

        def tiles(ap, i, n=NC):
            return ap[:, ds(i * (n * C), n * C)].rearrange("p (t c) -> p t c", c=C)

        def mod_of(l, bp, j):
            return mod[l][:, ds(bp * (6 * C) + j * C, C)]

        def over_tiles(ap, n=NC):
            return ap.unsqueeze(1).to_broadcast([P, n, C])

        def finish(eng, n):
            eng.drain().then_inc(phase_end, 1)
            eng.wait_ge(phase_end, 5 * n)

        def apart(eng):
            eng.sem_inc(passed, 1)

        @block.sync
        def _(sp):
            for b in range(B):
                bp, be = divmod(b, 2)
                sp.dma_start(x_sb[be * CH:(be + 1) * CH, bp * W8:(bp + 1) * W8].rearrange("p (t c) -> p t c", c=C),
                             A["L0_attn_u"][b].rearrange("(t p) c -> p t c", p=CH)).then_inc(x_in, 16)
            for l in range(2):
                sp.dma_start(ct[:, 8 * l:8 * l + 8], A[f"L{l}_cT"]).then_inc(c_in, 16)
                sp.dma_start(wm[l], A[f"L{l}_wmod"]).then_inc(wm_in, 16)
            col = lambda v: v.rearrange("(a b) -> a b", b=1)
            row = lambda v: v.rearrange("(a b) -> a b", a=1)
            for be in range(2):
                half = slice(be * S, be * S + S)
                sp.dma_start(dt2[half], col(A["L0_attn_dt"])).then_inc(a0_in, 16)
                sp.dma_start(a2[half], col(A["L0_attn_A"])).then_inc(a0_in, 16)
                sp.dma_start(cmat[half], A["L0_attn_C"]).then_inc(a0_in, 16)
            sp.dma_start(bmat, A["L0_attn_Bmat"]).then_inc(a0_in, 16)
            sp.dma_start(normw, col(A["L0_attn_norm_w"])).then_inc(a0_in, 16)
            sp.dma_start(d_bc, row(A["L0_attn_D"]).to_broadcast([P, C])).then_inc(a0_in, 16)
            for n, w in enumerate(("Wq", "Wk", "Wv")):
                sp.dma_start(w_qkv[:, n * HD:(n + 1) * HD], A[f"L1_attn_{w}T"]).then_inc(a1_w, 16)
            sp.dma_start(w_o[:, :].rearrange("r (p c) -> r p c", c=C),
                         A["L1_attn_WoT"].rearrange("(p r) c -> r p c", r=P)).then_inc(a1_w, 16)
            sp.wait_ge(consts_made, 1)
            w3 = w_init[:, :].rearrange("r (k p c) -> r k p c", k=2, c=P)
            for k, n in enumerate(("W_inT", "W_out")):
                for h in range(2):
                    half = slice(h * D, h * D + D)
                    sp.dma_start(w3[half, k, :, half], A[n].rearrange("(p h) r c -> h r p c", h=2)[h]).then_inc(a1_w, 16)
            finish(sp, 1)
            finish(sp, 2)

            def store_h(f, k):
                with sp.Fori(0, 2) as i:
                    for u in range(2):
                        bp = i * 2 + u
                        sp.wait_ge(h_ready, bp + (4 * k + 1))
                        sp.dma_start(h_dram[f][ds(bp * (NC * P), NC * P), :].rearrange("(t p) c -> p t c", p=P),
                                     h_st[u].rearrange("p (t c) -> p t c", c=C)).then_inc(h_stored[u], 16)

            sp.dma_start(w1a.rearrange("c (e f) -> c e f", e=E), A["L0_ffn_W1"].rearrange("e c f -> c e f")).then_inc(f0_w, 16)
            sp.dma_start(w2a.rearrange("r (e j c) -> r e j c", e=E, j=2),
                         A["L0_ffn_W2"].rearrange("e (j r) c -> r e j c", r=P)).then_inc(f0_w, 16)
            sp.dma_start(b1a, A["L0_ffn_b1"].rearrange("(a e) f -> a (e f)", a=1).to_broadcast([P, E * F0])).then_inc(f0_w, 16)
            sp.dma_start(b2a, A["L0_ffn_b2"].rearrange("(a e) f -> a (e f)", a=1).to_broadcast([P, E * C])).then_inc(f0_w, 16)
            sp.dma_start(wg_s[0:E, :], A["L0_ffn_wg"]).then_inc(gw, 16)
            sp.dma_start(wred_t[0:16, :], A["L0_ffn_w_redT"]).then_inc(gw, 16)
            store_h(0, 1)
            finish(sp, 3)
            finish(sp, 4)
            with sp.Fori(0, TILES0 // GRP // 2) as i:
                for u in range(2):
                    g = i * 2 + u
                    sp.wait_ge(o_ready, g * GRP + GRP)
                    sp.dma_start(o_dram[ds(g * (GRP * P), GRP * P), :].rearrange("(t p) c -> p t c", p=P),
                                 o_st[u].rearrange("p (t c) -> p t c", c=C)).then_inc(o_stored[u], 16)
            for u in range(2):
                sp.wait_ge(o_stored[u], 16 * (TILES0 // GRP // 2) + 16)
            finish(sp, 5)
            finish(sp, 6)
            sp.dma_start(w_lb[:, 0:32], A["L1_attn_WlrT"]).then_inc(wlb_in, 16)
            sp.dma_start(w_lb[:, 32:64], A["L1_attn_WbetaT"]).then_inc(wlb_in, 16)
            finish(sp, 7)
            finish(sp, 8)
            for n in range(2 * BP):
                r0 = P + n * NC * P
                sp.dma_start(y_dram[r0:r0 + NC * P, :].rearrange("(t p) c -> p t c", p=P),
                             hT[:, T * P:(T + 1) * P].unsqueeze(1).to_broadcast([P, NC, C])).then_inc(y_zeroed, 16)
            finish(sp, 9)

            sp.dma_start(wg1, A["L1_ffn_Wg"]).then_inc(gw, 16)
            sp.dma_start(b1t, A["L1_b1_cols"]).then_inc(f1_b, 16)
            sp.dma_start(b2b, A["L1_ffn_b2"].rearrange("(a e) f -> a (e f)", a=1).to_broadcast([P, E * C])).then_inc(f1_b, 16)
            def expert_weights(e, u):
                sp.dma_start(w1s[u], A["L1_ffn_W1"].rearrange("e c f -> (e c) f")[ds(e * C, C), :]).then_inc(f1_w[u], 16)
                sp.dma_start(w2s[u].rearrange("r (j c) -> r j c", j=4),
                             A["L1_ffn_W2"].rearrange("e f c -> (e f) c")[ds(e * F1, F1), :].rearrange("(j r) c -> r j c", r=P)
                             ).then_inc(f1_w[u], 16)

            store_h(1, 3)
            for u in range(2):
                expert_weights(u, u)
            finish(sp, 10)
            with sp.Fori(1, E // 2) as i:
                for u in range(2):
                    e = i * 2 + u
                    sp.wait_ge(o_mm, e + (TILES0 - 1))
                    expert_weights(e, u)
            finish(sp, 11)
            for bp in range(BP):
                for k in range(2):
                    r0 = P + k * B * L + bp * NC * P
                    sp.dma_start(back1[:, (2 * bp + k) * W8:(2 * bp + k + 1) * W8].rearrange("p (t c) -> p t c", c=C),
                                 y_dram[r0:r0 + NC * P, :].rearrange("(t p) c -> p t c", p=P)).then_inc(y_in[bp], 16)
            for b in range(B):
                bp, be = divmod(b, 2)
                sp.wait_ge(x_final, bp + 1)
                sp.dma_start(A["out"][b].rearrange("(t p) c -> p t c", p=CH),
                             x_sb[be * CH:(be + 1) * CH, bp * W8:(bp + 1) * W8].rearrange("p (t c) -> p t c", c=C)
                             ).then_inc(out_sem, 16)
            finish(sp, 12)
            sp.wait_ge(out_sem, 16 * B)

        @block.gpsimd
        def _(pool):
            chain = Chain(pool, pool_step)
            chain.link(pool.memset(ident[:, :], 0.0))
            chain.link(pool.memset(ones_f[:, :], 1.0))
            chain.link(pool.memset(ln_eps, LN_EPS))
            chain.link(pool.memset(rms_eps, RMS_EPS))
            chain.link(pool.memset(w_init[:, :], 0.0))
            chain.link(pool.memset(hT[:, T * P:(T + 1) * P], 0.0))
            chain.link(pool.affine_select(out=ident[:, :], in_=ident[:, :], compare_op=ALU.not_equal, fill=1.0, base=0,
                               pattern=[[-1, P]], channel_multiplier=1))
            chain.link(pool.memset(masks[:, :], 1.0))
            chain.link(pool.memset(part_no, 0.0))
            chain.link(pool.affine_select(out=masks[:, 0:2 * P].rearrange("q (k p) -> q k p", k=2), in_=masks[:, 0:2 * P].rearrange("q (k p) -> q k p", k=2),
                               compare_op=ALU.is_gt, fill=0.0, base=0, pattern=[[0, 2], [1, P]], channel_multiplier=-1))
            chain.link(pool.memset(before_own[0:CH, CH:P], 0.0))
            chain.link(pool.memset(own_ones[0:CH, CH:P], 0.0))
            chain.link(pool.memset(own_ones[CH:P, 0:CH], 0.0))
            imprecise = dict(allow_small_or_imprecise_dtypes=True)
            chain.link(pool.iota(iota_b[:, :], pattern=[[1, CAP]], base=0, channel_multiplier=0, **imprecise))
            chain.link(pool.iota(iota_t, pattern=[[1, 40]], base=0, channel_multiplier=0, **imprecise))
            chain.link(pool.iota(first_w, pattern=[[-1, E]], base=E, channel_multiplier=0, **imprecise))
            chain.link(pool.iota(iota_e, pattern=[[1, E]], base=0, channel_multiplier=0, **imprecise))
            chain.link(pool.iota(edges, pattern=[[P, T]], base=0, channel_multiplier=0, **imprecise))
            chain.link(pool.iota(tile_no, pattern=[[1, T]], base=0, channel_multiplier=0, **imprecise))
            chain.link(pool.iota(part_no, pattern=[[0, 1]], base=0, channel_multiplier=1, **imprecise))
            chain.link(pool.memset(batch_bit[0:CH], 0.0))
            chain.link(pool.memset(batch_bit[CH:P], 1.0))
            pool.sem_inc(consts_made, 1)
            for u in range(2):
                pool.sem_inc(h_stored[u], 16)
                pool.sem_inc(o_stored[u], 16)
            pool.sem_inc(h_turned, 2)
            finish(pool, 1)

            def add_shift(l, k, j, f=None):
                with pool.Fori(0, 2) as i:
                    for u in range(2):
                        bp = i * 2 + u
                        pool.wait_ge(ln_scaled, bp + (4 * k + 1))
                        pool.wait_ge(h_turned, bp + (4 * k + 1))
                        if f is not None:
                            pool.wait_ge(h_stored[u], i * 16 + (32 * f + 16))
                        pool.tensor_tensor(h_st[u].rearrange("p (t c) -> p t c", c=C), tiles(xc, bp),
                                           over_tiles(mod_of(l, bp, j)), ALU.add).then_inc(h_ready, 1)
                        yield bp

            for bp in add_shift(0, 0, SA):
                pass
            with pool.Fori(0, BP) as bp:
                pool.wait_ge(a0_gated, bp + 1)
                y3 = yg.rearrange("p (t c) -> p t c", c=C)
                chain.enter(bp, 1)
                chain.link(pool.tensor_tensor(y3, y3, over_tiles(ga_d[:, ds(bp * C, C)]), ALU.add))
                pool.tensor_tensor(tiles(x_sb, bp), tiles(x_sb, bp), y3, ALU.add).then_inc(a0_yg_used, 1)
            chain.leave(BP)
            finish(pool, 2)

            def gather_back(base):
                with pool.Fori(0, 2) as i:
                    for u in range(2):
                        bp = i * 2 + u
                        pool.wait_ge(back_used, bp + 1)
                        for t in range(NC):
                            pool.tensor_copy(idx_st[8 * u + t], slot_i[:, ds(bp * NC + t, 1)]).then_inc(pool_step2, 1)
                        pool.wait_ge(pool_step2, bp * NC + (base + NC))
                        apart(pool)
                        for t in range(NC):
                            pool.indirect_dma_start(
                                back[u][:, t * C:(t + 1) * C], None, o_dram[:, :],
                                bass.IndirectOffsetOnAxis(ap=idx_st[8 * u + t], axis=0),
                                bounds_check=TILES0 * P - 1, oob_is_err=False).then_inc(back_in[u], 16)

            for bp in add_shift(0, 1, SB, f=0):
                pass
            finish(pool, 3)
            finish(pool, 4)
            for u in range(2):
                pool.wait_ge(h_stored[u], 48)
            n0 = 0
            with pool.Fori(0, TILES0 // GRP // 2) as i:
                for u in range(2):
                    g = i * 2 + u
                    pool.wait_ge(x_turned, g + 1)
                    for t in range(GRP):
                        pool.tensor_copy(idx_st[GRP * u + t], ids_i[:, ds(g * GRP + t, 1)]).then_inc(pool_step2, 1)
                    pool.wait_ge(pool_step2, g * GRP + (n0 + GRP))
                    apart(pool)
                    for t in range(GRP):
                        pool.indirect_dma_start(gx[u][:, t * C:(t + 1) * C], None, h_dram[0][:, :],
                                                bass.IndirectOffsetOnAxis(ap=idx_st[GRP * u + t], axis=0),
                                                bounds_check=B * L - 1, oob_is_err=False).then_inc(gathered[u], 16)
            n0 += TILES0
            finish(pool, 5)
            gather_back(n0)
            n0 += T
            finish(pool, 6)

            chain.link(pool.memset(sel[0:64, :], 0.0))
            pool.affine_select(out=sel[0:64, :].rearrange("k (i p h m) -> k i p h m", i=2, p=HP, h=2),
                               in_=sel[0:64, :].rearrange("k (i p h m) -> k i p h m", i=2, p=HP, h=2),
                               compare_op=ALU.not_equal, fill=1.0, base=-2 * H,
                               pattern=[[-H, 2], [-2, HP], [-1, 2], [0, D]], channel_multiplier=1).then_inc(sel_made, 1)
            for bp in add_shift(1, 2, SA):
                pass
            finish(pool, 7)
            pool.memset(g_pad, 0.0)
            pool.memset(v_pad, 0.0)
            finish(pool, 8)

            pool.sem_inc(x_added, 1)
            with pool.Fori(0, BP) as bp:
                with pool.Fori(0, NC) as c:
                    t = bp * NC + c
                    pool.wait_ge(win_set, bp * 2 + 2)
                    pool.wait_ge(wout_set, bp * 2 + 2)
                    for be in range(2):
                        pool.wait_ge(win_new, t * 2 + (be + 1))
                        pool.wait_ge(wout_new, t * 2 + (be + 1))
                        for k, w in enumerate((w_in, w_out)):
                            last = pool.tensor_tensor(
                                w_dec[:, (2 * k + be) * 1024:(2 * k + be + 1) * 1024].rearrange("r (p c) -> r p c", c=P),
                                w[:, be * 1024:(be + 1) * 1024].rearrange("r (p c) -> r p c", c=P),
                                wd[:, ds(t * 32 + (16 * be + 8 * k), HP)].unsqueeze(2).to_broadcast([P, HP, P]), ALU.mult)
                        last.then_inc(dec_done, 1)
                    pool.wait_ge(vtok_out, t + 1)
                    chain.enter(t, 1)
                    for be in range(2):
                        half = slice(be * CH, be * CH + CH)
                        last = pool.tensor_tensor(v_pad[half, :].rearrange("r (h e d) -> r h e d", e=2, d=D)[:, :, be, :],
                                                  v_tok[half, :].rearrange("r (h d) -> r h d", d=D),
                                                  lr[half, ds(t * 32 + H, H)].unsqueeze(2).to_broadcast([CH, H, D]), ALU.mult)
                        if be == 0:
                            chain.link(last)
                    last.then_inc(v_scaled, 1)
                    pool.wait_ge(v_scaled, t + 1)
                    chain.base, chain.k = chain.outer, 0
                    pool.wait_ge(z_summed, t * 2 + 2)
                    z4 = zs.rearrange("r (e p k n) -> r e p k n", e=2, p=HP, k=2)
                    r4 = z_rec.rearrange("r (e p k) -> r e p k", e=2, p=HP)
                    pool.tensor_tensor(prob[:, 0:1024].rearrange("r (p e n) -> r e p n", e=2, n=CH), z4[:, :, :, 0, :],
                                       r4[:, :, :, 0].unsqueeze(3).to_broadcast([P, 2, HP, CH]), ALU.mult).then_inc(pq_norm, 1)
                    pool.wait_ge(ktok_out, t + 1)
                    b3 = k_tok.rearrange("r (h d) -> r h d", d=D)
                    pool.tensor_tensor(b3, b3, lr[:, ds(t * 32, H)].unsqueeze(2).to_broadcast([P, H, D]),
                                       ALU.mult).then_inc(k_scaled, 1)
                    pool.wait_ge(y_scaled, t + 2)
                    pool.tensor_tensor(x_sb[:, ds(t * C, C)], x_sb[:, ds(t * C, C)], y_gated, ALU.add).then_inc(x_added, 1)
            chain.base = chain.outer + T
            finish(pool, 9)

            for bp in add_shift(1, 3, SB, f=1):
                pass
            finish(pool, 10)
            for u in range(2):
                pool.wait_ge(h_stored[u], 80)
            pool.wait_ge(ids_ready, 2)
            def fetch_rows(e, u):
                pool.wait_ge(x_turned, e + (TILES0 // GRP + 1))
                for t in range(2):
                    pool.tensor_copy(idx_st[2 * u + t], ids_i[:, ds(e + E * t, 1)]).then_inc(pool_step2, 1)
                pool.wait_ge(pool_step2, e * 2 + (n0 + 2))
                apart(pool)
                for t in range(2):
                    pool.indirect_dma_start(gx1[u][:, t * C:(t + 1) * C], None, h_dram[1][:, :],
                                            bass.IndirectOffsetOnAxis(ap=idx_st[2 * u + t], axis=0),
                                            bounds_check=B * L - 1, oob_is_err=False).then_inc(gathered[u], 16)

            def scatter_rows(e, u, first=False):
                for t in range(2):
                    pool.tensor_copy(idx_st[4 + 2 * u + t], ids_i[:, ds(e + (2 * E + E * t), 1)]).then_inc(y_idx, 1)
                pool.wait_ge(y_idx, e * 2 + 2)
                pool.wait_ge(o_ready, e + (TILES0 + 1))
                apart(pool)
                for t in range(2):
                    if not (first and t == 0):
                        pool.wait_ge(y_scattered, e * 32 + 16 * t)
                        if t == 0:
                            pool.sem_inc(o1_free, 1)
                        else:
                            apart(pool)
                    pool.indirect_dma_start(y_dram[:, :], bass.IndirectOffsetOnAxis(ap=idx_st[4 + 2 * u + t], axis=0),
                                            o1_st[u][:, t * C:(t + 1) * C], None,
                                            bounds_check=P + 2 * B * L - 1, oob_is_err=False).then_inc(y_scattered, 16)

            for u in range(2):
                fetch_rows(u, u)
            pool.sem_inc(o1_free, 2)
            pool.wait_ge(y_zeroed, 32 * BP)
            fetch_rows(2, 0)
            scatter_rows(0, 0, first=True)
            with pool.Fori(0, E // 2 - 2) as i:
                for e, u in ((i * 2 + 1, 1), (i * 2 + 2, 0)):
                    fetch_rows(e + 2, u)
                    scatter_rows(e, u)
            fetch_rows(E - 1, 1)
            for e in range(E - 3, E):
                scatter_rows(e, e % 2)
            n0 += 2 * E
            pool.wait_ge(y_scattered, 32 * E)
            finish(pool, 11)
            with pool.Fori(0, BP) as bp:
                pool.wait_ge(y_sum, bp + 1)
                pool.tensor_tensor(tiles(x_sb, bp), tiles(x_sb, bp), tiles(back1, bp * 2), ALU.add).then_inc(x_final, 1)
            finish(pool, 12)

        @block.scalar
        def _(act):
            act.wait_ge(c_in, 32)
            act.activation(cth, ct, ACT.Tanh, scale=0.5).then_inc(cond_tanh, 1)
            for l in range(2):
                for bp in range(BP):
                    n = BP * l + bp
                    act.wait_ge(mod_mm, n + 1)
                    act.activation(mod[l][:, bp * 6 * C:(bp + 1) * 6 * C], ps[n % 4][:, 0:6 * C],
                                   ACT.Copy).then_inc(mod_out, 1)
            act.wait_ge(a0_in, 16 * 9)
            act.activation(tmp1[:, 0:1], dt2, ACT.Exp, scale=-1.0).then_inc(a0_exp, 1)
            act.wait_ge(a0_par, 1)
            act.activation(decay, tmp1[:, 3:4], ACT.Exp, scale=-1.0).then_inc(a0_exp, 1)
            finish(act, 1)

            def squares_and_std(k):
                with act.Fori(0, BP) as i:
                    act.wait_ge(ln_centered, i + (4 * k + 1))
                    act.activation(tiles(sq, i), tiles(xc, i), ACT.Square).then_inc(ln_squared, 1)
                act.wait_ge(ln_var, 4 * (k + 1))
                act.activation(rstd, var, ACT.Sqrt, bias=ln_eps, scale=1.0 / C).then_inc(ln_std, 1)

            squares_and_std(0)
            with act.Fori(0, 2) as i:
                for u in range(2):
                    bp = i * 2 + u
                    act.wait_ge(h_turned, bp + 3)
                    act.activation(hT_st[u].rearrange("c (e t n) -> c t e n", e=2, n=CH),
                                   ps[u][:, :].rearrange("c (t e n) -> c t e n", e=2, n=CH), ACT.Copy
                                   ).then_inc(hT_ready, 1)
                    act.wait_ge(hT_ready, bp + 1)
                    if u == 0:
                        pass
                    act.activation(hsq, hT_st[u], ACT.Square).then_inc(a0_sq, 1)
                    act.wait_ge(a0_up, bp + 1)
                    act.activation(rms, ps[2][:, 0:L], ACT.Sqrt, bias=rms_eps, scale=1.0 / C).then_inc(a0_rms, 1)
            finish(act, 2)

            def out_of_turn(k):
                with act.Fori(0, 2) as i:
                    for u in range(2):
                        bp = i * 2 + u
                        act.wait_ge(h_turned, bp + (4 * k + 3))
                        act.activation(hT_st[u], ps[u][:, :], ACT.Copy).then_inc(hT_ready, 1)

            act.wait_ge(gw, 33)
            act.activation(wg_n[0:E, 0:1], wg_t[0:E, 0:1], ACT.Sqrt).then_inc(gw, 1)
            squares_and_std(1)
            out_of_turn(1)
            finish(act, 3)
            act.wait_ge(oh_done, 1)
            act.activation(e_exp, shifted, ACT.Exp).then_inc(ex_done, 1)
            finish(act, 4)
            with act.Fori(0, TILES0 // GRP) as g:
                act.wait_ge(hb_ready, g * GRP + GRP)
                act.activation(hb, hb, ACT.Gelu).then_inc(hg_ready, 1)
            finish(act, 5)
            finish(act, 6)

            squares_and_std(2)
            with act.Fori(0, 2) as i:
                for u in range(2):
                    bp = i * 2 + u
                    act.wait_ge(h_turned, bp + (2 * BP + 3))
                    act.activation(hT[:, ds(bp * W8, W8)], ps[u][:, :], ACT.Copy).then_inc(hT_ready, 1)
            finish(act, 7)
            with act.Fori(0, 4) as i:
                for u in range(2):
                    n = i * 2 + u
                    act.wait_ge(rt_mm, n + 1)
                    act.wait_ge(rt_sum, n + 1)
                    act.activation(tg[u][0:64, :], ps[u][0:64, 0:512], ACT.Tanh, scale=0.5).then_inc(rt_tanh, 1)
            finish(act, 8)

            act.wait_ge(pe_pv, 1)
            act.activation(vT, ps[0][:, :], ACT.Copy).then_inc(vT_out, 1)
            act.wait_ge(pe_pq, 1)
            act.activation(th[0], ps[1][:, :], ACT.Tanh, scale=0.5).then_inc(tanh_out, 1)
            act.wait_ge(pe_pk, 1)
            act.activation(th[1], ps[2][:, :], ACT.Tanh, scale=0.5).then_inc(tanh_out, 1)
            with act.Fori(0, BP) as bp:
                act.wait_ge(win_new, bp * (2 * NC) + 2)
                act.activation(w_in[:, 0:1024], w_init[:, 0:1024], ACT.Copy).then_inc(win_set, 1)
                act.wait_ge(wout_new, bp * (2 * NC) + 2)
                for be in range(2):
                    act.activation(w_out[:, be * 1024:(be + 1) * 1024], w_init[:, 1024:2048], ACT.Copy).then_inc(wout_set, 1)
                with act.Fori(0, NC) as c:
                    t = bp * NC + c

                    def exponentials(be):
                        z = zs[:, be * 1024:(be + 1) * 1024]
                        act.wait_ge(z_centered, t * 2 + (be + 1))
                        act.activation(z, z, ACT.Exp, scale=0.5).then_inc(z_exp, 1)

                    exponentials(0)
                    for be, bank in ((0, 3), (1, 2)):
                        act.wait_ge(pe_wt, t * 2 + (be + 1))
                        act.activation(w_outT[:, be * 1024:(be + 1) * 1024], ps[bank][:, :], ACT.Copy).then_inc(woutT_out, 1)
                    exponentials(1)
                    act.wait_ge(pe_vt, t + 1)
                    act.activation(v_tok, ps[3][:, :], ACT.Copy).then_inc(vtok_out, 1)
                    act.wait_ge(pe_pq, t + 2)
                    act.activation(th[0], ps[1][:, :], ACT.Tanh, scale=0.5).then_inc(tanh_out, 1)
                    act.wait_ge(pe_pv, t + 2)
                    act.wait_ge(pe_a, t + 1)
                    act.activation(vT, ps[0][:, :], ACT.Copy).then_inc(vT_out, 1)
                    act.wait_ge(pe_pt, t + 1)
                    act.activation(p_tok, ps[3][:, :], ACT.Copy).then_inc(ptok_out, 1)
                    act.wait_ge(pe_pk, t + 2)
                    act.activation(th[1], ps[0][:, :], ACT.Tanh, scale=0.5).then_inc(tanh_out, 1)
                    act.wait_ge(pe_kt, t + 1)
                    act.activation(k_tok, ps[3][:, :], ACT.Copy).then_inc(ktok_out, 1)
                    act.wait_ge(pe_o, t + 1)
                    act.activation(oT, ps[1][:, :], ACT.Copy).then_inc(oT_out, 1)
            finish(act, 9)

            squares_and_std(3)
            out_of_turn(3)
            act.wait_ge(oh_done, 2)
            act.activation(pr1, sh1, ACT.Exp).then_inc(ex_done, 1)
            finish(act, 10)
            g0 = TILES0 // GRP
            act.wait_ge(f1_b, 32)
            with act.Fori(0, E // 2) as i:
                for u in range(2):
                    e = i * 2 + u
                    act.wait_ge(h_mm, e + (TILES0 + 1))
                    for j in range(4):
                        last = act.activation(hg1[u][:, j * 256:(j + 1) * 256], ps[1 + u][:, j * 256:(j + 1) * 256],
                                              ACT.Gelu_apprx_tanh, bias=b1t[:, ds(e * 4 + j, 1)])
                    last.then_inc(hg_ready, 1)
            finish(act, 11)
            finish(act, 12)

        @block.vector
        def _(dve):
            chain = Chain(dve, dve_step)
            dve.wait_ge(cond_tanh, 1)
            chain.link(dve.scalar_tensor_tensor(cth, cth, 1.0, ct, ALU.add, ALU.mult))
            for l in range(2):
                dve.tensor_scalar(st[l].rearrange("k (b n) -> k b n", n=CH),
                                  cth[:, 8 * l:8 * l + 8].unsqueeze(2).to_broadcast([P, B, CH]), 0.5, None, ALU.mult
                                  ).then_inc(cond_spread, 1)
            dve.wait_ge(a0_exp, 1)
            chain.link(dve.tensor_scalar(tmp1[:, 1:2], tmp1[:, 0:1], 1.0, None, ALU.add))
            chain.link(dve.reciprocal(dts, tmp1[:, 1:2]))
            chain.link(dve.scalar_tensor_tensor(tmp1[:, 2:3], a2, -1.0, a2, ALU.mult, ALU.max))
            dve.tensor_tensor(tmp1[:, 3:4], tmp1[:, 2:3], dts, ALU.mult).then_inc(a0_par, 1)
            chain.link(dve.tensor_scalar(nb, bmat, normw, None, ALU.mult))
            dve.wait_ge(a0_exp, 2)
            chain.link(dve.tensor_copy(a_bc, decay.to_broadcast([P, L])))
            for l in range(2):
                dve.wait_ge(mod_out, BP * (l + 1))
                m = mod[l][:, :].rearrange("p (b j c) -> p b j c", j=6, c=C)
                t3 = xc[:, 0:BP * C].rearrange("p (b c) -> p b c", c=C)
                t4 = xc[:, BP * C:2 * BP * C].rearrange("p (b c) -> p b c", c=C)
                for j in (CA, CB):
                    chain.link(dve.tensor_scalar(m[:, :, j, :], m[:, :, j, :], 1.0, None, ALU.add))
                for j in (GA, GB):
                    g = m[:, :, j, :]
                    chain.link(dve.tensor_scalar(t3, g, 0.0, 2.0, ALU.is_ge, ALU.mult))
                    chain.link(dve.scalar_tensor_tensor(t4, g, -1.0, g, ALU.mult, ALU.max))
                    chain.link(dve.tensor_scalar(t4, t4, 0.25, None, ALU.max))
                    chain.link(dve.scalar_tensor_tensor(g, t3, -1.0, t4, ALU.add, ALU.mult))
            m = mod[0][:, :].rearrange("p (b j c) -> p b j c", j=6, c=C)
            chain.link(dve.tensor_tensor(ga_d[:, :].rearrange("p (b c) -> p b c", c=C), m[:, :, GA, :],
                                         d_bc.unsqueeze(1).to_broadcast([P, BP, C]), ALU.mult))
            dve.wait_ge(x_in, 16 * B)
            finish(dve, 1)

            def layer_norm(l, k, j):
                with dve.Fori(0, BP) as i:
                    chain.enter(i, 1)
                    chain.link(dve.tensor_reduce(sums[:, ds(i * NC, NC)], tiles(x_sb, i), AX_X, ALU.add))
                    dve.scalar_tensor_tensor(tiles(xc, i), sums[:, ds(i * NC, NC)].unsqueeze(2).to_broadcast([P, NC, C]),
                                             -1.0 / C, tiles(x_sb, i), ALU.mult, ALU.add).then_inc(ln_centered, 1)
                chain.leave(BP)
                with dve.Fori(0, BP) as i:
                    dve.wait_ge(ln_squared, i + (4 * k + 1))
                    dve.tensor_reduce(var[:, ds(i * NC, NC)], tiles(sq, i), AX_X, ALU.add).then_inc(ln_var, 1)
                dve.wait_ge(ln_std, k + 1)
                chain.link(dve.reciprocal(rstd, rstd))
                with dve.Fori(0, BP) as i:
                    chain.enter(i, 1)
                    chain.link(dve.tensor_tensor(tiles(xc, i), tiles(xc, i),
                                                 rstd[:, ds(i * NC, NC)].unsqueeze(2).to_broadcast([P, NC, C]), ALU.mult))
                    dve.tensor_tensor(tiles(xc, i), tiles(xc, i), over_tiles(mod_of(l, i, j)), ALU.mult
                                      ).then_inc(ln_scaled, 1)
                chain.leave(BP)

            layer_norm(0, 0, CA)
            with dve.Fori(0, BP) as bp:
                chain.enter(bp, 2)
                dve.wait_ge(a0_rms, bp + 1)
                chain.link(dve.reciprocal(us, rms))
                chain.link(dve.scalar_tensor_tensor(us, ps[2][:, L:2 * L], dts, us, ALU.mult, ALU.mult))
                dve.tensor_tensor_scan(xs, a_bc, us, 0.0, ALU.mult, ALU.add).then_inc(a0_scan, 1)
                dve.wait_ge(a0_y, bp + 1)
                dve.wait_ge(a0_yg_used, bp + 1)
                dve.tensor_tensor(yg.rearrange("p (t c) -> p t c", c=C), ps[3][:, :].rearrange("p (t c) -> p t c", c=C),
                                  over_tiles(mod_of(0, bp, GA)), ALU.mult).then_inc(a0_gated, 1)
            chain.leave(BP)
            finish(dve, 2)

            def logits_out(k, dst):
                with dve.Fori(0, 2) as i:
                    for u in range(2):
                        bp = i * 2 + u
                        dve.wait_ge(lg_mm, bp + (4 * k + 1))
                        dve.tensor_copy(dst[:, ds(bp * (NC * E), NC * E)], ps[2][:, u * 512:u * 512 + NC * E]).then_inc(lg_out, 1)

            te = lambda ap: ap.rearrange("p (t e) -> p t e", e=E)
            over_e = lambda ap: ap.unsqueeze(2).to_broadcast([P, ap.shape[1], E])
            over_t = lambda ap, n=T: ap.unsqueeze(1).to_broadcast([P, n, ap.shape[1]])

            dve.wait_ge(gw, 32)
            chain.link(dve.tensor_tensor(wg_n[0:E, :], wg_s[0:E, :], wg_s[0:E, :], ALU.mult))
            dve.tensor_reduce(wg_t[0:E, 0:1], wg_n[0:E, :], AX_X, ALU.add).then_inc(gw, 1)
            dve.wait_ge(gw, 34)
            chain.link(dve.tensor_scalar(wg_t[0:E, 1:2], wg_n[0:E, 0:1], 1e-4, None, ALU.max))
            chain.link(dve.reciprocal(wg_t[0:E, 2:3], wg_t[0:E, 1:2]))
            dve.tensor_scalar(wg_n[0:E, :], wg_s[0:E, :], wg_t[0:E, 2:3], None, ALU.mult).then_inc(gw, 1)
            dve.wait_ge(gw, 36)
            dve.tensor_copy(wg_t[0:16, :], ps[3][0:16, 0:E]).then_inc(gw, 1)
            dve.wait_ge(gw, 38)
            dve.tensor_copy(w_gate, ps[3][:, 512:512 + E]).then_inc(gw, 1)
            layer_norm(0, 1, CB)
            logits_out(0, logits)
            finish(dve, 3)
            chain.link(dve.tensor_reduce(mx, te(logits), AX_X, ALU.max))
            chain.link(dve.tensor_tensor(te(shifted), te(logits), over_e(mx), ALU.subtract))
            chain.link(dve.scalar_tensor_tensor(te(pick), te(shifted), 0.0, over_t(first_w), ALU.is_equal, ALU.mult))
            dve.tensor_reduce(m2, te(pick), AX_X, ALU.max).then_inc(oh_done, 1)
            dve.wait_ge(oh_done, 1)
            chain.link(dve.tensor_tensor(te(onehot), te(pick), over_e(m2), ALU.is_equal))
            dve.tensor_copy(onehot_b, onehot).then_inc(rhs_ready, 1)
            dve.wait_ge(ex_done, 1)
            chain.link(dve.tensor_reduce(e_sum, te(e_exp), AX_X, ALU.add))
            chain.link(dve.reciprocal(score, e_sum))
            dve.wait_ge(cnt_done, 1)
            before_p, totals = ps[3][:, 0:256], ps[3][:, 512:768]
            for e in range(E):
                last = dve.tensor_tensor_scan(te(cum)[:, :, e], ones_f[:, 0:T], te(totals)[:, :, e], 0.0, ALU.mult, ALU.add)
            chain.link(last)
            chain.link(dve.tensor_tensor(rank, cum, totals, ALU.subtract))
            chain.link(dve.tensor_tensor(rank, rank, before_p, ALU.add))
            cnt = te(cum)[:, T - 1, :]
            c3 = n_cmp[:, 0:E * T].rearrange("p (e t) -> p e t", t=T)
            chain.link(dve.tensor_tensor(c3, cnt.unsqueeze(2).to_broadcast([P, E, T]), over_t(edges, E), ALU.is_gt))
            chain.link(dve.tensor_reduce(n_tiles[:, 0:E], c3, AX_X, ALU.add))
            chain.link(dve.tensor_tensor_scan(t_end[:, 0:E], ones_f[:, 0:E], n_tiles[:, 0:E], 0.0, ALU.mult, ALU.add))
            chain.link(dve.tensor_tensor(t_start[:, 0:E], t_end[:, 0:E], n_tiles[:, 0:E], ALU.subtract))
            chain.link(dve.tensor_scalar(t_start[:, 0:E], t_start[:, 0:E], float(P), None, ALU.mult))
            chain.link(dve.tensor_tensor(te(rank), te(rank), over_t(t_start[:, 0:E]), ALU.add))
            chain.link(dve.tensor_tensor(rank, rank, onehot, ALU.mult))
            chain.link(dve.tensor_reduce(slot_f, te(rank), AX_X, ALU.add))
            chain.link(dve.tensor_copy(slot_i[:, 0:T], slot_f))
            chain.link(dve.tensor_scalar(tile_i, slot_i[:, 0:T], 7, None, ALU.arith_shift_right))
            chain.link(dve.tensor_copy(tile_f, tile_i))
            chain.link(dve.scalar_tensor_tensor(row_f, tile_f, -float(P), slot_f, ALU.mult, ALU.add))
            c3 = n_cmp.rearrange("p (t e) -> p t e", e=E)
            chain.link(dve.tensor_tensor(c3, iota_t.unsqueeze(2).to_broadcast([P, 40, E]), over_t(t_end[:, 0:E], 40), ALU.is_ge))
            chain.link(dve.tensor_reduce(t_exp_f, c3, AX_X, ALU.add))
            chain.link(dve.tensor_scalar(t_exp_f, t_exp_f, float(E - 1), None, ALU.min))
            chain.link(dve.tensor_copy(t_exp_i, t_exp_f))
            t3 = tile_hot.rearrange("p (t s) -> p t s", s=40)
            r3 = t_rhs.rearrange("p (t k s) -> p t k s", k=2, s=40)
            chain.link(dve.tensor_tensor(t3, over_t(iota_t), tile_f.unsqueeze(2).to_broadcast([P, T, 40]), ALU.is_equal))
            dve.tensor_tensor(r3[:, :, 0, :], t3, tile_no.unsqueeze(2).to_broadcast([P, T, 40]), ALU.mult)
            dve.tensor_scalar(r3[:, :, 1, :], t3, part_no, None, ALU.mult).then_inc(rhs_ready, 1)
            with dve.Fori(0, T // 8) as i:
                dve.tensor_tensor(r_hot[:, ds(i * (8 * P), 8 * P)].rearrange("p (t s) -> p t s", s=P), over_t(iota_b[:, 0:P], 8),
                                  row_f[:, ds(i * 8, 8)].unsqueeze(2).to_broadcast([P, 8, P]), ALU.is_equal).then_inc(hot_made, 1)
            dve.wait_ge(ids_mm, 1)
            chain.link(dve.tensor_copy(id_f, ps[2][:, 0:80]))
            chain.link(dve.scalar_tensor_tensor(id_f[:, 0:40], id_f[:, 0:40], float(P), id_f[:, 40:80], ALU.mult, ALU.add))
            chain.link(dve.tensor_copy(ids_i, id_f[:, 0:40]))
            finish(dve, 4)
            dve.wait_ge(f0_w, 64)

            def add_bias1(g):
                of = [dve.value_load(t_exp_i[0:1, ds(g * GRP + t, 1)], min_val=0, max_val=E - 1) for t in range(GRP)]
                for t, e in enumerate(of):
                    dve.wait_ge(h_mm, g * GRP + (t // 2 * 2 + 2))
                    dve.tensor_tensor(hb[:, t * F0:(t + 1) * F0], ps[1][:, t * F0:(t + 1) * F0], b1a[:, ds(e * F0, F0)],
                                      ALU.add).then_inc(hb_ready, 1)

            def turned_out(g):
                dve.wait_ge(hg_turned, g + 1)
                dve.tensor_copy(hgT, ps[2][:, :]).then_inc(hgT_ready, 1)

            def add_bias2(g, u, n):
                of = [dve.value_load(t_exp_i[0:1, ds(g * GRP + t, 1)], min_val=0, max_val=E - 1) for t in range(GRP)]
                dve.wait_ge(o_stored[u], n * 16 + 16)
                dve.wait_ge(o_mm, g * GRP + GRP)
                for t, e in enumerate(of):
                    dve.tensor_tensor(o_st[u][:, t * C:(t + 1) * C], ps[3][:, t * C:(t + 1) * C], b2a[:, ds(e * C, C)],
                                      ALU.add).then_inc(o_ready, 1)

            def rows_out(g):
                dve.wait_ge(x_turned, g + 3)
                dve.tensor_copy(xg, ps[0][:, 0:GRP * C]).then_inc(xg_ready, 1)

            last = TILES0 // GRP - 1
            rows_out(0)
            add_bias1(0)
            with dve.Fori(0, (last - 1) // 2) as i:
                for g, u, n in ((i * 2 + 1, 0, i), (i * 2 + 2, 1, i)):
                    rows_out(g)
                    turned_out(g - 1)
                    add_bias1(g)
                    add_bias2(g - 1, u, n)
            rows_out(last)
            turned_out(last - 1)
            add_bias1(last)
            add_bias2(last - 1, 0, last // 2)
            turned_out(last)
            add_bias2(last, 1, last // 2)
            finish(dve, 5)

            with dve.Fori(0, 2) as i:
                for u in range(2):
                    bp = i * 2 + u
                    b3 = back[u].rearrange("p (t c) -> p t c", c=C)
                    dve.wait_ge(back_in[u], i * 128 + 128)
                    chain.enter(bp, 2)
                    chain.link(dve.tensor_tensor(b3, b3, score[:, ds(bp * NC, NC)].unsqueeze(2).to_broadcast([P, NC, C]), ALU.mult))
                    chain.link(dve.tensor_tensor(b3, b3, over_tiles(mod_of(0, bp, GB)), ALU.mult))
                    dve.tensor_tensor(tiles(x_sb, bp), tiles(x_sb, bp), b3, ALU.add).then_inc(back_used, 1)
                    if u == 0:
                        chain.base, chain.k = chain.outer, 0
            chain.leave(BP)
            finish(dve, 6)

            layer_norm(1, 2, CA)
            finish(dve, 7)
            with dve.Fori(0, 4) as i:
                for u in range(2):
                    n = i * 2 + u
                    dve.wait_ge(rt_tanh, n + 1)
                    dve.tensor_reduce(rate_sums[0:64, ds(n * 8, 8)], tg[u][0:64, :].rearrange("r (g n) -> r g n", n=CH),
                                      AX_X, ALU.add).then_inc(rt_sum, 1)
            dve.wait_ge(rt_sum, 10)
            dve.tensor_copy(rate_spread[0:32, :].rearrange("r (g n) -> r g n", n=CH),
                            rate_sums[0:32, :].unsqueeze(2).to_broadcast([32, 64, CH])).then_inc(rt_spread, 1)
            dve.wait_ge(rt_wd, 1)
            for k in range(2):
                dve.tensor_scalar(wd.rearrange("r (g k p) -> r k p g", k=2, p=HP)[:, k],
                                  ps[2][:, k * 512:(k + 1) * 512].rearrange("r (p g) -> r p g", p=HP),
                                  BASE_WD * 0.5 / CH, BASE_WD * 0.5, ALU.mult, ALU.add)
            dve.wait_ge(rt_lr, 1)
            for k in range(2):
                f = BASE_LR * (0.25, 0.5)[k]
                dve.tensor_scalar(lr.rearrange("r (t k h) -> r k t h", k=2, h=H)[:, k],
                                  ps[3][:, :].rearrange("r (t k h) -> r k t h", k=2, h=H)[:, k],
                                  f / CH, f, ALU.mult, ALU.add)
            finish(dve, 8)

            for j, bank in ((0, 1), (1, 2)):
                dve.wait_ge(tanh_out, j + 1)
                dve.scalar_tensor_tensor(qk[:, j * 1024:(j + 1) * 1024], th[j], 1.0, ps[bank][:, :],
                                         ALU.add, ALU.mult).then_inc(silu_done, 1)
            with dve.Fori(0, BP) as bp:
                dve.wait_ge(win_new, bp * (2 * NC) + 2)
                dve.tensor_copy(w_in[:, 1024:2048], w_init[:, 0:1024]).then_inc(win_set, 1)
                with dve.Fori(0, NC) as c:
                    t = bp * NC + c
                    chain.enter(t, 6)
                    for be in range(2):
                        g = slice(16 * be, 16 * be + 16)
                        z3 = zs[:, be * 1024:(be + 1) * 1024].rearrange("r (g n) -> r g n", n=CH)
                        p3 = ps[be][:, :].rearrange("r (g n) -> r g n", n=CH)
                        dve.wait_ge(pe_z, t * 2 + (be + 1))
                        chain.link(dve.tensor_reduce(z_max[:, g], p3, AX_X, ALU.max))
                        dve.tensor_tensor(z3, p3, z_max[:, g].unsqueeze(2).to_broadcast([P, 16, CH]), ALU.subtract
                                          ).then_inc(z_centered, 1)
                    for be in range(2):
                        g = slice(16 * be, 16 * be + 16)
                        dve.wait_ge(z_exp, t * 2 + (be + 1))
                        chain.link(dve.tensor_reduce(z_sum[:, g], zs[:, be * 1024:(be + 1) * 1024].rearrange(
                            "r (g n) -> r g n", n=CH), AX_X, ALU.add))
                        dve.reciprocal(z_rec[:, g], z_sum[:, g]).then_inc(z_summed, 1)
                    dve.wait_ge(z_summed, t * 2 + 2)
                    z4 = zs.rearrange("r (e p k n) -> r e p k n", e=2, p=HP, k=2)
                    r4 = z_rec.rearrange("r (e p k) -> r e p k", e=2, p=HP)
                    dve.tensor_tensor(prob[:, 1024:2048].rearrange("r (p e n) -> r e p n", e=2, n=CH), z4[:, :, :, 1, :],
                                      r4[:, :, :, 1].unsqueeze(3).to_broadcast([P, 2, HP, CH]), ALU.mult).then_inc(pk_norm, 1)

                    def silu_next(j, bank):
                        dve.wait_ge(tanh_out, t * 2 + (j + 3))
                        dve.scalar_tensor_tensor(qk[:, j * 1024:(j + 1) * 1024], th[j], 1.0, ps[bank][:, :],
                                                 ALU.add, ALU.mult).then_inc(silu_done, 1)

                    silu_next(0, 1)
                    h3 = lambda ap: ap.rearrange("r (h d) -> r h d", d=D)
                    dve.wait_ge(pe_a, t + 1)
                    dve.wait_ge(ptok_out, t + 1)
                    dve.wait_ge(v_scaled, t + 1)
                    chain.link(dve.tensor_tensor(pa, p_tok, ps[2][:, :], ALU.mult))
                    chain.link(dve.tensor_reduce(s_sum, h3(pa), AX_X, ALU.add))
                    dve.wait_ge(pe_kt, t + 1)
                    silu_next(1, 0)
                    dve.tensor_tensor(h3(pa), h3(ps[2][:, :]), s_sum.unsqueeze(2).to_broadcast([P, H, D]), ALU.subtract
                                      ).then_inc(dve_step2, 1)
                    dve.wait_ge(dve_step2, t + 1)
                    for be in range(2):
                        half = slice(be * CH, be * CH + CH)
                        last = dve.tensor_tensor(g_pad[half, :].rearrange("r (h e d) -> r h e d", e=2, d=D)[:, :, be, :],
                                                 h3(pa[half, :]), h3(p_tok[half, :]), ALU.mult)
                    last.then_inc(g_done, 1)

                    def update(w, k, be, bank, done):
                        for h in range(2):
                            half = slice(h * D, h * D + D)
                            last = dve.tensor_tensor(
                                w[half, be * 1024:(be + 1) * 1024].rearrange("r (p c) -> r p c", c=P)[:, :, half],
                                w_dec[half, (2 * k + be) * 1024:(2 * k + be + 1) * 1024].rearrange("r (p c) -> r p c", c=P)[:, :, half],
                                ps[bank][half, :].rearrange("r (p e c) -> r p e c", e=2, c=D)[:, :, be, :], ALU.add)
                        last.then_inc(done, 1)

                    dve.wait_ge(pe_gout, t + 1)
                    for be in range(2):
                        dve.wait_ge(dec_done, t * 2 + (be + 1))
                        update(w_out, 1, be, 0, wout_new)
                    dve.wait_ge(pe_gin, t + 1)
                    for be in range(2):
                        update(w_in, 0, be, 2, win_new)
                    dve.wait_ge(pe_y, t + 1)
                    dve.wait_ge(x_added, t + 1)
                    dve.tensor_tensor(y_gated, ps[1][:, 0:C], mod_of(1, bp, GA), ALU.mult).then_inc(y_scaled, 1)
            chain.base = chain.outer + T * chain.per
            chain.k = 0
            finish(dve, 9)

            layer_norm(1, 3, CB)
            logits_out(1, lg1)
            dve.wait_ge(lg_out, 10)
            chain.link(dve.tensor_reduce(mx, te(lg1), AX_X, ALU.max))
            dve.tensor_tensor(te(sh1), te(lg1), over_e(mx), ALU.subtract).then_inc(oh_done, 1)
            dve.wait_ge(ex_done, 2)
            chain.link(dve.tensor_reduce(e_sum, te(pr1), AX_X, ALU.add))
            chain.link(dve.reciprocal(e_sum, e_sum))
            chain.link(dve.tensor_tensor(te(pr1), te(pr1), over_e(e_sum), ALU.mult))
            top = [slot_f, tile_f]
            for k in range(2):
                hot = oh1[:, k * 256:(k + 1) * 256]
                chain.link(dve.tensor_reduce(top[k], te(pr1), AX_X, ALU.max))
                chain.link(dve.tensor_tensor(te(sh1), te(pr1), over_e(top[k]), ALU.is_equal))
                chain.link(dve.tensor_tensor(te(sh1), te(sh1), over_t(first_w), ALU.mult))
                chain.link(dve.tensor_reduce(m2, te(sh1), AX_X, ALU.max))
                chain.link(dve.tensor_tensor(te(hot), te(sh1), over_e(m2), ALU.is_equal))
                if k == 0:
                    chain.link(dve.scalar_tensor_tensor(pr1, hot, -2.0, pr1, ALU.mult, ALU.add))
            dve.tensor_copy(ohb1, oh1).then_inc(rhs_ready, 1)
            chain.link(dve.tensor_tensor(row_f, top[0], top[1], ALU.add))
            chain.link(dve.tensor_scalar(row_f, row_f, 1e-9, None, ALU.add))
            chain.link(dve.reciprocal(row_f, row_f))
            for k in range(2):
                chain.link(dve.tensor_tensor(wk[:, k * T:(k + 1) * T], top[k], row_f, ALU.mult))
            dve.wait_ge(cnt_done, 2)
            own, both, pref = ps[3][:, 512:1024], ps[2][:, 0:512], ps[3][:, 0:512]
            sums_over_c = lambda ap: ap.rearrange("p (k c e) -> p k e c", c=NC, e=E)
            k3 = lambda ap: ap.rearrange("p (k e) -> p k e", e=E)
            chain.link(dve.tensor_reduce(k3(own_t), sums_over_c(own), AX_X, ALU.add))
            chain.link(dve.tensor_reduce(k3(both_t), sums_over_c(both), AX_X, ALU.add))
            chain.link(dve.tensor_tensor(off1, both_t, own_t, ALU.subtract))
            chain.link(dve.tensor_scalar(off1, off1, batch_bit, None, ALU.mult))
            b4, o4 = (ap.rearrange("p (k b e) -> p k b e", k=2, b=BP) for ap in (both_t, off1))
            c2 = k3(cnt1)
            chain.link(dve.memset(cnt1, 0.0))
            for b in range(BP):
                chain.link(dve.tensor_tensor(o4[:, :, b, :], o4[:, :, b, :], c2, ALU.add))
                chain.link(dve.tensor_tensor(c2, c2, b4[:, :, b, :], ALU.add))
            chain.link(dve.tensor_scalar(cnt1[:, 0:E], cnt1[:, 0:E], float(CAP), None, ALU.min))
            chain.link(dve.tensor_tensor(o4[:, 1, :, :], o4[:, 1, :, :], cnt1[:, 0:E].unsqueeze(1).to_broadcast([P, BP, E]), ALU.add))
            r4, w4 = (ap.rearrange("p (k c e) -> p k c e", c=NC, e=E) for ap in (run1, own))
            chain.link(dve.tensor_copy(r4[:, :, 0, :], k3(off1)))
            for c in range(1, NC):
                chain.link(dve.tensor_tensor(r4[:, :, c, :], r4[:, :, c - 1, :], w4[:, :, c - 1, :], ALU.add))
            chain.link(dve.tensor_tensor(rk1, run1, pref, ALU.add))
            chain.link(dve.tensor_tensor(scr1, rk1, oh1, ALU.mult))
            chain.link(dve.tensor_reduce(pos, te(scr1), AX_X, ALU.add))
            r5 = rhs1.rearrange("p (t m e) -> p t m e", m=2, e=E)
            for k in range(2):
                dve.scalar_tensor_tensor(r5[:, k * T:(k + 1) * T, 0, :], over_e(tile_no), float(1 + k * T),
                                         te(oh1[:, k * 256:(k + 1) * 256]), ALU.add, ALU.mult)
            dve.tensor_scalar(r5[:, :, 1, :], te(oh1), part_no, None, ALU.mult).then_inc(rhs_ready, 1)
            with dve.Fori(0, T // 2) as i:
                for u in range(2):
                    t = i * 2 + u
                    dve.wait_ge(hot_used, t + 1)
                    for k in range(2):
                        last = dve.tensor_scalar(pos_hot[u][:, k * CAP:(k + 1) * CAP], iota_b[:, :], pos[:, ds(t + k * T, 1)],
                                                 None, ALU.is_equal)
                    last.then_inc(hot_made, 1)
            dve.wait_ge(ids_mm, 2)
            id3 = id_f[:, 0:32].rearrange("p (j m) -> p j m", j=2)
            chain.link(dve.tensor_copy(id3, ps[0][:, :].rearrange("p (j m) -> p j m", j=2)[:, :, 0:16]))
            chain.link(dve.scalar_tensor_tensor(id3[:, :, 0:E], id3[:, :, 0:E], float(P), id3[:, :, E:2 * E], ALU.mult, ALU.add))
            row3, in3, off3 = id3[:, :, 0:E], id3[:, :, E:2 * E], id_f[:, 32:48].rearrange("p (j e) -> p j e", j=2)
            chain.link(dve.tensor_scalar(off3, row3, 0.0, part_no, ALU.is_equal, ALU.mult))
            chain.link(dve.tensor_tensor(off3, off3, row3, ALU.add))
            chain.link(dve.tensor_copy(ids_i[:, 2 * E:4 * E].rearrange("p (j e) -> p j e", j=2), off3))
            chain.link(dve.tensor_scalar(in3, row3, -float(P), 0.0, ALU.add, ALU.max))
            chain.link(dve.tensor_scalar(off3, in3, float(B * L), -float(B * L), ALU.is_ge, ALU.mult))
            chain.link(dve.tensor_tensor(in3, in3, off3, ALU.add))
            chain.link(dve.tensor_copy(ids_i[:, 0:2 * E].rearrange("p (j e) -> p j e", j=2), in3))
            dve.sem_inc(ids_ready, 2)
            finish(dve, 10)
            def slot_rows_out(e):
                dve.wait_ge(x_turned, e + (TILES0 // GRP + 3))
                dve.tensor_copy(xg1, ps[0][:, 0:2 * C]).then_inc(xg_ready, 1)

            def results_out(e, u):
                dve.wait_ge(o1_free, e + 1)
                dve.wait_ge(o_mm, e + (TILES0 + 1))
                dve.tensor_tensor(o1_st[u].rearrange("p (t c) -> p t c", c=C),
                                  ps[3][:, u * 512:u * 512 + 2 * C].rearrange("p (t c) -> p t c", c=C),
                                  over_tiles(b2b[:, ds(e * C, C)], 2), ALU.add).then_inc(o_ready, 1)

            dve.wait_ge(f1_b, 32)
            slot_rows_out(0)
            with dve.Fori(0, E // 2 - 1) as i:
                for e, u in ((i * 2 + 1, 0), (i * 2 + 2, 1)):
                    slot_rows_out(e)
                    results_out(e - 1, u)
            slot_rows_out(E - 1)
            results_out(E - 2, 0)
            results_out(E - 1, 1)
            finish(dve, 11)
            for bp in range(BP):
                dve.wait_ge(y_in[bp], 32)
                b3 = [back1[:, (2 * bp + k) * W8:(2 * bp + k + 1) * W8].rearrange("p (t c) -> p t c", c=C) for k in range(2)]
                for k in range(2):
                    last = dve.tensor_tensor(b3[k], b3[k], wk[:, k * T + bp * NC:k * T + (bp + 1) * NC].unsqueeze(2
                                             ).to_broadcast([P, NC, C]), ALU.mult)
                chain.link(last)
                chain.link(dve.tensor_tensor(b3[0], b3[0], b3[1], ALU.add))
                dve.tensor_tensor(b3[0], b3[0], over_tiles(mod[1][:, (bp * 6 + GB) * C:(bp * 6 + GB + 1) * C]), ALU.mult
                                  ).then_inc(y_sum, 1)
            finish(dve, 12)

        @block.tensor
        def _(pe):
            pe.wait_ge(wm_in, 32)
            for l in range(2):
                pe.wait_ge(cond_spread, l + 1)
                for bp in range(BP):
                    n = BP * l + bp
                    if n >= 4:
                        pe.wait_ge(mod_out, n - 3)
                    for a, b in ((0, 512), (512, 768)):
                        mm = pe.matmul(ps[n % 4][:, a:b], st[l][:, bp * P:(bp + 1) * P], wm[l][:, a:b],
                                       start=True, stop=True)
                    mm.then_inc(mod_mm, 1)
            pe.wait_ge(consts_made, 1)
            pe.sem_inc(a0_yg_used, 1)
            finish(pe, 1)

            def turn(u, bp, k, last_use):
                pe.wait_ge(h_ready, bp + (4 * k + 1))
                for t in range(NC):
                    mm = pe.transpose(ps[u][:, t * P:(t + 1) * P], h_st[u][:, t * C:(t + 1) * C], ident[:, :])
                mm.then_inc(h_turned, 1)

            with pe.Fori(0, 2) as i:
                for u in range(2):
                    bp = i * 2 + u
                    turn(u, bp, 0, None)
                    pe.wait_ge(a0_sq, bp + 1)
                    for be in range(2):
                        pe.matmul(ps[2][be * S:(be + 1) * S, 0:L], ones_f[:, 0:S], hsq[:, be * L:(be + 1) * L],
                                  start=True, stop=True)
                    for be in range(2):
                        mm = pe.matmul(ps[2][be * S:(be + 1) * S, L:2 * L], nb, hT_st[u][:, be * L:(be + 1) * L],
                                       start=True, stop=True)
                    mm.then_inc(a0_up, 1)
                    pe.wait_ge(a0_scan, bp + 1)
                    apart(pe)
                    for t in range(NC):
                        for be in range(2):
                            half = slice(be * S, be * S + S)
                            mm = pe.matmul(ps[3][be * CH:(be + 1) * CH, t * C:(t + 1) * C],
                                           xs[half, t * CH:(t + 1) * CH], cmat[half, :], start=True, stop=True)
                    mm.then_inc(a0_y, 1)
            finish(pe, 2)

            def turn_and_gate(k, f, w):
                with pe.Fori(0, 2) as i:
                    for u in range(2):
                        bp = i * 2 + u
                        turn(u, bp, k, None)
                        pe.wait_ge(hT_ready, bp + (4 * k + 1))
                        pe.wait_ge(lg_out, bp + (4 * f + 1))
                        for t in range(NC):
                            mm = pe.matmul(ps[2][:, u * 512 + t * E:u * 512 + (t + 1) * E], hT_st[u][:, t * P:(t + 1) * P], w,
                                           start=True, stop=True)
                        mm.then_inc(lg_mm, 1)

            pe.wait_ge(gw, 35)
            pe.transpose(ps[3][0:16, 0:E], wg_n[0:E, :], ident[0:E, 0:E]).then_inc(gw, 1)
            pe.wait_ge(gw, 37)
            pe.matmul(ps[3][:, 512:512 + E], wred_t[0:16, :], wg_t[0:16, :], start=True, stop=True).then_inc(gw, 1)
            pe.wait_ge(gw, 39)
            pe.sem_inc(lg_out, 2)
            turn_and_gate(1, 0, w_gate)
            pe.sem_inc(x_turned, 2)
            pe.sem_inc(back_used, 2)
            finish(pe, 3)
            pe.wait_ge(rhs_ready, 1)
            pe.matmul(ps[3][:, 0:T * E], before, onehot_b, start=True, stop=True)
            pe.matmul(ps[3][:, 512:512 + T * E], all_ones, onehot_b, start=True, stop=True).then_inc(cnt_done, 1)
            pe.wait_ge(rhs_ready, 2)
            for t in range(T):
                if t % 8 == 0:
                    pe.wait_ge(hot_made, t // 8 + 1)
                mm = pe.matmul(ps[2][:, 0:80], r_hot[:, t * P:(t + 1) * P], t_rhs[:, t * 80:(t + 1) * 80],
                               start=(t == 0), stop=(t == T - 1))
            mm.then_inc(ids_mm, 1)
            finish(pe, 4)

            pe.wait_ge(f0_w, 64)

            def turn_x(g, u, n):
                pe.wait_ge(gathered[u], n * (16 * GRP) + 16 * GRP)
                for t in range(GRP):
                    mm = pe.transpose(ps[0][:, t * P:(t + 1) * P], gx[u][:, t * C:(t + 1) * C], ident[:, :])
                mm.then_inc(x_turned, 1)

            def first_product(g):
                of = [pe.value_load(t_exp_i[0:1, ds(g * GRP + t, 1)], min_val=0, max_val=E - 1) for t in range(GRP)]
                pe.wait_ge(xg_ready, g + 1)
                for t, e in enumerate(of):
                    pe.matmul(ps[1][:, t * F0:(t + 1) * F0], xg[:, t * P:(t + 1) * P], w1a[:, ds(e * F0, F0)],
                              start=True, stop=True).then_inc(h_mm, 1)

            def turn_hidden(g):
                pe.wait_ge(hg_ready, g + 1)
                for t in range(2 * GRP):
                    mm = pe.transpose(ps[2][:, t * P:(t + 1) * P], hb[:, t * P:(t + 1) * P], ident[:, :])
                mm.then_inc(hg_turned, 1)

            def second_product(g):
                of = [pe.value_load(t_exp_i[0:1, ds(g * GRP + t, 1)], min_val=0, max_val=E - 1) for t in range(GRP)]
                pe.wait_ge(hgT_ready, g + 1)
                for t, e in enumerate(of):
                    for j in range(2):
                        mm = pe.matmul(ps[3][:, t * C:(t + 1) * C], hgT[:, (2 * t + j) * P:(2 * t + j + 1) * P],
                                       w2a[:, ds(e * F0 + j * C, C)], start=(j == 0), stop=(j == 1))
                    mm.then_inc(o_mm, 1)

            last = TILES0 // GRP - 1
            turn_x(0, 0, 0)
            first_product(0)
            with pe.Fori(0, (last - 1) // 2) as i:
                for g, u, n in ((i * 2 + 1, 1, i), (i * 2 + 2, 0, i + 1)):
                    turn_x(g, u, n)
                    turn_hidden(g - 1)
                    first_product(g)
                    second_product(g - 1)
            turn_x(last, 1, last // 2)
            turn_hidden(last - 1)
            first_product(last)
            second_product(last - 1)
            turn_hidden(last)
            second_product(last)
            finish(pe, 5)
            finish(pe, 6)

            with pe.Fori(0, 2) as i:
                for u in range(2):
                    bp = i * 2 + u
                    pe.wait_ge(hT_ready, bp + (2 * BP - 1))
                    turn(u, bp, 2, None)
            pe.sem_inc(rt_sum, 2)
            finish(pe, 7)
            pe.wait_ge(wlb_in, 32)
            with pe.Fori(0, 4) as i:
                for u in range(2):
                    n = i * 2 + u
                    pe.wait_ge(rt_sum, n + 1)
                    pe.matmul(ps[u][0:64, 0:512], w_lb, hT[:, ds(n * 512, 512)], start=True, stop=True).then_inc(rt_mm, 1)
            pe.wait_ge(rt_sum, 10)
            for n in range(2 * HP):
                mm = pe.matmul(ps[2][:, n * 64:(n + 1) * 64], sel[0:64, n * P:(n + 1) * P], rate_sums[0:64, :],
                               start=True, stop=True)
            mm.then_inc(rt_wd, 1)
            pe.wait_ge(rt_spread, 1)
            for t in range(T):
                mm = pe.matmul(ps[3][:, t * 32:(t + 1) * 32], rate_spread[0:32, t * P:(t + 1) * P], ident[0:32, 0:32],
                               start=True, stop=True)
            mm.then_inc(rt_lr, 1)
            pe.sem_inc(win_new, 2)
            pe.sem_inc(wout_new, 2)
            pe.sem_inc(y_scaled, 1)
            finish(pe, 8)

            def project(j, bank, at, done):
                for p in range(HP):
                    mm = pe.matmul(ps[bank][:, p * P:(p + 1) * P], w_qkv[:, j * HD + p * P:j * HD + (p + 1) * P],
                                   hT[:, ds(at, P)], start=True, stop=True)
                mm.then_inc(done, 1)

            def turn_pairs(src, bank, done):
                for p in range(HP):
                    mm = pe.transpose(ps[bank][:, p * P:(p + 1) * P], src(p), ident[:, :])
                mm.then_inc(done, 1)

            def gradient(left, right, bank, done):
                for h in range(H):
                    mm = pe.matmul(ps[bank][h % 2 * D:(h % 2 + 1) * D, h // 2 * P:(h // 2 + 1) * P],
                                   left[:, h * D:(h + 1) * D], right[:, h * P:(h + 1) * P], start=True, stop=True)
                mm.then_inc(done, 1)

            pe.wait_ge(a1_w, 16 * 8)
            project(2, 0, 0, pe_pv)
            project(0, 1, 0, pe_pq)
            project(1, 2, 0, pe_pk)
            pe.wait_ge(vT_out, 1)
            with pe.Fori(0, BP) as bp:
                with pe.Fori(0, NC) as c:
                    t = bp * NC + c
                    pe.wait_ge(win_set, bp * 2 + 2)
                    w4 = lambda w, be, p: w[:, be * 1024 + p * P:be * 1024 + (p + 1) * P]
                    pe.wait_ge(silu_done, t * 2 + 2)
                    for be in range(2):
                        pe.wait_ge(win_new, t * 2 + (be + 1))
                        if be == 1:
                            pe.wait_ge(y_scaled, t + 1)
                        for p in range(HP):
                            mm = pe.matmul(ps[be][:, p * P:(p + 1) * P].rearrange("r (k n) -> r k n", k=2), w4(w_in, be, p),
                                           qk.rearrange("r (k p e n) -> r k p e n", k=2, p=HP, e=2)[:, :, p, be, :],
                                           start=True, stop=True)
                        mm.then_inc(pe_z, 1)
                    pe.wait_ge(wout_set, bp * 2 + 2)
                    for be, bank in ((0, 3), (1, 2)):
                        pe.wait_ge(wout_new, t * 2 + (be + 1))
                        turn_pairs(lambda p: w4(w_out, be, p), bank, pe_wt)
                    pe.wait_ge(z_centered, t * 2 + 1)
                    project(2, 0, t * P + P, pe_pv)
                    pe.wait_ge(woutT_out, t * 2 + 1)
                    pe.wait_ge(vT_out, t + 1)
                    turn_pairs(lambda p: vT[:, p * P:(p + 1) * P], 3, pe_vt)
                    pe.wait_ge(z_centered, t * 2 + 2)
                    project(0, 1, t * P + P, pe_pq)
                    pe.wait_ge(woutT_out, t * 2 + 2)
                    for p in range(HP):
                        for be in range(2):
                            mm = pe.matmul(ps[2][be * CH:(be + 1) * CH, p * P:(p + 1) * P],
                                           vT[:, p * P + be * CH:p * P + (be + 1) * CH], w4(w_outT, be, p),
                                           start=True, stop=True)
                    mm.then_inc(pe_a, 1)
                    pe.wait_ge(vtok_out, t + 1)
                    pe.wait_ge(pk_norm, t + 1)
                    turn_pairs(lambda p: prob[:, 1024 + p * P:1024 + (p + 1) * P], 3, pe_pt)
                    pe.wait_ge(vT_out, t + 2)
                    project(1, 0, t * P + P, pe_pk)
                    pe.wait_ge(ptok_out, t + 1)
                    turn_pairs(lambda p: qk[:, 1024 + p * P:1024 + (p + 1) * P], 3, pe_kt)
                    pe.wait_ge(silu_done, t * 2 + 3)
                    pe.wait_ge(pq_norm, t + 1)
                    for p in range(HP):
                        for be in range(2):
                            mm = pe.matmul(ps[1][:, p * P + be * CH:p * P + (be + 1) * CH], w4(w_out, be, p),
                                           prob[:, p * P + be * CH:p * P + (be + 1) * CH], start=True, stop=True)
                    mm.then_inc(pe_o, 1)
                    pe.wait_ge(silu_done, t * 2 + 4)
                    pe.wait_ge(v_scaled, t + 1)
                    gradient(p_tok, v_pad, 0, pe_gout)
                    pe.wait_ge(g_done, t + 1)
                    pe.wait_ge(k_scaled, t + 1)
                    gradient(k_tok, g_pad, 2, pe_gin)
                    pe.wait_ge(oT_out, t + 1)
                    for p in range(HP):
                        mm = pe.matmul(ps[1][:, 0:C], oT[:, p * P:(p + 1) * P], w_o[:, p * C:(p + 1) * C],
                                       start=(p == 0), stop=(p == HP - 1))
                    mm.then_inc(pe_y, 1)
            finish(pe, 9)

            pe.wait_ge(gw, 55)
            turn_and_gate(3, 1, wg1)
            pe.sem_inc(hot_used, 2)
            pe.wait_ge(rhs_ready, 3)
            pe.matmul(ps[3][:, 0:512], before_own, ohb1, start=True, stop=True)
            pe.matmul(ps[3][:, 512:1024], own_ones, ohb1, start=True, stop=True)
            pe.wait_ge(lg_out, 10)
            pe.matmul(ps[2][:, 0:512], all_ones, ohb1, start=True, stop=True).then_inc(cnt_done, 1)
            pe.wait_ge(rhs_ready, 4)

            def slot_numbers(t, u, first, last):
                pe.wait_ge(hot_made, t + (T // 8 + 1))
                for k in range(2):
                    for j in range(2):
                        mm = pe.matmul(ps[0][:, j * 512:j * 512 + 16], pos_hot[u][:, k * CAP + j * P:k * CAP + (j + 1) * P],
                                       rhs1[:, ds((t + k * T) * 16, 16)], start=first and k == 0, stop=last and k == 1)
                mm.then_inc(hot_used, 1)
                return mm

            for u in range(2):
                slot_numbers(u, u, u == 0, False)
            with pe.Fori(1, T // 2 - 1) as i:
                for u in range(2):
                    slot_numbers(i * 2 + u, u, False, False)
            for u in range(2):
                slot_numbers(T - 2 + u, u, False, u == 1)
            pe.wait_ge(hot_used, T + 2)
            pe.sem_inc(ids_mm, 1)
            finish(pe, 10)
            g0 = TILES0 // GRP
            def turn_slots(e, u, n):
                pe.wait_ge(gathered[u], n * 32 + (16 * TILES0 // 2 + 32))
                for t in range(2):
                    mm = pe.transpose(ps[0][:, t * P:(t + 1) * P], gx1[u][:, t * C:(t + 1) * C], ident[:, :])
                mm.then_inc(x_turned, 1)

            def slots_first(e, u, n):
                pe.wait_ge(f1_w[u], n * 32 + 32)
                pe.wait_ge(xg_ready, e + (g0 + 1))
                for j in range(4):
                    mm = pe.matmul(ps[1 + u][:, j * 256:(j + 1) * 256], w1s[u][:, j * P:(j + 1) * P], xg1, start=True, stop=True)
                mm.then_inc(h_mm, 1)

            def slots_second(e, u):
                pe.wait_ge(hg_ready, e + (g0 + 1))
                for t in range(2):
                    for j in range(4):
                        mm = pe.matmul(ps[3][:, u * 512 + t * C:u * 512 + (t + 1) * C],
                                       hg1[u][:, j * 256 + t * P:j * 256 + (t + 1) * P],
                                       w2s[u][:, j * C:(j + 1) * C], start=(j == 0), stop=(j == 3))
                mm.then_inc(o_mm, 1)

            turn_slots(0, 0, 0)
            slots_first(0, 0, 0)
            with pe.Fori(0, E // 2 - 1) as i:
                for e, u, n in ((i * 2 + 1, 1, i), (i * 2 + 2, 0, i + 1)):
                    turn_slots(e, u, n)
                    slots_first(e, u, n)
                    slots_second(e - 1, 1 - u)
            turn_slots(E - 1, 1, E // 2 - 1)
            slots_first(E - 1, 1, E // 2 - 1)
            slots_second(E - 2, 0)
            slots_second(E - 1, 1)
            finish(pe, 11)
            finish(pe, 12)


INS = ["L0_attn_u", "L0_attn_dt", "L0_attn_A", "L0_attn_Bmat", "L0_attn_C", "L0_attn_D", "L0_attn_norm_w",
       "L0_ffn_wg", "L0_ffn_W1", "L0_ffn_b1", "L0_ffn_W2", "L0_ffn_b2", "L0_wmod",
       "L1_ffn_Wg", "L1_ffn_W1", "L1_ffn_b1", "L1_ffn_W2", "L1_ffn_b2", "L1_wmod"]


def layouts(inputs):
    import numpy as np

    a = {n: np.ascontiguousarray(inputs[n]) for n in INS}
    t = lambda x, *axes: np.ascontiguousarray(np.transpose(np.asarray(x), axes))
    a["L0_cT"], a["L1_cT"] = t(inputs["L0_c"], 1, 0), t(inputs["L1_c"], 1, 0)
    for n in ("Wq", "Wk", "Wv", "Wlr", "Wbeta", "Wo"):
        a[f"L1_attn_{n}T"] = t(inputs[f"L1_attn_{n}"], 1, 0)
    w_in, w_out = np.asarray(inputs["L1_attn_W_in_init"])[0], np.asarray(inputs["L1_attn_W_out_init"])[0]
    a["L0_ffn_w_redT"] = t(inputs["L0_ffn_w_red"], 1, 0)
    a["L1_b1_cols"] = t(np.asarray(inputs["L1_ffn_b1"]).reshape(E, F1 // P, P), 2, 0, 1).reshape(P, -1)
    a["W_inT"] = t(w_in, 1, 2, 0)
    a["W_out"] = t(w_out, 1, 0, 2)
    return a


def kernel(**inputs):
    import numpy as np
    import concourse.bacc as bacc
    from concourse.bass_utils import run_bass_kernel_spmd

    nc = bacc.Bacc("TRN2", target_bir_lowering=False, num_devices=1)
    arrays = layouts(inputs)
    A = {n: nc.dram_tensor(f"in_{n}", a.shape, mybir.dt.from_np(a.dtype), kind="ExternalInput").ap()
         for n, a in arrays.items()}
    A["out"] = nc.dram_tensor("out_x", (B, L, C), F32, kind="ExternalOutput").ap()
    program(nc, A)
    r = run_bass_kernel_spmd(nc, [{f"in_{n}": a for n, a in arrays.items()}], core_ids=[0])
    return r.results[0]["out_x"]
```

```python
from contextlib import ExitStack

import concourse.bass as bass
from concourse import mybir

ALU = mybir.AluOpType
ACT = mybir.ActivationFunctionType
AX_X = mybir.AxisListType.X
F32 = mybir.dt.float32
BF16 = mybir.dt.bfloat16
I32 = mybir.dt.int32
ds = bass.ds

P = 128
B, L, C = 8, 512, 128
BP = B // 2
CH = 64
NC = L // CH
T = BP * NC
W8 = NC * C
S = 64
E = 8
F0 = 256
F1 = 512
CAP = 256
H, D = 16, 64
HP = H // 2
HD = H * D
TILES0 = T + E
GRP = 4
ACT_TILES = 5
LN_ONCE = (0, 1, 2, 6)
LN_EPS, RMS_EPS = 1e-5, 1e-6
BASE_LR, BASE_WD = 0.001, 0.9
SA, CA, GA, SB, CB, GB = range(6)


class Chain:

    def __init__(self, eng, sem):
        self.eng, self.sem, self.base, self.k = eng, sem, 0, 0

    def link(self, ins):
        ins.then_inc(self.sem, 1)
        self.k += 1
        self.eng.wait_ge(self.sem, self.base + self.k)

    def enter(self, i, per):
        self.outer, self.per = self.base + self.k, per
        self.base, self.k = self.outer + i * per, 0

    def step(self):
        assert self.k == self.per, (self.k, self.per)
        self.base, self.k = self.outer, 0

    def leave(self, n):
        if self.k:
            self.step()
        self.base = self.outer + n * self.per


def program(nc, A):
    ctx = ExitStack()
    with ctx:
        def sb(name, shape, dt=F32):
            return ctx.enter_context(nc.sbuf_tensor(name, shape, dt))

        def sem(name):
            return ctx.enter_context(nc.semaphore(name))

        x_sb = sb("x_sb", [P, T * C])
        mod = [sb(f"mod{l}", [P, BP * 6 * C]) for l in range(2)]
        ident = sb("ident", [P, P])
        ones_f = sb("ones_f", [P, P])
        hT = sb("hT", [P, (T + 1) * P])
        w_qkv = sb("w_qkv", [P, 3 * HD])
        w_o = sb("w_o", [P, HP * C])
        w_init = sb("w_init", [P, 2 * HP * P])
        small = sb("small", [P, 512])
        masks = sb("masks", [P, 4 * P], BF16)
        before, before_own, all_ones, own_ones = (masks[:, n * P:(n + 1) * P] for n in range(4))
        iota_b = sb("iota_b", [P, CAP], BF16)
        consts = sb("consts", [P, 128])
        iota_t, first_w, edges, tile_no = (consts[:, a:b] for a, b in ((0, 40), (40, 48), (56, 88), (88, 120)))
        part_no, batch_bit = consts[:, 120:121], consts[:, 121:122]
        arena = sb("arena", [P, 27648])

        def view(at, n, dt=F32):
            v = arena[:, at:at + n]
            return v if dt is F32 else v.bitcast(dt)

        sums, var, rstd = small[:, 0:T], small[:, 32:32 + T], small[:, 64:64 + T]
        ln_eps, rms_eps = small[:, 96:97], small[:, 97:98]
        dt2, a2, dts, decay = (small[:, 98 + n:99 + n] for n in range(4))
        dt_terms = small[:, 102:106]

        ps = [ctx.enter_context(nc.psum_tensor(f"ps{i}", [P, 1024], F32)) for i in range(4)]

        xc = view(0, T * C)
        sq = view(4096, T * C)
        stats = view(8192, 6 * T)
        spread = view(8384, 3 * T)
        yg = [view(8704 + 1024 * u, W8) for u in range(2)]
        states = [view(12800 + L * u, L) for u in range(2)]
        xs = [view(10752 + 1024 * u, W8) for u in range(2)]
        a_bc = view(15872, L)
        nb = view(16384, S)
        bmat = view(16448, S)
        normw = view(16512, 1)
        cmat = view(16576, C)
        d_row = view(13824, 4 * C)
        ct = view(17000, 16)
        cth = view(17016, 16)
        st = [view(17100 + 512 * l, 512) for l in range(2)]
        wm = [view(18200 + 768 * l, 768) for l in range(2)]

        w1a, w2a, b1a, b2a = view(12288, E * F0), view(14336, E * F0), view(16384, E * F0), view(18432, E * C)
        logits, shifted, e_exp, pick, onehot, cum, rank = (view(19456 + 256 * n, T * E) for n in range(7))
        onehot_b = view(21504, T * E // 2, BF16)
        n_cmp = view(21632, 320)
        tile_hot = view(21952, T * 40)
        w_gate, wg_n, wg_s, wg_t, wred_t = view(23232, E), view(23240, 16), view(23256, 16), view(23272, E), view(23280, C)
        r_hot = view(0, T * P // 2, BF16)
        t_rhs = view(2048, T * 80 // 2, BF16)
        gx = [view(4096 + 512 * u, GRP * C) for u in range(2)]
        xg = view(5120, GRP * C)
        hb = view(5632, GRP * F0)
        hgT = view(6656, GRP * F0)
        o_st = [view(7680 + 512 * u, GRP * C) for u in range(2)]
        back = [view(21600 + 1024 * u, W8) for u in range(2)]
        route = sb("route", [P, 1024])
        mx, m2, slot_f, tile_f, row_f, score, e_sum, n_tiles, t_end, t_start = (route[:, 32 * n:32 * n + 32] for n in range(10))
        wk, pos, e_of, keep = (route[:, 320 + 64 * n:384 + 64 * n] for n in range(4))
        id_f = route[:, 576:656]
        ids_i = route[:, 656:696].bitcast(I32)
        t_exp_i = route[:, 696:736].bitcast(I32)
        slot_i = route[:, 736:800].bitcast(I32)
        tile_i = route[:, 800:832].bitcast(I32)
        idx_st = [route[:, 832 + n:833 + n].bitcast(I32) for n in range(32)]
        t_exp_f = route[:, 864:904]
        w1s = [view(12288 + 512 * u, F1) for u in range(2)]
        w2s = view(19840, E * F1)
        b1t, b2b = view(14336, E * 4), view(14400, E * C)
        wg1 = view(15424, E)
        lg1, sh1, pr1 = view(15488, 256), view(15744, 256), view(16000, 256)
        oh1 = view(16256, 512)
        ohb1 = view(16768, 256, BF16)
        run1 = view(17024, 512)
        rk1, scr1 = view(17536, 512), view(18048, 512)
        own_t, both_t, off1 = view(18560, 64), view(18624, 64), view(18688, 64)
        rhs1 = view(18752, 1024, BF16)
        numbers = view(17024, 512, BF16)
        cnt1 = view(19776, 16)
        pos_hot = view(0, T * P, BF16)
        gx1 = [view(4096 + 256 * u, 2 * C) for u in range(2)]
        xg1 = view(5120, 2 * C)
        hg1 = [view(5632 + 1024 * u, 4 * 2 * C) for u in range(2)]
        back1 = view(0, 2 * BP * W8)
        o1_st = [view(7680 + 256 * u, 2 * C) for u in range(2)]

        h_dram = [nc.dram_tensor(f"h_rows{f}", (B * L, C), F32, kind="Internal").ap() for f in range(2)]
        o_dram = nc.dram_tensor("o_rows", (TILES0 * P, C), F32, kind="Internal").ap()
        y_dram = nc.dram_tensor("y_rows", (P + 2 * B * L, C), F32, kind="Internal").ap()

        w_lb = view(14336, S)
        own_f, parity = view(12288, P), view(12416, P)
        tg = [view(16384 + 512 * u, 512) for u in range(2)]
        t_tok = view(17408, T * 2 * H)
        rate_sums = view(18432, 64)
        rate_diag = view(18496, 1024)
        rate_row, rate_pair = small[:, 368:400], small[:, 400:416]
        qk = view(0, 2048)
        vT = view(2048, 1024)
        k_tok, v_tok = view(3072, 1024), view(4096, 1024)
        zs = view(5120, 2048)
        prob = view(7168, 2048)
        p_tok, pa = view(9216, 1024), v_tok
        g_pad, v_pad = view(10240, 2048), sb("v_pad", [P, 2048])[:, :]
        oT = view(12288, 1024)
        th = [view(13312 + 1024 * u, 1024) for u in range(2)]
        w_dec = view(15360, 4096)
        w_in, w_out, w_outT = view(19456, 2048), view(21504, 2048), view(23552, 2048)
        wd = view(25600, 1024)
        lr = view(26624, 1024)
        y_gated = small[:, 128:256]
        z_max, z_sum, z_rec = small[:, 256:288], small[:, 288:320], small[:, 320:352]
        s_sum = small[:, 352:368]

        phase_end, passed = sem("phase_end"), sem("passed")
        x_in, c_in, wm_in, a0_in = sem("x_in"), sem("c_in"), sem("wm_in"), sem("a0_in")
        stats_done, difference_made = sem("stats_done"), sem("difference_made")
        consts_made, dve_step, pool_step = sem("consts_made"), sem("dve_step"), sem("pool_step")
        cond_tanh, cond_spread = sem("cond_tanh"), sem("cond_spread")
        mod_mm, mod_out = sem("mod_mm"), sem("mod_out")
        ln_var, ln_std, ln_rates, ln_normed, ln_scaled = (sem("ln_" + n) for n in ("var", "std", "rates", "normed", "scaled"))
        h_ready, h_turned, hT_ready = (sem(n) for n in ("h_ready", "h_turned", "hT_ready"))
        a0_exp, a0_par, a0_sq, a0_sum, a0_rms, a0_rec, a0_normed, a0_up, a0_scan, a0_spread, a0_y, a0_gated, a0_added = (
            sem("a0_" + n) for n in ("exp", "par", "sq", "sum", "rms", "rec", "normed", "up", "scan", "spread", "y", "gated", "added"))
        a1_w, wlb_in = sem("a1_w"), sem("wlb_in")
        rt_mm, rt_tanh, rt_sum, rt_spread, rt_wd, rt_lr, rt_tok, rt_tok_tanh = (
            sem("rt_" + n) for n in ("mm", "tanh", "sum", "spread", "wd", "lr", "tok", "tok_tanh"))
        pe_z, pe_a, pe_vt, pe_kt, pe_pv, pe_pq, pe_pk, pe_pt, pe_o, pe_gout, pe_y, pe_gin, pe_wt = (
            sem("pe_" + n) for n in ("z", "a", "vt", "kt", "pv", "pq", "pk", "pt", "o", "gout", "y", "gin", "wt"))
        win_set, wout_set = sem("win_set"), sem("wout_set")
        z_centered, z_summed, pk_norm, silu_done, g_done, wout_new, y_scaled, win_new = (
            sem(n) for n in ("z_centered", "z_summed", "pk_norm", "silu_done", "g_done", "wout_new", "y_scaled", "win_new"))
        z_exp, vT_out, tanh_out, vtok_out, ktok_out, ptok_out, oT_out, woutT_out = (
            sem(n) for n in ("z_exp", "vT_out", "tanh_out", "vtok_out", "ktok_out", "ptok_out", "oT_out", "woutT_out"))
        pq_norm, v_scaled, k_scaled, dec_done, x_added = (sem(n) for n in ("pq_norm", "v_scaled", "k_scaled", "dec_done", "x_added"))
        h_stored = sem("h_stored")
        lg_mm, lg_out, ex_done, oh_done, cnt_done, rhs_ready, ids_mm, gw = (
            sem(n) for n in ("lg_mm", "lg_out", "ex_done", "oh_done", "cnt_done", "rhs_ready", "ids_mm", "gw"))
        f0_w, f1_b, idx_copied = sem("f0_w"), sem("f1_b"), sem("idx_copied")
        f1_w = [sem(f"f1_w{u}") for u in range(2)]
        y_zeroed, y_idx_copied, y_scattered, o1_free, y_sum, y_second, x_final = (
            sem(n) for n in ("y_zeroed", "y_idx_copied", "y_scattered", "o1_free", "y_sum", "y_second", "x_final"))
        y_in = [sem(f"y_in{bp}") for bp in range(BP)]
        gathered = [sem(f"gathered{u}") for u in range(2)]
        x_turned, xg_ready, h_mm, hb_ready, hg_ready, hg_turned, hgT_ready, o_mm, o_ready = (
            sem("ex_" + n) for n in ("x_turned", "xg_ready", "h_mm", "hb_ready", "hg_ready", "hg_turned", "hgT_ready", "o_mm", "o_ready"))
        o_stored = [sem(f"o_stored{u}") for u in range(2)]
        back_in = [sem(f"back_in{u}") for u in range(2)]
        back_used, hot_made = sem("back_used"), sem("hot_made")
        out_sem = sem("out_sem")

        block = ctx.enter_context(nc.Block())

        def tiles(ap, i, n=NC):
            return ap[:, ds(i * (n * C), n * C)].rearrange("p (t c) -> p t c", c=C)

        def mod_of(l, bp, j):
            return mod[l][:, ds(bp * (6 * C) + j * C, C)]

        def over_tiles(ap, n=NC):
            return ap.unsqueeze(1).to_broadcast([P, n, C])

        def finish(eng, n):
            eng.drain().then_inc(phase_end, 1)
            eng.wait_ge(phase_end, 5 * n)

        def apart(eng):
            eng.sem_inc(passed, 1)

        def experts_of(eng, g):
            four = eng.value_load(t_exp_i[0:1, ds(g, 1)], min_val=0, max_val=E ** GRP - 1)
            return [((four >> (3 * t)) & (E - 1)).with_bounds(min_val=0, max_val=E - 1) for t in range(GRP)]

        @block.sync
        def _(sp):
            for b in range(B):
                bp, be = divmod(b, 2)
                sp.dma_start(x_sb[be * CH:(be + 1) * CH, bp * W8:(bp + 1) * W8].rearrange("p (t c) -> p t c", c=C),
                             A["L0_attn_u"][b].rearrange("(t p) c -> p t c", p=CH)).then_inc(x_in, 16)
            for l in range(2):
                sp.dma_start(ct[:, 8 * l:8 * l + 8], A[f"L{l}_cT"]).then_inc(c_in, 16)
                sp.dma_start(wm[l], A[f"L{l}_wmod"]).then_inc(wm_in, 16)
            col = lambda v: v.rearrange("(a b) -> a b", b=1)
            row = lambda v: v.rearrange("(a b) -> a b", a=1)
            for be in range(2):
                half = slice(be * S, be * S + S)
                sp.dma_start(dt2[half], col(A["L0_attn_dt"])).then_inc(a0_in, 16)
                sp.dma_start(a2[half], col(A["L0_attn_A"])).then_inc(a0_in, 16)
                sp.dma_start(cmat[half], A["L0_attn_C"]).then_inc(a0_in, 16)
            sp.dma_start(bmat, A["L0_attn_Bmat"]).then_inc(a0_in, 16)
            sp.dma_start(normw, col(A["L0_attn_norm_w"])).then_inc(a0_in, 16)
            sp.dma_start(d_row[0:1, :].rearrange("a (k c) -> a k c", c=C),
                         row(A["L0_attn_D"]).unsqueeze(1).to_broadcast([1, 4, C])).then_inc(a0_in, 16)
            sp.dma_start(wg_s[0:E, :], A["L0_ffn_wg"]).then_inc(gw, 16)
            sp.dma_start(wred_t[0:16, :], A["L0_ffn_w_redT"]).then_inc(gw, 16)
            for n, w in enumerate(("Wq", "Wk", "Wv")):
                sp.dma_start(w_qkv[:, n * HD:(n + 1) * HD], A[f"L1_attn_{w}T"]).then_inc(a1_w, 16)
            sp.dma_start(w_o[:, :].rearrange("r (p c) -> r p c", c=C),
                         A["L1_attn_WoT"].rearrange("(p r) c -> r p c", r=P)).then_inc(a1_w, 16)
            sp.wait_ge(consts_made, 1)
            w3 = w_init[:, :].rearrange("r (k p c) -> r k p c", k=2, c=P)
            for k, n in enumerate(("W_inT", "W_out")):
                for h in range(2):
                    half = slice(h * D, h * D + D)
                    sp.dma_start(w3[half, k, :, half], A[n].rearrange("(p h) r c -> h r p c", h=2)[h]).then_inc(a1_w, 16)
            finish(sp, 1)
            finish(sp, 2)

            def store_h(f, k):
                with sp.Fori(0, BP) as bp:
                    sp.wait_ge(h_ready, bp + (4 * k + 1))
                    sp.dma_start(h_dram[f][ds(bp * (NC * P), NC * P), :].rearrange("(t p) c -> p t c", p=P),
                                 tiles(xc, bp)).then_inc(h_stored, 16)

            sp.dma_start(w1a.rearrange("c (e f) -> c e f", e=E), A["L0_ffn_W1"].rearrange("e c f -> c e f")).then_inc(f0_w, 16)
            sp.dma_start(w2a.rearrange("r (e j c) -> r e j c", e=E, j=2),
                         A["L0_ffn_W2"].rearrange("e (j r) c -> r e j c", r=P)).then_inc(f0_w, 16)
            sp.dma_start(b1a, A["L0_ffn_b1"].rearrange("(a e) f -> a (e f)", a=1).to_broadcast([P, E * F0])).then_inc(f0_w, 16)
            sp.dma_start(b2a, A["L0_ffn_b2"].rearrange("(a e) f -> a (e f)", a=1).to_broadcast([P, E * C])).then_inc(f0_w, 16)
            store_h(0, 1)
            finish(sp, 3)
            finish(sp, 4)
            with sp.Fori(0, TILES0 // GRP // 2) as i:
                for u in range(2):
                    g = i * 2 + u
                    sp.wait_ge(o_ready, g * GRP + GRP)
                    sp.dma_start(o_dram[ds(g * (GRP * P), GRP * P), :].rearrange("(t p) c -> p t c", p=P),
                                 o_st[u].rearrange("p (t c) -> p t c", c=C)).then_inc(o_stored[u], 16)
            for u in range(2):
                sp.wait_ge(o_stored[u], 16 * (TILES0 // GRP // 2) + 16)
            finish(sp, 5)
            sp.dma_start(w_lb[:, 0:32], A["L1_attn_WlrT"]).then_inc(wlb_in, 16)
            sp.dma_start(w_lb[:, 32:64], A["L1_attn_WbetaT"]).then_inc(wlb_in, 16)
            finish(sp, 6)
            for n in range(2 * BP):
                r0 = P + n * NC * P
                sp.dma_start(y_dram[r0:r0 + NC * P, :].rearrange("(t p) c -> p t c", p=P),
                             hT[:, T * P:(T + 1) * P].unsqueeze(1).to_broadcast([P, NC, C])).then_inc(y_zeroed, 16)
            finish(sp, 7)

            sp.dma_start(wg1, A["L1_ffn_Wg"]).then_inc(gw, 16)
            sp.dma_start(b1t, A["L1_b1_cols"]).then_inc(f1_b, 16)
            sp.dma_start(b2b, A["L1_ffn_b2"].rearrange("(a e) f -> a (e f)", a=1).to_broadcast([P, E * C])).then_inc(f1_b, 16)

            def expert_weights(e, u):
                sp.dma_start(w1s[u], A["L1_ffn_W1"].rearrange("e c f -> (e c) f")[ds(e * C, C), :]).then_inc(f1_w[u], 16)

            for u in range(2):
                expert_weights(u, u)
            store_h(1, 3)
            sp.dma_start(w2s.rearrange("r (e j c) -> r e j c", e=E, j=4),
                         A["L1_ffn_W2"].rearrange("e (j r) c -> r e j c", r=P)).then_inc(f1_b, 16)
            finish(sp, 8)
            with sp.Fori(1, E // 2) as i:
                for u in range(2):
                    e = i * 2 + u
                    sp.wait_ge(h_mm, e + (TILES0 - 1))
                    expert_weights(e, u)
            finish(sp, 9)
            for bp in range(BP):
                for k in range(2):
                    r0 = P + k * B * L + bp * NC * P
                    sp.dma_start(back1[:, (2 * bp + k) * W8:(2 * bp + k + 1) * W8].rearrange("p (t c) -> p t c", c=C),
                                 y_dram[r0:r0 + NC * P, :].rearrange("(t p) c -> p t c", p=P)).then_inc(y_in[bp], 16)
            for b in range(B):
                bp, be = divmod(b, 2)
                sp.wait_ge(x_final, bp + 1)
                sp.dma_start(A["out"][b].rearrange("(t p) c -> p t c", p=CH),
                             x_sb[be * CH:(be + 1) * CH, bp * W8:(bp + 1) * W8].rearrange("p (t c) -> p t c", c=C)
                             ).then_inc(out_sem, 16)
            finish(sp, 10)
            sp.wait_ge(out_sem, 16 * B)

        @block.gpsimd
        def _(pool):
            chain = Chain(pool, pool_step)
            chain.link(pool.memset(ident[:, :], 0.0))
            chain.link(pool.memset(ones_f[:, :], 1.0))
            chain.link(pool.memset(ln_eps, LN_EPS))
            chain.link(pool.memset(rms_eps, RMS_EPS))
            chain.link(pool.memset(w_init[:, :], 0.0))
            chain.link(pool.memset(hT[:, T * P:(T + 1) * P], 0.0))
            chain.link(pool.affine_select(out=ident[:, :], in_=ident[:, :], compare_op=ALU.not_equal, fill=1.0, base=0,
                               pattern=[[-1, P]], channel_multiplier=1))
            chain.link(pool.memset(masks[:, :], 1.0))
            chain.link(pool.memset(part_no, 0.0))
            chain.link(pool.affine_select(out=masks[:, 0:2 * P].rearrange("q (k p) -> q k p", k=2), in_=masks[:, 0:2 * P].rearrange("q (k p) -> q k p", k=2),
                               compare_op=ALU.is_gt, fill=0.0, base=0, pattern=[[0, 2], [1, P]], channel_multiplier=-1))
            chain.link(pool.memset(before_own[0:CH, CH:P], 0.0))
            chain.link(pool.memset(own_ones[0:CH, CH:P], 0.0))
            chain.link(pool.memset(own_ones[CH:P, 0:CH], 0.0))
            imprecise = dict(allow_small_or_imprecise_dtypes=True)
            chain.link(pool.iota(iota_b[:, :], pattern=[[1, CAP]], base=0, channel_multiplier=0, **imprecise))
            chain.link(pool.iota(iota_t, pattern=[[1, 40]], base=0, channel_multiplier=0, **imprecise))
            chain.link(pool.iota(first_w, pattern=[[-1, E]], base=E, channel_multiplier=0, **imprecise))
            chain.link(pool.iota(edges, pattern=[[P, T]], base=0, channel_multiplier=0, **imprecise))
            chain.link(pool.iota(tile_no, pattern=[[1, T]], base=0, channel_multiplier=0, **imprecise))
            chain.link(pool.iota(part_no, pattern=[[0, 1]], base=0, channel_multiplier=1, **imprecise))
            chain.link(pool.memset(rate_row, 0.0))
            chain.link(pool.affine_select(out=rate_row[0:32, :], in_=rate_row[0:32, :], compare_op=ALU.not_equal, fill=1.0, base=0,
                                          pattern=[[-1, 2 * H]], channel_multiplier=1))
            chain.link(pool.memset(batch_bit[0:CH], 0.0))
            chain.link(pool.memset(batch_bit[CH:P], 1.0))
            pool.sem_inc(consts_made, 1)
            for u in range(2):
                chain.link(pool.memset(xs[u], 0.0))
                pool.sem_inc(o_stored[u], 16)
            finish(pool, 1)

            def add_shift(l, k, j):
                with pool.Fori(0, BP) as bp:
                    pool.wait_ge(ln_scaled, bp + (4 * min(k, 2) + 1))
                    pool.tensor_tensor(tiles(xc, bp), tiles(xc, bp), over_tiles(mod_of(l, bp, j)), ALU.add).then_inc(h_ready, 1)

            add_shift(0, 0, SA)
            with pool.Fori(0, 2) as i:
                for u in range(2):
                    bp = i * 2 + u
                    pool.wait_ge(a0_gated, bp + 1)
                    pool.tensor_tensor(tiles(x_sb, bp), tiles(x_sb, bp), yg[u].rearrange("p (t c) -> p t c", c=C), ALU.add
                                       ).then_inc(a0_added, 1)
            finish(pool, 2)

            def gather_back(base):
                with pool.Fori(0, 2) as i:
                    for u in range(2):
                        bp = i * 2 + u
                        pool.wait_ge(back_used, bp + 1)
                        for t in range(NC):
                            pool.tensor_copy(idx_st[8 * u + t], slot_i[:, ds(bp * NC + t, 1)]).then_inc(idx_copied, 1)
                        pool.wait_ge(idx_copied, bp * NC + (base + NC))
                        apart(pool)
                        for t in range(NC):
                            pool.indirect_dma_start(
                                back[u][:, t * C:(t + 1) * C], None, o_dram[:, :],
                                bass.IndirectOffsetOnAxis(ap=idx_st[8 * u + t], axis=0),
                                bounds_check=TILES0 * P - 1, oob_is_err=False).then_inc(back_in[u], 16)

            add_shift(0, 1, SB)
            finish(pool, 3)
            finish(pool, 4)
            pool.wait_ge(h_stored, 64)
            n0 = 0
            with pool.Fori(0, TILES0 // GRP // 2) as i:
                for u in range(2):
                    g = i * 2 + u
                    pool.wait_ge(x_turned, g + 1)
                    for t in range(GRP):
                        pool.tensor_copy(idx_st[GRP * u + t], ids_i[:, ds(g * GRP + t, 1)]).then_inc(idx_copied, 1)
                    pool.wait_ge(idx_copied, g * GRP + (n0 + GRP))
                    apart(pool)
                    for t in range(GRP):
                        pool.indirect_dma_start(gx[u][:, t * C:(t + 1) * C], None, h_dram[0][:, :],
                                                bass.IndirectOffsetOnAxis(ap=idx_st[GRP * u + t], axis=0),
                                                bounds_check=B * L - 1, oob_is_err=False).then_inc(gathered[u], 16)
            n0 += TILES0
            finish(pool, 5)
            gather_back(n0)
            n0 += T
            pool.memset(g_pad, 0.0)
            pool.memset(v_pad, 0.0)
            finish(pool, 6)

            pool.sem_inc(x_added, 1)
            with pool.Fori(0, BP) as bp:
                with pool.Fori(0, NC) as c:
                    t = bp * NC + c
                    pool.wait_ge(win_set, bp * 2 + 2)
                    pool.wait_ge(wout_set, bp * 2 + 2)
                    for be in range(2):
                        pool.wait_ge(win_new, t * 2 + (be + 1))
                        pool.wait_ge(wout_new, t * 2 + (be + 1))
                        for k, w in enumerate((w_in, w_out)):
                            last = pool.tensor_tensor(
                                w_dec[:, (2 * k + be) * 1024:(2 * k + be + 1) * 1024].rearrange("r (p c) -> r p c", c=P),
                                w[:, be * 1024:(be + 1) * 1024].rearrange("r (p c) -> r p c", c=P),
                                wd[:, ds(t * 32 + (16 * be + 8 * k), HP)].unsqueeze(2).to_broadcast([P, HP, P]), ALU.mult)
                        last.then_inc(dec_done, 1)
                    pool.wait_ge(vtok_out, t + 1)
                    chain.enter(t, 1)
                    for be in range(2):
                        half = slice(be * CH, be * CH + CH)
                        last = pool.tensor_tensor(v_pad[half, :].rearrange("r (h e d) -> r h e d", e=2, d=D)[:, :, be, :],
                                                  v_tok[half, :].rearrange("r (h d) -> r h d", d=D),
                                                  lr[half, ds(t * 32 + H, H)].unsqueeze(2).to_broadcast([CH, H, D]), ALU.mult)
                        if be == 0:
                            chain.link(last)
                    last.then_inc(v_scaled, 1)
                    pool.wait_ge(v_scaled, t + 1)
                    chain.step()
                    pool.wait_ge(z_summed, t * 2 + 2)
                    z4 = zs.rearrange("r (e p k n) -> r e p k n", e=2, p=HP, k=2)
                    r4 = z_rec.rearrange("r (e p k) -> r e p k", e=2, p=HP)
                    pool.tensor_tensor(prob[:, 0:1024].rearrange("r (p e n) -> r e p n", e=2, n=CH), z4[:, :, :, 0, :],
                                       r4[:, :, :, 0].unsqueeze(3).to_broadcast([P, 2, HP, CH]), ALU.mult).then_inc(pq_norm, 1)
                    pool.wait_ge(ktok_out, t + 1)
                    b3 = k_tok.rearrange("r (h d) -> r h d", d=D)
                    pool.tensor_tensor(b3, b3, lr[:, ds(t * 32, H)].unsqueeze(2).to_broadcast([P, H, D]),
                                       ALU.mult).then_inc(k_scaled, 1)
                    pool.wait_ge(y_scaled, t + 2)
                    pool.tensor_tensor(x_sb[:, ds(t * C, C)], x_sb[:, ds(t * C, C)], y_gated, ALU.add).then_inc(x_added, 1)
            chain.leave(T)
            finish(pool, 7)

            add_shift(1, 3, SB)
            finish(pool, 8)
            pool.wait_ge(h_stored, 128)
            def fetch_rows(e, u):
                pool.wait_ge(x_turned, e + (TILES0 // GRP + 1))
                for t in range(2):
                    pool.tensor_copy(idx_st[2 * u + t], ids_i[:, ds(e + E * t, 1)]).then_inc(idx_copied, 1)
                pool.wait_ge(idx_copied, e * 2 + (n0 + 2))
                apart(pool)
                for t in range(2):
                    pool.indirect_dma_start(gx1[u][:, t * C:(t + 1) * C], None, h_dram[1][:, :],
                                            bass.IndirectOffsetOnAxis(ap=idx_st[2 * u + t], axis=0),
                                            bounds_check=B * L - 1, oob_is_err=False).then_inc(gathered[u], 16)

            def scatter_rows(e, u, fetch, first=False):
                for t in range(2):
                    pool.tensor_copy(idx_st[4 + 2 * u + t], ids_i[:, ds(e + (2 * E + E * t), 1)]).then_inc(y_idx_copied, 1)
                pool.wait_ge(y_idx_copied, e * 2 + 2)
                pool.wait_ge(o_ready, e + (TILES0 + 1))
                for t in range(2):
                    if t:
                        if fetch:
                            fetch_rows(e + 3, 1 - u)
                        pool.wait_ge(y_scattered, e * 32 + 16)
                    elif not first:
                        pool.wait_ge(y_scattered, e * 32)
                        pool.sem_inc(o1_free, 1)
                    apart(pool)
                    pool.indirect_dma_start(y_dram[:, :], bass.IndirectOffsetOnAxis(ap=idx_st[4 + 2 * u + t], axis=0),
                                            o1_st[u][:, t * C:(t + 1) * C], None,
                                            bounds_check=P + 2 * B * L - 1, oob_is_err=False).then_inc(y_scattered, 16)

            for u in range(2):
                fetch_rows(u, u)
            pool.sem_inc(o1_free, 2)
            fetch_rows(2, 0)
            pool.wait_ge(y_zeroed, 32 * BP)
            scatter_rows(0, 0, True, first=True)
            with pool.Fori(0, E // 2 - 2) as i:
                for e, u in ((i * 2 + 1, 1), (i * 2 + 2, 0)):
                    scatter_rows(e, u, True)
            for e in range(E - 3, E):
                scatter_rows(e, e % 2, False)
            n0 += 2 * E
            pool.wait_ge(y_scattered, 32 * E)
            finish(pool, 9)
            with pool.Fori(0, BP) as bp:
                pool.wait_ge(y_sum, bp + 1)
                pool.tensor_tensor(tiles(x_sb, bp), tiles(x_sb, bp), tiles(back1, bp * 2), ALU.add).then_inc(x_final, 1)
            finish(pool, 10)

        @block.scalar
        def _(act):
            act.wait_ge(c_in, 32)
            act.activation(cth, ct, ACT.Tanh, scale=0.5).then_inc(cond_tanh, 1)

            def modulations_out(l):
                for bp in range(BP):
                    n = BP * l + bp
                    act.wait_ge(mod_mm, n + 1)
                    act.activation(mod[l][:, bp * 6 * C:(bp + 1) * 6 * C], ps[n % 4][:, 0:6 * C],
                                   ACT.Copy).then_inc(mod_out, 1)

            modulations_out(0)
            act.wait_ge(a0_in, 16 * 9)
            act.activation(dt_terms[:, 0:1], dt2, ACT.Exp, scale=-1.0).then_inc(a0_exp, 1)
            act.wait_ge(a0_par, 1)
            act.activation(decay, dt_terms[:, 3:4], ACT.Exp, scale=-1.0).then_inc(a0_exp, 1)
            modulations_out(1)
            finish(act, 1)

            def normalise(k):
                act.wait_ge(ln_var, LN_ONCE[k] + 1)
                act.activation(rstd, var, ACT.Sqrt, bias=ln_eps, scale=1.0 / C).then_inc(ln_std, 1)
                act.wait_ge(ln_rates, LN_ONCE[k] + 1)
                with act.Fori(0, BP) as bp:
                    for t in range(ACT_TILES):
                        last = act.activation(xc[:, ds(bp * W8 + t * C, C)], x_sb[:, ds(bp * W8 + t * C, C)], ACT.Identity,
                                              scale=rstd[:, ds(bp * NC + t, 1)], bias=sums[:, ds(bp * NC + t, 1)])
                    last.then_inc(ln_normed, 1)

            normalise(0)

            def square(bp):
                act.wait_ge(h_ready, bp + 1)
                act.activation(tiles(sq, bp), tiles(xc, bp), ACT.Square).then_inc(a0_sq, 1)

            def spread_states(bp):
                u = bp % 2
                act.wait_ge(a0_scan, bp + 1)
                if bp >= 2:
                    act.wait_ge(a0_y, bp - 1)
                for be in range(2):
                    half = slice(be * S, be * S + S)
                    last = act.activation(xs[u][half, :].rearrange("r (t e n) -> r t e n", e=2, n=CH)[:, :, be, :],
                                          states[u][half, :].rearrange("r (t n) -> r t n", n=CH), ACT.Copy)
                last.then_inc(a0_spread, 1)

            square(0)
            for bp in range(BP):
                act.wait_ge(a0_sum, bp + 1)
                act.activation(spread[:, bp * NC:(bp + 1) * NC], spread[:, bp * NC:(bp + 1) * NC], ACT.Sqrt, bias=rms_eps,
                               scale=1.0 / C).then_inc(a0_rms, 1)
                if bp + 1 < BP:
                    square(bp + 1)
                act.wait_ge(h_turned, bp + 1)
                act.activation(hT[:, bp * W8:(bp + 1) * W8].rearrange("c (e t n) -> c t e n", e=2, n=CH),
                               ps[bp % 2][:, :].rearrange("c (t e n) -> c t e n", e=2, n=CH), ACT.Copy).then_inc(hT_ready, 1)
                if bp:
                    spread_states(bp - 1)
            spread_states(BP - 1)
            finish(act, 2)

            def out_of_turn(k):
                with act.Fori(0, 2) as i:
                    for u in range(2):
                        bp = i * 2 + u
                        act.wait_ge(h_turned, bp + (4 * k + 1))
                        act.activation(hT[:, ds(bp * W8, W8)], ps[u][:, :], ACT.Copy).then_inc(hT_ready, 1)

            act.wait_ge(gw, 33)
            act.activation(wg_n[0:E, 0:1], wg_t[0:E, 0:1], ACT.Sqrt).then_inc(gw, 1)
            normalise(1)
            out_of_turn(1)
            finish(act, 3)
            act.wait_ge(oh_done, 1)
            act.activation(e_exp, shifted, ACT.Exp).then_inc(ex_done, 1)
            finish(act, 4)
            with act.Fori(0, TILES0 // GRP // 2) as i:
                for u in range(2):
                    act.wait_ge(hb_ready, i * (2 * GRP) + (u + 1) * GRP)
                    act.activation(hb, hb, ACT.Gelu).then_inc(hg_ready, 1)
            finish(act, 5)

            def rate_tanh(n):
                act.wait_ge(rt_mm, n + 1)
                if n >= 2:
                    act.wait_ge(rt_sum, n - 1)
                act.activation(tg[n % 2][0:32, :], ps[3][0:32, n % 2 * 512:(n % 2 + 1) * 512], ACT.Tanh, scale=0.5
                               ).then_inc(rt_tanh, 1)

            def turned_out(bp):
                act.wait_ge(h_turned, 2 * BP + bp + 1)
                act.activation(hT[:, bp * W8:(bp + 1) * W8], ps[bp % 2][:, :], ACT.Copy).then_inc(hT_ready, 1)

            def rates(bp):
                for n in (2 * bp, 2 * bp + 1):
                    rate_tanh(n)
                act.wait_ge(rt_tok, bp + 1)
                act.activation(t_tok[:, bp * 256:(bp + 1) * 256], ps[2][:, bp % 2 * 512:bp % 2 * 512 + 256], ACT.Tanh, scale=0.5
                               ).then_inc(rt_tok_tanh, 1)

            for bp in range(BP):
                act.wait_ge(ln_var, LN_ONCE[2] + bp + 1)
                now = slice(bp * NC, (bp + 1) * NC)
                act.activation(rstd[:, now], var[:, now], ACT.Sqrt, bias=ln_eps, scale=1.0 / C).then_inc(ln_std, 1)
                if bp:
                    turned_out(bp - 1)
                act.wait_ge(ln_rates, LN_ONCE[2] + bp + 1)
                for t in range(bp * NC, (bp + 1) * NC):
                    last = act.activation(xc[:, t * C:(t + 1) * C], x_sb[:, t * C:(t + 1) * C], ACT.Identity,
                                          scale=rstd[:, t:t + 1], bias=sums[:, t:t + 1])
                last.then_inc(ln_normed, 1)
                if bp:
                    rates(bp - 1)
            turned_out(BP - 1)
            rates(BP - 1)
            finish(act, 6)

            act.wait_ge(pe_pv, 1)
            act.activation(vT, ps[0][:, :], ACT.Copy).then_inc(vT_out, 1)
            act.wait_ge(pe_pq, 1)
            act.activation(th[0], ps[1][:, :], ACT.Tanh, scale=0.5).then_inc(tanh_out, 1)
            act.wait_ge(pe_pk, 1)
            act.activation(th[1], ps[2][:, :], ACT.Tanh, scale=0.5).then_inc(tanh_out, 1)
            with act.Fori(0, BP) as bp:
                act.wait_ge(win_new, bp * (2 * NC) + 2)
                act.activation(w_in[:, 0:1024], w_init[:, 0:1024], ACT.Copy).then_inc(win_set, 1)
                act.wait_ge(wout_new, bp * (2 * NC) + 2)
                for be in range(2):
                    act.activation(w_out[:, be * 1024:(be + 1) * 1024], w_init[:, 1024:2048], ACT.Copy).then_inc(wout_set, 1)
                with act.Fori(0, NC) as c:
                    t = bp * NC + c

                    def exponentials(be):
                        z = zs[:, be * 1024:(be + 1) * 1024]
                        act.wait_ge(z_centered, t * 2 + (be + 1))
                        act.activation(z, z, ACT.Exp, scale=0.5).then_inc(z_exp, 1)

                    exponentials(0)
                    for be, bank in ((0, 3), (1, 2)):
                        act.wait_ge(pe_wt, t * 2 + (be + 1))
                        act.activation(w_outT[:, be * 1024:(be + 1) * 1024], ps[bank][:, :], ACT.Copy).then_inc(woutT_out, 1)
                    exponentials(1)
                    act.wait_ge(pe_vt, t + 1)
                    act.activation(v_tok, ps[3][:, :], ACT.Copy).then_inc(vtok_out, 1)
                    act.wait_ge(pe_pq, t + 2)
                    act.activation(th[0], ps[1][:, :], ACT.Tanh, scale=0.5).then_inc(tanh_out, 1)
                    act.wait_ge(pe_pv, t + 2)
                    act.wait_ge(pe_a, t + 1)
                    act.activation(vT, ps[0][:, :], ACT.Copy).then_inc(vT_out, 1)
                    act.wait_ge(pe_pt, t + 1)
                    act.activation(p_tok, ps[3][:, :], ACT.Copy).then_inc(ptok_out, 1)
                    act.wait_ge(pe_pk, t + 2)
                    act.activation(th[1], ps[0][:, :], ACT.Tanh, scale=0.5).then_inc(tanh_out, 1)
                    act.wait_ge(pe_kt, t + 1)
                    act.activation(k_tok, ps[3][:, :], ACT.Copy).then_inc(ktok_out, 1)
                    act.wait_ge(pe_o, t + 1)
                    act.activation(oT, ps[1][:, :], ACT.Copy).then_inc(oT_out, 1)
            finish(act, 7)

            normalise(3)
            out_of_turn(3)
            act.wait_ge(oh_done, 2)
            act.activation(pr1, sh1, ACT.Exp).then_inc(ex_done, 1)
            finish(act, 8)
            g0 = TILES0 // GRP
            act.wait_ge(f1_b, 48)
            with act.Fori(0, E // 2) as i:
                for u in range(2):
                    e = i * 2 + u
                    act.wait_ge(h_mm, e + (TILES0 + 1))
                    for j in range(4):
                        last = act.activation(hg1[u][:, j * 256:(j + 1) * 256], ps[1 + u][:, j * 256:(j + 1) * 256],
                                              ACT.Gelu_apprx_tanh, bias=b1t[:, ds(e * 4 + j, 1)])
                    last.then_inc(hg_ready, 1)
            finish(act, 9)
            for bp in range(BP):
                act.wait_ge(y_in[bp], 32)
                for t in range(NC):
                    at = (2 * bp + 1) * W8 + t * C
                    last = act.activation(back1[:, at:at + C], back1[:, at:at + C], ACT.Copy,
                                          scale=wk[:, T + bp * NC + t:T + bp * NC + t + 1])
                last.then_inc(y_second, 1)
            finish(act, 10)

        @block.vector
        def _(dve):
            chain = Chain(dve, dve_step)
            dve.wait_ge(cond_tanh, 1)
            chain.link(dve.scalar_tensor_tensor(cth, cth, 1.0, ct, ALU.add, ALU.mult))
            for l in range(2):
                dve.tensor_scalar(st[l].rearrange("k (b n) -> k b n", n=CH),
                                  cth[:, 8 * l:8 * l + 8].unsqueeze(2).to_broadcast([P, B, CH]), 0.5, None, ALU.mult
                                  ).then_inc(cond_spread, 1)

            def statistics():
                with dve.Fori(0, BP) as bp:
                    for t in range(NC):
                        last = dve.bn_stats(stats[:, ds(bp * (NC * 6) + t * 6, 6)], x_sb[:, ds(bp * W8 + t * C, C)])
                    last.then_inc(stats_done, 1)

            dve.wait_ge(x_in, 16 * B)
            statistics()
            dve.wait_ge(a0_exp, 1)
            chain.link(dve.tensor_scalar(dt_terms[:, 1:2], dt_terms[:, 0:1], 1.0, None, ALU.add))
            chain.link(dve.reciprocal(dts, dt_terms[:, 1:2]))
            chain.link(dve.scalar_tensor_tensor(dt_terms[:, 2:3], a2, -1.0, a2, ALU.mult, ALU.max))
            dve.tensor_tensor(dt_terms[:, 3:4], dt_terms[:, 2:3], dts, ALU.mult).then_inc(a0_par, 1)
            chain.link(dve.tensor_scalar(nb, bmat, normw, None, ALU.mult))
            dve.wait_ge(a0_exp, 2)
            chain.link(dve.tensor_copy(a_bc, decay.to_broadcast([P, L])))
            chain.link(dve.tensor_scalar(cmat, cmat, dts, None, ALU.mult))

            def hold_gates(l):
                dve.wait_ge(mod_out, BP * (l + 1))
                m = mod[l][:, :].rearrange("p (b j c) -> p b j c", j=6, c=C)
                t3, t4 = (xc[:, n * BP * C:(n + 1) * BP * C].rearrange("p (b c) -> p b c", c=C) for n in range(2))
                for j in (CA, CB):
                    chain.link(dve.tensor_scalar(m[:, :, j, :], m[:, :, j, :], 1.0, None, ALU.add))
                for j in (GA, GB):
                    g = m[:, :, j, :]
                    chain.link(dve.tensor_scalar(t3, g, 0.0, 2.0, ALU.is_ge, ALU.mult))
                    chain.link(dve.scalar_tensor_tensor(t4, g, -1.0, g, ALU.mult, ALU.max))
                    chain.link(dve.tensor_scalar(t4, t4, 0.25, None, ALU.max))
                    chain.link(dve.scalar_tensor_tensor(g, t3, -1.0, t4, ALU.add, ALU.mult))

            hold_gates(0)
            finish(dve, 1)

            def rate_sum(n):
                dve.wait_ge(rt_tanh, n + 1)
                dve.tensor_reduce(rate_sums[0:32, n * 8:(n + 1) * 8], tg[n % 2][0:32, :].rearrange("r (g n) -> r g n", n=CH),
                                  AX_X, ALU.add).then_inc(rt_sum, 1)

            def normalising(k, bp, a, b, meanwhile=()):
                s3 = stats.rearrange("p (t s) -> p s t", s=6)[:, :, a:b]
                total, diff, both = sums[:, a:b], spread[:, T + a:T + b], spread[:, 2 * T + a:2 * T + b]
                dve.tensor_tensor(total, s3[:, 1, :], s3[:, 4, :], ALU.add)
                dve.tensor_tensor(both, s3[:, 2, :], s3[:, 5, :], ALU.add)
                chain.link(dve.tensor_tensor(diff, s3[:, 1, :], s3[:, 4, :], ALU.subtract))
                chain.link(dve.tensor_tensor(diff, diff, diff, ALU.mult))
                dve.scalar_tensor_tensor(var[:, a:b], diff, C / 4.0, both, ALU.mult, ALU.add).then_inc(ln_var, 1)
                for n in meanwhile:
                    rate_sum(n)
                dve.wait_ge(ln_std, LN_ONCE[k] + bp + 1)
                chain.link(dve.reciprocal(rstd[:, a:b], rstd[:, a:b]))
                dve.scalar_tensor_tensor(total, total, -0.5, rstd[:, a:b], ALU.mult, ALU.mult).then_inc(ln_rates, 1)
                dve.wait_ge(ln_rates, LN_ONCE[k] + bp + 1)

            def layer_norm(l, k, j):
                if k:
                    statistics()
                dve.wait_ge(stats_done, BP * (min(k, 2) + 1))
                normalising(k, 0, 0, T)
                with dve.Fori(0, BP) as bp:
                    chain.enter(bp, 1)
                    for t in range(ACT_TILES, NC):
                        last = dve.tensor_scalar(xc[:, ds(bp * W8 + t * C, C)], x_sb[:, ds(bp * W8 + t * C, C)],
                                                 rstd[:, ds(bp * NC + t, 1)], sums[:, ds(bp * NC + t, 1)], ALU.mult, ALU.add)
                    chain.link(last)
                    dve.wait_ge(ln_normed, bp + (4 * k + 1))
                    dve.tensor_tensor(tiles(xc, bp), tiles(xc, bp), over_tiles(mod_of(l, bp, j)), ALU.mult
                                      ).then_inc(ln_scaled, 1)
                chain.leave(BP)

            layer_norm(0, 0, CA)

            def sum_squares(bp):
                dve.wait_ge(a0_sq, bp + 1)
                dve.tensor_reduce(spread[:, bp * NC:(bp + 1) * NC], tiles(sq, bp), AX_X, ALU.add).then_inc(a0_sum, 1)

            def rms_norm(bp):
                rec = spread[:, bp * NC:(bp + 1) * NC]
                dve.wait_ge(a0_rms, bp + 1)
                dve.reciprocal(rec, rec).then_inc(a0_rec, 1)
                dve.wait_ge(a0_rec, bp + 1)
                dve.tensor_tensor(tiles(xc, bp), tiles(xc, bp), rec.unsqueeze(2).to_broadcast([P, NC, C]), ALU.mult
                                  ).then_inc(a0_normed, 1)

            def scan(bp):
                u = bp % 2
                dve.wait_ge(a0_up, bp + 1)
                if bp >= 2:
                    dve.wait_ge(a0_spread, bp - 1)
                dve.tensor_tensor_scan(states[u], a_bc, ps[2][:, u * L:(u + 1) * L], 0.0, ALU.mult, ALU.add).then_inc(a0_scan, 1)

            def gate(bp):
                u = bp % 2
                dve.wait_ge(a0_y, bp + 1)
                if bp >= 2:
                    dve.wait_ge(a0_added, bp - 1)
                dve.tensor_tensor(yg[u].rearrange("p (t c) -> p t c", c=C), ps[3][:, :].rearrange("p (t c) -> p t c", c=C),
                                  over_tiles(mod_of(0, bp, GA)), ALU.mult).then_inc(a0_gated, 1)

            for bp in range(BP):
                sum_squares(bp)
                rms_norm(bp)
                if bp >= 2:
                    gate(bp - 2)
                if bp:
                    scan(bp - 1)
            gate(BP - 2)
            scan(BP - 1)
            gate(BP - 1)
            finish(dve, 2)

            def logits_out(f, dst):
                dve.wait_ge(lg_mm, f + 1)
                dve.tensor_copy(dst, ps[2][:, 0:T * E]).then_inc(lg_out, 1)

            te = lambda ap: ap.rearrange("p (t e) -> p t e", e=E)
            over_e = lambda ap: ap.unsqueeze(2).to_broadcast([P, ap.shape[1], E])
            over_t = lambda ap, n=T: ap.unsqueeze(1).to_broadcast([P, n, ap.shape[1]])

            dve.wait_ge(gw, 32)
            chain.link(dve.tensor_tensor(wg_n[0:E, :], wg_s[0:E, :], wg_s[0:E, :], ALU.mult))
            dve.tensor_reduce(wg_t[0:E, 0:1], wg_n[0:E, :], AX_X, ALU.add).then_inc(gw, 1)
            dve.wait_ge(gw, 34)
            chain.link(dve.tensor_scalar(wg_t[0:E, 1:2], wg_n[0:E, 0:1], 1e-4, None, ALU.max))
            chain.link(dve.reciprocal(wg_t[0:E, 2:3], wg_t[0:E, 1:2]))
            dve.tensor_scalar(wg_n[0:E, :], wg_s[0:E, :], wg_t[0:E, 2:3], None, ALU.mult).then_inc(gw, 1)
            dve.wait_ge(gw, 36)
            dve.tensor_copy(wg_t[0:16, :], ps[3][0:16, 0:E]).then_inc(gw, 1)
            dve.wait_ge(gw, 38)
            dve.tensor_copy(w_gate, ps[3][:, 512:512 + E]).then_inc(gw, 1)
            layer_norm(0, 1, CB)
            logits_out(0, logits)
            finish(dve, 3)
            chain.link(dve.tensor_reduce(mx, te(logits), AX_X, ALU.max))
            chain.link(dve.tensor_tensor(te(shifted), te(logits), over_e(mx), ALU.subtract))
            chain.link(dve.scalar_tensor_tensor(te(pick), te(shifted), 0.0, over_t(first_w), ALU.is_equal, ALU.mult))
            dve.tensor_reduce(m2, te(pick), AX_X, ALU.max).then_inc(oh_done, 1)
            dve.wait_ge(oh_done, 1)
            chain.link(dve.tensor_tensor(te(onehot), te(pick), over_e(m2), ALU.is_equal))
            dve.tensor_copy(onehot_b, onehot).then_inc(rhs_ready, 1)
            dve.wait_ge(ex_done, 1)
            chain.link(dve.tensor_reduce(e_sum, te(e_exp), AX_X, ALU.add))
            chain.link(dve.reciprocal(score, e_sum))
            dve.wait_ge(cnt_done, 1)
            before_p, totals = ps[3][:, 0:256], ps[3][:, 512:768]
            for e in range(E):
                last = dve.tensor_tensor_scan(te(cum)[:, :, e], ones_f[:, 0:T], te(totals)[:, :, e], 0.0, ALU.mult, ALU.add)
            chain.link(last)
            chain.link(dve.tensor_tensor(rank, cum, totals, ALU.subtract))
            chain.link(dve.tensor_tensor(rank, rank, before_p, ALU.add))
            cnt = te(cum)[:, T - 1, :]
            c3 = n_cmp[:, 0:E * T].rearrange("p (e t) -> p e t", t=T)
            chain.link(dve.tensor_tensor(c3, cnt.unsqueeze(2).to_broadcast([P, E, T]), over_t(edges, E), ALU.is_gt))
            chain.link(dve.tensor_reduce(n_tiles[:, 0:E], c3, AX_X, ALU.add))
            chain.link(dve.tensor_tensor_scan(t_end[:, 0:E], ones_f[:, 0:E], n_tiles[:, 0:E], 0.0, ALU.mult, ALU.add))
            chain.link(dve.tensor_tensor(t_start[:, 0:E], t_end[:, 0:E], n_tiles[:, 0:E], ALU.subtract))
            chain.link(dve.tensor_scalar(t_start[:, 0:E], t_start[:, 0:E], float(P), None, ALU.mult))
            chain.link(dve.tensor_tensor(te(rank), te(rank), over_t(t_start[:, 0:E]), ALU.add))
            chain.link(dve.tensor_tensor(rank, rank, onehot, ALU.mult))
            chain.link(dve.tensor_reduce(slot_f, te(rank), AX_X, ALU.add))
            chain.link(dve.tensor_copy(slot_i[:, 0:T], slot_f))
            chain.link(dve.tensor_scalar(tile_i, slot_i[:, 0:T], 7, None, ALU.arith_shift_right))
            chain.link(dve.tensor_copy(tile_f, tile_i))
            chain.link(dve.scalar_tensor_tensor(row_f, tile_f, -float(P), slot_f, ALU.mult, ALU.add))
            c3 = n_cmp.rearrange("p (t e) -> p t e", e=E)
            chain.link(dve.tensor_tensor(c3, iota_t.unsqueeze(2).to_broadcast([P, 40, E]), over_t(t_end[:, 0:E], 40), ALU.is_ge))
            chain.link(dve.tensor_reduce(t_exp_f, c3, AX_X, ALU.add))
            chain.link(dve.tensor_scalar(t_exp_f, t_exp_f, float(E - 1), None, ALU.min))
            g4 = t_exp_f.rearrange("p (g t) -> p t g", t=GRP)
            packed = g4[:, GRP - 1, :]
            for t in range(GRP - 2, -1, -1):
                chain.link(dve.scalar_tensor_tensor(packed, packed, float(E), g4[:, t, :], ALU.mult, ALU.add))
            chain.link(dve.tensor_copy(t_exp_i[:, 0:TILES0 // GRP], packed))
            dve.wait_ge(h_stored, 64)
            t3 = tile_hot.rearrange("p (t s) -> p t s", s=40)
            r3 = t_rhs.rearrange("p (t k s) -> p t k s", k=2, s=40)
            chain.link(dve.tensor_tensor(t3, over_t(iota_t), tile_f.unsqueeze(2).to_broadcast([P, T, 40]), ALU.is_equal))
            dve.tensor_tensor(r3[:, :, 0, :], t3, tile_no.unsqueeze(2).to_broadcast([P, T, 40]), ALU.mult)
            dve.tensor_scalar(r3[:, :, 1, :], t3, part_no, None, ALU.mult).then_inc(rhs_ready, 1)
            with dve.Fori(0, T // 8) as i:
                dve.tensor_tensor(r_hot[:, ds(i * (8 * P), 8 * P)].rearrange("p (t s) -> p t s", s=P), over_t(iota_b[:, 0:P], 8),
                                  row_f[:, ds(i * 8, 8)].unsqueeze(2).to_broadcast([P, 8, P]), ALU.is_equal).then_inc(hot_made, 1)
            dve.wait_ge(ids_mm, 1)
            chain.link(dve.tensor_copy(id_f, ps[2][:, 0:80]))
            chain.link(dve.scalar_tensor_tensor(id_f[:, 0:40], id_f[:, 0:40], float(P), id_f[:, 40:80], ALU.mult, ALU.add))
            chain.link(dve.tensor_copy(ids_i, id_f[:, 0:40]))
            finish(dve, 4)
            dve.wait_ge(f0_w, 64)

            def add_bias1(g):
                of = experts_of(dve, g)
                for t, e in enumerate(of):
                    dve.wait_ge(h_mm, g * GRP + (t // 2 * 2 + 2))
                    dve.tensor_tensor(hb[:, t * F0:(t + 1) * F0], ps[1][:, t * F0:(t + 1) * F0], b1a[:, ds(e * F0, F0)],
                                      ALU.add).then_inc(hb_ready, 1)

            def turned_out(g):
                dve.wait_ge(hg_turned, g + 1)
                dve.tensor_copy(hgT, ps[2][:, :]).then_inc(hgT_ready, 1)

            def add_bias2(g, u, n):
                of = experts_of(dve, g)
                dve.wait_ge(o_stored[u], n * 16 + 16)
                dve.wait_ge(o_mm, g * GRP + GRP)
                for t, e in enumerate(of):
                    dve.tensor_tensor(o_st[u][:, t * C:(t + 1) * C], ps[3][:, t * C:(t + 1) * C], b2a[:, ds(e * C, C)],
                                      ALU.add).then_inc(o_ready, 1)

            def rows_out(g):
                dve.wait_ge(x_turned, g + 3)
                dve.tensor_copy(xg, ps[0][:, 0:GRP * C]).then_inc(xg_ready, 1)

            last = TILES0 // GRP - 1
            rows_out(0)
            add_bias1(0)
            with dve.Fori(0, (last - 1) // 2) as i:
                for g, u, n in ((i * 2 + 1, 0, i), (i * 2 + 2, 1, i)):
                    rows_out(g)
                    turned_out(g - 1)
                    add_bias1(g)
                    add_bias2(g - 1, u, n)
            rows_out(last)
            turned_out(last - 1)
            add_bias1(last)
            add_bias2(last - 1, 0, last // 2)
            turned_out(last)
            add_bias2(last, 1, last // 2)
            finish(dve, 5)

            hold_gates(1)

            chain.link(dve.tensor_copy(own_f, own_ones))
            chain.link(dve.tensor_reduce(rate_pair[0:32, :], rate_row[0:32, :].rearrange("r (q h) -> r q h", h=2), AX_X, ALU.add))
            chain.link(dve.tensor_reduce(rate_sums[0:32, 0:2], rate_row[0:32, :].rearrange("r (q h) -> r h q", h=2), AX_X, ALU.add))
            chain.link(dve.tensor_copy(parity[0:32, :].rearrange("r (h m) -> r h m", h=2),
                                       rate_sums[0:32, 0:2].unsqueeze(2).to_broadcast([32, 2, D])))

            def scale_and_shift(bp):
                dve.wait_ge(ln_normed, 2 * BP + bp + 1)
                chain.link(dve.tensor_tensor(tiles(xc, bp), tiles(xc, bp), over_tiles(mod_of(1, bp, CA)), ALU.mult))
                dve.tensor_tensor(tiles(xc, bp), tiles(xc, bp), over_tiles(mod_of(1, bp, SA)), ALU.add).then_inc(h_ready, 1)

            for bp in range(BP):
                b3 = back[bp % 2].rearrange("p (t c) -> p t c", c=C)
                dve.wait_ge(back_in[bp % 2], bp // 2 * 128 + 128)
                chain.link(dve.tensor_tensor(b3, b3, score[:, bp * NC:(bp + 1) * NC].unsqueeze(2).to_broadcast([P, NC, C]), ALU.mult))
                chain.link(dve.tensor_tensor(b3, b3, over_tiles(mod_of(0, bp, GB)), ALU.mult))
                dve.tensor_tensor(tiles(x_sb, bp), tiles(x_sb, bp), b3, ALU.add).then_inc(back_used, 1)
                if bp:
                    scale_and_shift(bp - 1)
                dve.wait_ge(back_used, bp + 3)
                for t in range(bp * NC, (bp + 1) * NC):
                    last = dve.bn_stats(stats[:, t * 6:(t + 1) * 6], x_sb[:, t * C:(t + 1) * C])
                chain.link(last)
                normalising(2, bp, bp * NC, (bp + 1) * NC, (2 * bp - 4, 2 * bp - 3) if bp >= 2 else ())
            scale_and_shift(BP - 1)
            for n in range(2 * BP - 4, 2 * BP):
                rate_sum(n)
            dve.wait_ge(rt_sum, 8)
            dve.tensor_tensor(rate_diag[0:32, :].rearrange("r (q g) -> r q g", g=64),
                              rate_sums[0:32, :].unsqueeze(1).to_broadcast([32, 16, 64]),
                              rate_pair[0:32, :].unsqueeze(2).to_broadcast([32, 16, 64]), ALU.mult).then_inc(rt_spread, 1)
            dve.wait_ge(rt_wd, 1)
            for k in range(2):
                dve.tensor_scalar(wd.rearrange("r (g k p) -> r k p g", k=2, p=HP)[:, k],
                                  ps[2][:, k * 512:(k + 1) * 512].rearrange("r (p g) -> r p g", p=HP),
                                  BASE_WD * 0.5 / CH, BASE_WD * 0.5, ALU.mult, ALU.add)
            dve.wait_ge(rt_lr, 1)
            for k in range(2):
                f = BASE_LR * (0.25, 0.5)[k]
                dve.tensor_scalar(lr.rearrange("r (t k h) -> r k t h", k=2, h=H)[:, k],
                                  ps[0][:, :].rearrange("r (t k h) -> r k t h", k=2, h=H)[:, k],
                                  f / CH, f, ALU.mult, ALU.add)
            finish(dve, 6)

            for j, bank in ((0, 1), (1, 2)):
                dve.wait_ge(tanh_out, j + 1)
                dve.scalar_tensor_tensor(qk[:, j * 1024:(j + 1) * 1024], th[j], 1.0, ps[bank][:, :],
                                         ALU.add, ALU.mult).then_inc(silu_done, 1)
            with dve.Fori(0, BP) as bp:
                dve.wait_ge(win_new, bp * (2 * NC) + 2)
                dve.tensor_copy(w_in[:, 1024:2048], w_init[:, 0:1024]).then_inc(win_set, 1)
                with dve.Fori(0, NC) as c:
                    t = bp * NC + c
                    chain.enter(t, 6)
                    for be in range(2):
                        g = slice(16 * be, 16 * be + 16)
                        z3 = zs[:, be * 1024:(be + 1) * 1024].rearrange("r (g n) -> r g n", n=CH)
                        p3 = ps[be][:, :].rearrange("r (g n) -> r g n", n=CH)
                        dve.wait_ge(pe_z, t * 2 + (be + 1))
                        chain.link(dve.tensor_reduce(z_max[:, g], p3, AX_X, ALU.max))
                        dve.tensor_tensor(z3, p3, z_max[:, g].unsqueeze(2).to_broadcast([P, 16, CH]), ALU.subtract
                                          ).then_inc(z_centered, 1)
                    for be in range(2):
                        g = slice(16 * be, 16 * be + 16)
                        dve.wait_ge(z_exp, t * 2 + (be + 1))
                        chain.link(dve.tensor_reduce(z_sum[:, g], zs[:, be * 1024:(be + 1) * 1024].rearrange(
                            "r (g n) -> r g n", n=CH), AX_X, ALU.add))
                        dve.reciprocal(z_rec[:, g], z_sum[:, g]).then_inc(z_summed, 1)
                    dve.wait_ge(z_summed, t * 2 + 2)
                    z4 = zs.rearrange("r (e p k n) -> r e p k n", e=2, p=HP, k=2)
                    r4 = z_rec.rearrange("r (e p k) -> r e p k", e=2, p=HP)
                    dve.tensor_tensor(prob[:, 1024:2048].rearrange("r (p e n) -> r e p n", e=2, n=CH), z4[:, :, :, 1, :],
                                      r4[:, :, :, 1].unsqueeze(3).to_broadcast([P, 2, HP, CH]), ALU.mult).then_inc(pk_norm, 1)

                    def silu_next(j, bank):
                        dve.wait_ge(tanh_out, t * 2 + (j + 3))
                        dve.scalar_tensor_tensor(qk[:, j * 1024:(j + 1) * 1024], th[j], 1.0, ps[bank][:, :],
                                                 ALU.add, ALU.mult).then_inc(silu_done, 1)

                    silu_next(0, 1)
                    h3 = lambda ap: ap.rearrange("r (h d) -> r h d", d=D)
                    dve.wait_ge(pe_a, t + 1)
                    dve.wait_ge(ptok_out, t + 1)
                    dve.wait_ge(v_scaled, t + 1)
                    chain.link(dve.tensor_tensor(pa, p_tok, ps[2][:, :], ALU.mult))
                    chain.link(dve.tensor_reduce(s_sum, h3(pa), AX_X, ALU.add))
                    dve.tensor_tensor(h3(pa), h3(ps[2][:, :]), s_sum.unsqueeze(2).to_broadcast([P, H, D]), ALU.subtract
                                      ).then_inc(difference_made, 1)
                    dve.wait_ge(pe_kt, t + 1)
                    silu_next(1, 0)
                    dve.wait_ge(difference_made, t + 1)
                    for be in range(2):
                        half = slice(be * CH, be * CH + CH)
                        last = dve.tensor_tensor(g_pad[half, :].rearrange("r (h e d) -> r h e d", e=2, d=D)[:, :, be, :],
                                                 h3(pa[half, :]), h3(p_tok[half, :]), ALU.mult)
                    last.then_inc(g_done, 1)

                    def update(w, k, be, bank, done):
                        for h in range(2):
                            half = slice(h * D, h * D + D)
                            last = dve.tensor_tensor(
                                w[half, be * 1024:(be + 1) * 1024].rearrange("r (p c) -> r p c", c=P)[:, :, half],
                                w_dec[half, (2 * k + be) * 1024:(2 * k + be + 1) * 1024].rearrange("r (p c) -> r p c", c=P)[:, :, half],
                                ps[bank][half, :].rearrange("r (p e c) -> r p e c", e=2, c=D)[:, :, be, :], ALU.add)
                        last.then_inc(done, 1)

                    dve.wait_ge(pe_gout, t + 1)
                    for be in range(2):
                        dve.wait_ge(dec_done, t * 2 + (be + 1))
                        update(w_out, 1, be, 0, wout_new)
                    dve.wait_ge(pe_gin, t + 1)
                    for be in range(2):
                        update(w_in, 0, be, 2, win_new)
                    dve.wait_ge(pe_y, t + 1)
                    dve.wait_ge(x_added, t + 1)
                    dve.tensor_tensor(y_gated, ps[1][:, 0:C], mod_of(1, bp, GA), ALU.mult).then_inc(y_scaled, 1)
            chain.leave(T)
            finish(dve, 7)

            layer_norm(1, 3, CB)
            logits_out(1, lg1)
            dve.wait_ge(lg_out, 2)
            chain.link(dve.tensor_reduce(mx, te(lg1), AX_X, ALU.max))
            dve.tensor_tensor(te(sh1), te(lg1), over_e(mx), ALU.subtract).then_inc(oh_done, 1)
            dve.wait_ge(ex_done, 2)
            chain.link(dve.tensor_reduce(e_sum, te(pr1), AX_X, ALU.add))
            chain.link(dve.reciprocal(e_sum, e_sum))
            chain.link(dve.tensor_tensor(te(pr1), te(pr1), over_e(e_sum), ALU.mult))
            top = [slot_f, tile_f]
            for k in range(2):
                hot = oh1[:, k * 256:(k + 1) * 256]
                chain.link(dve.tensor_reduce(top[k], te(pr1), AX_X, ALU.max))
                chain.link(dve.tensor_tensor(te(sh1), te(pr1), over_e(top[k]), ALU.is_equal))
                chain.link(dve.tensor_tensor(te(sh1), te(sh1), over_t(first_w), ALU.mult))
                chain.link(dve.tensor_reduce(m2, te(sh1), AX_X, ALU.max))
                chain.link(dve.tensor_tensor(te(hot), te(sh1), over_e(m2), ALU.is_equal))
                if k == 0:
                    chain.link(dve.scalar_tensor_tensor(pr1, hot, -2.0, pr1, ALU.mult, ALU.add))
            dve.tensor_copy(ohb1, oh1).then_inc(rhs_ready, 1)
            chain.link(dve.tensor_tensor(row_f, top[0], top[1], ALU.add))
            chain.link(dve.tensor_scalar(row_f, row_f, 1e-9, None, ALU.add))
            chain.link(dve.reciprocal(row_f, row_f))
            for k in range(2):
                chain.link(dve.tensor_tensor(wk[:, k * T:(k + 1) * T], top[k], row_f, ALU.mult))
            dve.wait_ge(cnt_done, 2)
            own, both, pref = ps[3][:, 512:1024], ps[2][:, 0:512], ps[3][:, 0:512]
            sums_over_c = lambda ap: ap.rearrange("p (k c e) -> p k e c", c=NC, e=E)
            k3 = lambda ap: ap.rearrange("p (k e) -> p k e", e=E)
            chain.link(dve.tensor_reduce(k3(own_t), sums_over_c(own), AX_X, ALU.add))
            chain.link(dve.tensor_reduce(k3(both_t), sums_over_c(both), AX_X, ALU.add))
            chain.link(dve.tensor_tensor(off1, both_t, own_t, ALU.subtract))
            chain.link(dve.tensor_scalar(off1, off1, batch_bit, None, ALU.mult))
            b4, o4 = (ap.rearrange("p (k b e) -> p k b e", k=2, b=BP) for ap in (both_t, off1))
            c2 = k3(cnt1)
            chain.link(dve.memset(cnt1, 0.0))
            for b in range(BP):
                chain.link(dve.tensor_tensor(o4[:, :, b, :], o4[:, :, b, :], c2, ALU.add))
                chain.link(dve.tensor_tensor(c2, c2, b4[:, :, b, :], ALU.add))
            chain.link(dve.tensor_scalar(cnt1[:, 0:E], cnt1[:, 0:E], float(CAP), None, ALU.min))
            chain.link(dve.tensor_tensor(o4[:, 1, :, :], o4[:, 1, :, :], cnt1[:, 0:E].unsqueeze(1).to_broadcast([P, BP, E]), ALU.add))
            r4, w4 = (ap.rearrange("p (k c e) -> p k c e", c=NC, e=E) for ap in (run1, own))
            chain.link(dve.tensor_copy(r4[:, :, 0, :], k3(off1)))
            for c in range(1, NC):
                chain.link(dve.tensor_tensor(r4[:, :, c, :], r4[:, :, c - 1, :], w4[:, :, c - 1, :], ALU.add))
            chain.link(dve.tensor_tensor(rk1, run1, pref, ALU.add))
            chain.link(dve.tensor_tensor(scr1, rk1, oh1, ALU.mult))
            chain.link(dve.tensor_reduce(pos, te(scr1), AX_X, ALU.add))
            second, row1, first = keep, e_of, scr1[:, 0:2 * T]
            chain.link(dve.tensor_scalar(second, pos, float(P), None, ALU.is_ge))
            chain.link(dve.scalar_tensor_tensor(row1, second, -float(P), pos, ALU.mult, ALU.add))
            chain.link(dve.tensor_scalar(first, pos, float(P), None, ALU.is_lt))
            chain.link(dve.scalar_tensor_tensor(second, pos, float(CAP), second, ALU.is_lt, ALU.mult))
            r5 = numbers.rearrange("p (t m e) -> p t m e", m=2, e=E)
            for k in range(2):
                dve.scalar_tensor_tensor(r5[:, k * T:(k + 1) * T, 0, :], over_e(tile_no), float(1 + k * T),
                                         te(oh1[:, k * 256:(k + 1) * 256]), ALU.add, ALU.mult)
            chain.link(dve.tensor_scalar(r5[:, :, 1, :], te(oh1), part_no, None, ALU.mult))
            r6 = rhs1.rearrange("p (t j m) -> p t j m", j=2, m=2 * E)
            for j, tile in enumerate((first, second)):
                last = dve.tensor_tensor(r6[:, :, j, :], numbers.rearrange("p (t m) -> p t m", m=2 * E),
                                         tile.unsqueeze(2).to_broadcast([P, 2 * T, 2 * E]), ALU.mult)
            last.then_inc(rhs_ready, 1)
            dve.wait_ge(h_stored, 128)
            with dve.Fori(0, 2 * T // 8) as n:
                dve.tensor_tensor(pos_hot[:, ds(n * (8 * P), 8 * P)].rearrange("p (t s) -> p t s", s=P), over_t(iota_b[:, 0:P], 8),
                                  row1[:, ds(n * 8, 8)].unsqueeze(2).to_broadcast([P, 8, P]), ALU.is_equal).then_inc(hot_made, 1)
            dve.wait_ge(ids_mm, 2)
            id3 = id_f[:, 0:32].rearrange("p (j m) -> p j m", j=2)
            chain.link(dve.tensor_copy(id_f[:, 0:32], ps[0][:, 0:32]))
            chain.link(dve.scalar_tensor_tensor(id3[:, :, 0:E], id3[:, :, 0:E], float(P), id3[:, :, E:2 * E], ALU.mult, ALU.add))
            row3, in3, off3 = id3[:, :, 0:E], id3[:, :, E:2 * E], id_f[:, 32:48].rearrange("p (j e) -> p j e", j=2)
            chain.link(dve.tensor_scalar(off3, row3, 0.0, part_no, ALU.is_equal, ALU.mult))
            chain.link(dve.tensor_tensor(off3, off3, row3, ALU.add))
            chain.link(dve.tensor_copy(ids_i[:, 2 * E:4 * E].rearrange("p (j e) -> p j e", j=2), off3))
            chain.link(dve.tensor_scalar(in3, row3, -float(P), 0.0, ALU.add, ALU.max))
            chain.link(dve.tensor_scalar(off3, in3, float(B * L), -float(B * L), ALU.is_ge, ALU.mult))
            chain.link(dve.tensor_tensor(in3, in3, off3, ALU.add))
            chain.link(dve.tensor_copy(ids_i[:, 0:2 * E].rearrange("p (j e) -> p j e", j=2), in3))
            finish(dve, 8)
            def slot_rows_out(e):
                dve.wait_ge(x_turned, e + (TILES0 // GRP + 3))
                dve.tensor_copy(xg1, ps[0][:, 0:2 * C]).then_inc(xg_ready, 1)

            def results_out(e, u):
                dve.wait_ge(o1_free, e + 1)
                dve.wait_ge(o_mm, e + (TILES0 + 1))
                dve.tensor_tensor(o1_st[u].rearrange("p (t c) -> p t c", c=C),
                                  ps[3][:, u * 512:u * 512 + 2 * C].rearrange("p (t c) -> p t c", c=C),
                                  over_tiles(b2b[:, ds(e * C, C)], 2), ALU.add).then_inc(o_ready, 1)

            dve.wait_ge(f1_b, 48)
            slot_rows_out(0)
            with dve.Fori(0, E // 2 - 1) as i:
                for e, u in ((i * 2 + 1, 0), (i * 2 + 2, 1)):
                    slot_rows_out(e)
                    results_out(e - 1, u)
            slot_rows_out(E - 1)
            results_out(E - 2, 0)
            results_out(E - 1, 1)
            finish(dve, 9)
            for bp in range(BP):
                dve.wait_ge(y_in[bp], 32)
                b3 = [back1[:, (2 * bp + k) * W8:(2 * bp + k + 1) * W8].rearrange("p (t c) -> p t c", c=C) for k in range(2)]
                chain.link(dve.tensor_tensor(b3[0], b3[0], wk[:, bp * NC:(bp + 1) * NC].unsqueeze(2).to_broadcast([P, NC, C]),
                                             ALU.mult))
                dve.wait_ge(y_second, bp + 1)
                chain.link(dve.tensor_tensor(b3[0], b3[0], b3[1], ALU.add))
                dve.tensor_tensor(b3[0], b3[0], over_tiles(mod[1][:, (bp * 6 + GB) * C:(bp * 6 + GB + 1) * C]), ALU.mult
                                  ).then_inc(y_sum, 1)
            finish(dve, 10)

        @block.tensor
        def _(pe):
            pe.wait_ge(wm_in, 32)
            for l in range(2):
                pe.wait_ge(cond_spread, l + 1)
                for bp in range(BP):
                    n = BP * l + bp
                    if n >= 4:
                        pe.wait_ge(mod_out, n - 3)
                    for a, b in ((0, 512), (512, 768)):
                        mm = pe.matmul(ps[n % 4][:, a:b], st[l][:, bp * P:(bp + 1) * P], wm[l][:, a:b],
                                       start=True, stop=True)
                    mm.then_inc(mod_mm, 1)
            pe.wait_ge(consts_made, 1)
            finish(pe, 1)

            def turn(bp, k):
                pe.wait_ge(h_ready, 4 * k + bp + 1)
                if bp >= 2:
                    pe.wait_ge(hT_ready, 4 * k + bp - 1)
                for t in range(NC):
                    mm = pe.transpose(ps[bp % 2][:, t * P:(t + 1) * P], xc[:, bp * W8 + t * C:bp * W8 + (t + 1) * C], ident[:, :])
                mm.then_inc(h_turned, 1)

            def read_states(bp):
                if bp:
                    pe.wait_ge(a0_gated, bp)
                for n in range(2):
                    pe.matmul(ps[3][:, n * 4 * C:(n + 1) * 4 * C], ones_f[0:1, 0:P], d_row[0:1, :], start=True, stop=False)
                pe.wait_ge(a0_spread, bp + 1)
                for t in range(NC):
                    mm = pe.matmul(ps[3][:, t * C:(t + 1) * C], xs[bp % 2][:, t * P:(t + 1) * P], cmat, start=False,
                                   stop=(t % 4 == 3))
                mm.then_inc(a0_y, 1)

            for bp in range(BP):
                pe.wait_ge(a0_normed, bp + 1)
                turn(bp, 0)
                pe.wait_ge(hT_ready, bp + 1)
                if bp >= 2:
                    pe.wait_ge(a0_scan, bp - 1)
                for be in range(2):
                    mm = pe.matmul(ps[2][be * S:(be + 1) * S, bp % 2 * L:(bp % 2 + 1) * L], nb,
                                   hT[:, bp * W8 + be * L:bp * W8 + (be + 1) * L], start=True, stop=True)
                mm.then_inc(a0_up, 1)
                if bp:
                    read_states(bp - 1)
            read_states(BP - 1)
            finish(pe, 2)

            def turn_and_gate(k, w):
                for bp in range(BP + 1):
                    if bp < BP:
                        turn(bp, k)
                    if bp:
                        pe.wait_ge(hT_ready, 4 * k + bp)
                        for t in range((bp - 1) * NC, bp * NC):
                            mm = pe.matmul(ps[2][:, t * E:(t + 1) * E], hT[:, t * P:(t + 1) * P], w, start=True, stop=True)
                mm.then_inc(lg_mm, 1)

            pe.wait_ge(gw, 35)
            pe.transpose(ps[3][0:16, 0:E], wg_n[0:E, :], ident[0:E, 0:E]).then_inc(gw, 1)
            pe.wait_ge(gw, 37)
            pe.matmul(ps[3][:, 512:512 + E], wred_t[0:16, :], wg_t[0:16, :], start=True, stop=True).then_inc(gw, 1)
            pe.wait_ge(gw, 39)
            turn_and_gate(1, w_gate)
            pe.sem_inc(x_turned, 2)
            pe.sem_inc(back_used, 2)
            finish(pe, 3)
            pe.wait_ge(rhs_ready, 1)
            pe.matmul(ps[3][:, 0:T * E], before, onehot_b, start=True, stop=True)
            pe.matmul(ps[3][:, 512:512 + T * E], all_ones, onehot_b, start=True, stop=True).then_inc(cnt_done, 1)
            pe.wait_ge(rhs_ready, 2)
            for t in range(T):
                if t % 8 == 0:
                    pe.wait_ge(hot_made, t // 8 + 1)
                mm = pe.matmul(ps[2][:, 0:80], r_hot[:, t * P:(t + 1) * P], t_rhs[:, t * 80:(t + 1) * 80],
                               start=(t == 0), stop=(t == T - 1))
            mm.then_inc(ids_mm, 1)
            finish(pe, 4)

            pe.wait_ge(f0_w, 64)

            def turn_x(g, u, n):
                pe.wait_ge(gathered[u], n * (16 * GRP) + 16 * GRP)
                for t in range(GRP):
                    mm = pe.transpose(ps[0][:, t * P:(t + 1) * P], gx[u][:, t * C:(t + 1) * C], ident[:, :])
                mm.then_inc(x_turned, 1)

            def first_product(g):
                of = experts_of(pe, g)
                pe.wait_ge(xg_ready, g + 1)
                for t, e in enumerate(of):
                    pe.matmul(ps[1][:, t * F0:(t + 1) * F0], xg[:, t * P:(t + 1) * P], w1a[:, ds(e * F0, F0)],
                              start=True, stop=True).then_inc(h_mm, 1)

            def turn_hidden(g):
                pe.wait_ge(hg_ready, g + 1)
                for t in range(2 * GRP):
                    mm = pe.transpose(ps[2][:, t * P:(t + 1) * P], hb[:, t * P:(t + 1) * P], ident[:, :])
                mm.then_inc(hg_turned, 1)

            def second_product(g):
                of = experts_of(pe, g)
                pe.wait_ge(hgT_ready, g + 1)
                for t, e in enumerate(of):
                    for j in range(2):
                        mm = pe.matmul(ps[3][:, t * C:(t + 1) * C], hgT[:, (2 * t + j) * P:(2 * t + j + 1) * P],
                                       w2a[:, ds(e * F0 + j * C, C)], start=(j == 0), stop=(j == 1))
                    mm.then_inc(o_mm, 1)

            last = TILES0 // GRP - 1
            turn_x(0, 0, 0)
            first_product(0)
            with pe.Fori(0, (last - 1) // 2) as i:
                for g, u, n in ((i * 2 + 1, 1, i), (i * 2 + 2, 0, i + 1)):
                    turn_x(g, u, n)
                    turn_hidden(g - 1)
                    first_product(g)
                    second_product(g - 1)
            turn_x(last, 1, last // 2)
            turn_hidden(last - 1)
            first_product(last)
            second_product(last - 1)
            turn_hidden(last)
            second_product(last)
            finish(pe, 5)

            pe.wait_ge(wlb_in, 32)
            for bp in range(BP):
                turn(bp, 2)
                pe.wait_ge(hT_ready, 2 * BP + bp + 1)
                for n in (2 * bp, 2 * bp + 1):
                    if n >= 2:
                        pe.wait_ge(rt_tanh, n - 1)
                    pe.matmul(ps[3][0:32, n % 2 * 512:(n % 2 + 1) * 512], w_lb[:, 32:64], hT[:, n * 512:(n + 1) * 512],
                              start=True, stop=True).then_inc(rt_mm, 1)
                if bp >= 2:
                    pe.wait_ge(rt_tok_tanh, bp - 1)
                for t in range(NC):
                    mm = pe.matmul(ps[2][:, bp % 2 * 512 + t * 32:bp % 2 * 512 + (t + 1) * 32],
                                   hT[:, (bp * NC + t) * P:(bp * NC + t + 1) * P], w_lb[:, 0:32], start=True, stop=True)
                mm.then_inc(rt_tok, 1)
            pe.wait_ge(rt_tok_tanh, BP)
            for n in range(2):
                mm = pe.matmul(ps[0][:, n * 512:(n + 1) * 512], own_f, t_tok[:, n * 512:(n + 1) * 512], start=True, stop=True)
            mm.then_inc(rt_lr, 1)
            pe.wait_ge(rt_spread, 1)
            for n in range(2):
                mm = pe.matmul(ps[2][:, n * 512:(n + 1) * 512], parity[0:32, :], rate_diag[0:32, n * 512:(n + 1) * 512],
                               start=True, stop=True)
            mm.then_inc(rt_wd, 1)
            pe.sem_inc(win_new, 2)
            pe.sem_inc(wout_new, 2)
            pe.sem_inc(y_scaled, 1)
            finish(pe, 6)

            def project(j, bank, at, done):
                for p in range(HP):
                    mm = pe.matmul(ps[bank][:, p * P:(p + 1) * P], w_qkv[:, j * HD + p * P:j * HD + (p + 1) * P],
                                   hT[:, ds(at, P)], start=True, stop=True)
                mm.then_inc(done, 1)

            def turn_pairs(src, bank, done):
                for p in range(HP):
                    mm = pe.transpose(ps[bank][:, p * P:(p + 1) * P], src(p), ident[:, :])
                mm.then_inc(done, 1)

            def gradient(left, right, bank, done):
                for h in range(H):
                    mm = pe.matmul(ps[bank][h % 2 * D:(h % 2 + 1) * D, h // 2 * P:(h // 2 + 1) * P],
                                   left[:, h * D:(h + 1) * D], right[:, h * P:(h + 1) * P], start=True, stop=True)
                mm.then_inc(done, 1)

            pe.wait_ge(a1_w, 16 * 8)
            project(2, 0, 0, pe_pv)
            project(0, 1, 0, pe_pq)
            project(1, 2, 0, pe_pk)
            pe.wait_ge(vT_out, 1)
            with pe.Fori(0, BP) as bp:
                with pe.Fori(0, NC) as c:
                    t = bp * NC + c
                    pe.wait_ge(win_set, bp * 2 + 2)
                    w4 = lambda w, be, p: w[:, be * 1024 + p * P:be * 1024 + (p + 1) * P]
                    pe.wait_ge(silu_done, t * 2 + 2)
                    for be in range(2):
                        pe.wait_ge(win_new, t * 2 + (be + 1))
                        if be == 1:
                            pe.wait_ge(y_scaled, t + 1)
                        for p in range(HP):
                            mm = pe.matmul(ps[be][:, p * P:(p + 1) * P].rearrange("r (k n) -> r k n", k=2), w4(w_in, be, p),
                                           qk.rearrange("r (k p e n) -> r k p e n", k=2, p=HP, e=2)[:, :, p, be, :],
                                           start=True, stop=True)
                        mm.then_inc(pe_z, 1)
                    pe.wait_ge(wout_set, bp * 2 + 2)
                    for be, bank in ((0, 3), (1, 2)):
                        pe.wait_ge(wout_new, t * 2 + (be + 1))
                        turn_pairs(lambda p: w4(w_out, be, p), bank, pe_wt)
                    pe.wait_ge(z_centered, t * 2 + 1)
                    project(2, 0, t * P + P, pe_pv)
                    pe.wait_ge(woutT_out, t * 2 + 1)
                    pe.wait_ge(vT_out, t + 1)
                    turn_pairs(lambda p: vT[:, p * P:(p + 1) * P], 3, pe_vt)
                    pe.wait_ge(z_centered, t * 2 + 2)
                    project(0, 1, t * P + P, pe_pq)
                    pe.wait_ge(woutT_out, t * 2 + 2)
                    for p in range(HP):
                        for be in range(2):
                            mm = pe.matmul(ps[2][be * CH:(be + 1) * CH, p * P:(p + 1) * P],
                                           vT[:, p * P + be * CH:p * P + (be + 1) * CH], w4(w_outT, be, p),
                                           start=True, stop=True)
                    mm.then_inc(pe_a, 1)
                    pe.wait_ge(vtok_out, t + 1)
                    pe.wait_ge(pk_norm, t + 1)
                    turn_pairs(lambda p: prob[:, 1024 + p * P:1024 + (p + 1) * P], 3, pe_pt)
                    pe.wait_ge(vT_out, t + 2)
                    project(1, 0, t * P + P, pe_pk)
                    pe.wait_ge(ptok_out, t + 1)
                    turn_pairs(lambda p: qk[:, 1024 + p * P:1024 + (p + 1) * P], 3, pe_kt)
                    pe.wait_ge(silu_done, t * 2 + 3)
                    pe.wait_ge(pq_norm, t + 1)
                    for p in range(HP):
                        for be in range(2):
                            mm = pe.matmul(ps[1][:, p * P + be * CH:p * P + (be + 1) * CH], w4(w_out, be, p),
                                           prob[:, p * P + be * CH:p * P + (be + 1) * CH], start=True, stop=True)
                    mm.then_inc(pe_o, 1)
                    pe.wait_ge(silu_done, t * 2 + 4)
                    pe.wait_ge(v_scaled, t + 1)
                    gradient(p_tok, v_pad, 0, pe_gout)
                    pe.wait_ge(g_done, t + 1)
                    pe.wait_ge(k_scaled, t + 1)
                    gradient(k_tok, g_pad, 2, pe_gin)
                    pe.wait_ge(oT_out, t + 1)
                    for p in range(HP):
                        mm = pe.matmul(ps[1][:, 0:C], oT[:, p * P:(p + 1) * P], w_o[:, p * C:(p + 1) * C],
                                       start=(p == 0), stop=(p == HP - 1))
                    mm.then_inc(pe_y, 1)
            finish(pe, 7)

            pe.wait_ge(gw, 55)
            turn_and_gate(3, wg1)
            pe.wait_ge(rhs_ready, 3)
            pe.matmul(ps[3][:, 0:512], before_own, ohb1, start=True, stop=True)
            pe.matmul(ps[3][:, 512:1024], own_ones, ohb1, start=True, stop=True)
            pe.wait_ge(lg_out, 2)
            pe.matmul(ps[2][:, 0:512], all_ones, ohb1, start=True, stop=True).then_inc(cnt_done, 1)
            pe.wait_ge(rhs_ready, 4)

            for t in range(2 * T):
                if t % 8 == 0:
                    pe.wait_ge(hot_made, T // 8 + t // 8 + 1)
                mm = pe.matmul(ps[0][:, 0:32], pos_hot[:, t * P:(t + 1) * P], rhs1[:, t * 32:(t + 1) * 32],
                               start=(t == 0), stop=(t == 2 * T - 1))
            mm.then_inc(ids_mm, 1)
            finish(pe, 8)
            g0 = TILES0 // GRP
            def turn_slots(e, u, n):
                pe.wait_ge(gathered[u], n * 32 + (16 * TILES0 // 2 + 32))
                for t in range(2):
                    mm = pe.transpose(ps[0][:, t * P:(t + 1) * P], gx1[u][:, t * C:(t + 1) * C], ident[:, :])
                mm.then_inc(x_turned, 1)

            def slots_first(e, u, n):
                pe.wait_ge(f1_w[u], n * 16 + 16)
                pe.wait_ge(xg_ready, e + (g0 + 1))
                for j in range(4):
                    mm = pe.matmul(ps[1 + u][:, j * 256:(j + 1) * 256], w1s[u][:, j * P:(j + 1) * P], xg1, start=True, stop=True)
                mm.then_inc(h_mm, 1)

            def slots_second(e, u):
                pe.wait_ge(hg_ready, e + (g0 + 1))
                for t in range(2):
                    for j in range(4):
                        mm = pe.matmul(ps[3][:, u * 512 + t * C:u * 512 + (t + 1) * C],
                                       hg1[u][:, j * 256 + t * P:j * 256 + (t + 1) * P],
                                       w2s[:, ds(e * F1 + j * C, C)], start=(j == 0), stop=(j == 3))
                mm.then_inc(o_mm, 1)

            pe.wait_ge(f1_b, 48)
            turn_slots(0, 0, 0)
            slots_first(0, 0, 0)
            with pe.Fori(0, E // 2 - 1) as i:
                for e, u, n in ((i * 2 + 1, 1, i), (i * 2 + 2, 0, i + 1)):
                    turn_slots(e, u, n)
                    slots_first(e, u, n)
                    slots_second(e - 1, 1 - u)
            turn_slots(E - 1, 1, E // 2 - 1)
            slots_first(E - 1, 1, E // 2 - 1)
            slots_second(E - 2, 0)
            slots_second(E - 1, 1)
            finish(pe, 9)
            finish(pe, 10)


INS = ["L0_attn_u", "L0_attn_dt", "L0_attn_A", "L0_attn_Bmat", "L0_attn_C", "L0_attn_D", "L0_attn_norm_w",
       "L0_ffn_wg", "L0_ffn_W1", "L0_ffn_b1", "L0_ffn_W2", "L0_ffn_b2", "L0_wmod",
       "L1_ffn_Wg", "L1_ffn_W1", "L1_ffn_b1", "L1_ffn_W2", "L1_ffn_b2", "L1_wmod"]


def layouts(inputs):
    import numpy as np

    a = {n: np.ascontiguousarray(inputs[n]) for n in INS}
    t = lambda x, *axes: np.ascontiguousarray(np.transpose(np.asarray(x), axes))
    a["L0_cT"], a["L1_cT"] = t(inputs["L0_c"], 1, 0), t(inputs["L1_c"], 1, 0)
    for n in ("Wq", "Wk", "Wv", "Wlr", "Wbeta", "Wo"):
        a[f"L1_attn_{n}T"] = t(inputs[f"L1_attn_{n}"], 1, 0)
    w_in, w_out = np.asarray(inputs["L1_attn_W_in_init"])[0], np.asarray(inputs["L1_attn_W_out_init"])[0]
    a["L0_ffn_w_redT"] = t(inputs["L0_ffn_w_red"], 1, 0)
    a["L1_b1_cols"] = t(np.asarray(inputs["L1_ffn_b1"]).reshape(E, F1 // P, P), 2, 0, 1).reshape(P, -1)
    a["W_inT"] = t(w_in, 1, 2, 0)
    a["W_out"] = t(w_out, 1, 0, 2)
    return a


def kernel(**inputs):
    import numpy as np
    import concourse.bacc as bacc
    from concourse.bass_utils import run_bass_kernel_spmd

    nc = bacc.Bacc("TRN2", target_bir_lowering=False, num_devices=1)
    arrays = layouts(inputs)
    A = {n: nc.dram_tensor(f"in_{n}", a.shape, mybir.dt.from_np(a.dtype), kind="ExternalInput").ap()
         for n, a in arrays.items()}
    A["out"] = nc.dram_tensor("out_x", (B, L, C), F32, kind="ExternalOutput").ap()
    program(nc, A)
    r = run_bass_kernel_spmd(nc, [{f"in_{n}": a for n, a in arrays.items()}], core_ids=[0])
    return r.results[0]["out_x"]
```
